# Optimizing a Trainium2 kernel written in Bass

```python
import numpy as np
import jax
import jax.numpy as jnp

def _softmax(x, axis=-1):
    return jax.nn.softmax(x, axis=axis)

def _gelu(x):
    return jax.nn.gelu(x, approximate=True)

def _silu(x):
    return jax.nn.silu(x)

def _sigmoid(x):
    return jax.nn.sigmoid(x)

def _layernorm(x, axis=-1, eps=1e-05):
    m = jnp.mean(x, axis=axis, keepdims=True)
    v = jnp.var(x, axis=axis, keepdims=True)
    return (x - m) / jnp.sqrt(v + eps)

def _scatter_add(tgt, idx, src, axis=0):
    return tgt.at[idx].add(src)

def _segment_sum(src, seg, n):
    return jax.ops.segment_sum(src, seg, n)
kernel_name = 'mk_sandwich_d1_jaxref_r8_b9611b'

def setup_inputs(seed: int=0):
    np.random.seed(seed)
    _w = jnp.asarray

    def _L0_attn_setup():
        import jax, jax.numpy as jnp
        import numpy as np
        EMBED = 128
        HEADS = 16
        HD = EMBED // HEADS
        M = 32
        R = 2
        EPS = 1e-06
        C_CONST = 2.0 + EPS
        CHUNK = 64

        def _features(x, omega, quad_nodes, quad_weights):
            B, H, T, D = x.shape
            xn = x / jnp.maximum(jnp.linalg.norm(x, axis=-1, keepdims=True), 1e-12)
            proj = jnp.einsum('bhtd,rhdm->rbhtm', xn, omega)
            s = quad_nodes[:, None, None, None, None]
            sqrt_2s = jnp.sqrt(2.0 * jnp.maximum(s, 0.0))
            arg = jnp.clip(proj * sqrt_2s - s, -20.0, 20.0)
            feat = jnp.exp(arg) / np.sqrt(M).astype(np.float32)
            feat = feat * jnp.sqrt(jnp.maximum(quad_weights, 0.0))[:, None, None, None, None]
            return jnp.transpose(feat, (1, 2, 3, 0, 4)).reshape(B, H, T, R * M)
        key = jax.random.key(seed)
        ks = jax.random.split(key, 4)
        B, T = (2, 256)
        x = jax.random.normal(ks[0], (B, T, EMBED), jnp.float32)
        Wqkv = jax.random.normal(ks[1], (EMBED, 3 * EMBED), jnp.float32) * 0.02
        bqkv = jnp.zeros((3 * EMBED,), jnp.float32)
        Wout = jax.random.normal(ks[2], (EMBED, EMBED), jnp.float32) * 0.02
        bout = jnp.zeros((EMBED,), jnp.float32)
        omega = jax.random.normal(ks[3], (R, HEADS, HD, M), jnp.float32)
        nodes, weights = np.polynomial.laguerre.laggauss(R)
        quad_nodes = jnp.asarray(nodes / C_CONST, jnp.float32)
        quad_weights = jnp.asarray(weights * (C_CONST / 4.0), jnp.float32)
        return {'x': x, 'Wqkv': Wqkv, 'bqkv': bqkv, 'Wout': Wout, 'bout': bout, 'omega': omega, 'quad_nodes': quad_nodes, 'quad_weights': quad_weights}
    _L0_attn_in = _L0_attn_setup()

    def _L0_ffn_setup():
        import jax, jax.numpy as jnp
        import numpy as np
        DIM = 128
        DEPTH = 2
        HEADS = 8
        DIM_HEAD = 64
        WINDOW = 64
        INNER = HEADS * DIM_HEAD
        HID = int(DIM * 4 * 2 / 3)
        B, N = (2, 1024)
        QK_SCALE = 8.0

        def shift_token(t):
            t1, t2 = jnp.split(t, 2, axis=-1)
            t2 = jnp.pad(t2, ((0, 0), (1, 0), (0, 0)))[:, :-1]
            return jnp.concatenate([t1, t2], axis=-1)

        def l2norm(t):
            return t / jnp.clip(jnp.linalg.norm(t, axis=-1, keepdims=True), 1e-12)

        def rotate_half(x):
            x1, x2 = jnp.split(x, 2, axis=-1)
            return jnp.concatenate([-x2, x1], axis=-1)

        def rotary_xpos(q, k):
            n = q.shape[-2]
            half_idx = jnp.arange(0, DIM_HEAD, 2, dtype=jnp.float32)
            inv_freq = 1.0 / 10000.0 ** (half_idx / DIM_HEAD)
            t = jnp.arange(n, dtype=jnp.float32)
            freqs = t[:, None] * inv_freq[None, :]
            freqs = jnp.concatenate([freqs, freqs], axis=-1)
            base = (half_idx + 0.4 * DIM_HEAD) / (1.4 * DIM_HEAD)
            power = (t - n // 2) / float(WINDOW // 2)
            scale = base[None, :] ** power[:, None]
            scale = jnp.concatenate([scale, scale], axis=-1)
            cos, sin = (jnp.cos(freqs), jnp.sin(freqs))
            q = q * cos * scale + rotate_half(q) * sin * scale
            k = k * cos / scale + rotate_half(k) * sin / scale
            return (q, k)

        def local_attention(q, k, v):
            b, h, n, d = q.shape
            w = n // WINDOW
            bq = q.reshape(b, h, w, WINDOW, d) * QK_SCALE
            bk = k.reshape(b, h, w, WINDOW, d)
            bv = v.reshape(b, h, w, WINDOW, d)

            def look_around(t):
                p = jnp.pad(t, ((0, 0), (0, 0), (1, 0), (0, 0), (0, 0)))
                return jnp.concatenate([p[:, :, :w], p[:, :, 1:]], axis=3)
            bk, bv = (look_around(bk), look_around(bv))
            bt = jnp.arange(n).reshape(w, WINDOW)
            btp = jnp.pad(bt, ((1, 0), (0, 0)), constant_values=-1)
            btk = jnp.concatenate([btp[:w], btp[1:]], axis=1)
            sim = jnp.einsum('bhwid,bhwjd->bhwij', bq, bk)
            i = bt[:, :, None]
            j = btk[:, None, :]
            mask = (i < j) | (i > j + WINDOW) | (j == -1)
            sim = jnp.where(mask, -jnp.finfo(sim.dtype).max, sim)
            attn = jax.nn.softmax(sim, axis=-1)
            out = jnp.einsum('bhwij,bhwjd->bhwid', attn, bv)
            return out.reshape(b, h, n, d)

        def _layer(x, wqkv, qs, ksc, wo, lg, lb, w1, b1, w2, b2):
            b, n, _ = x.shape
            h = shift_token(x)
            qkv = h @ wqkv
            q, k, v = jnp.split(qkv, 3, axis=-1)
            to_heads = lambda t: t.reshape(b, n, HEADS, DIM_HEAD).transpose(0, 2, 1, 3)
            q, k, v = (to_heads(q), to_heads(k), to_heads(v))
            q = l2norm(q) * qs
            k = l2norm(k) * ksc
            q, k = rotary_xpos(q, k)
            o = local_attention(q, k, v)
            o = o.transpose(0, 2, 1, 3).reshape(b, n, INNER)
            x = x + o @ wo
            h = shift_token(x)
            mu = h.mean(-1, keepdims=True)
            var = h.var(-1, keepdims=True)
            h = (h - mu) / jnp.sqrt(var + 1e-05) * lg + lb
            h = h @ w1 + b1
            a, g = jnp.split(h, 2, axis=-1)
            h = a * jax.nn.gelu(g, approximate=False)
            x = x + h @ w2 + b2
            return x
        key = jax.random.key(seed)
        ks = jax.random.split(key, 6)
        return {'x': jax.random.normal(ks[0], (B, N, DIM), jnp.float32), 'wqkv': jax.random.normal(ks[1], (DEPTH, DIM, 3 * INNER), jnp.float32) * 0.02, 'q_scale': jnp.ones((DEPTH, DIM_HEAD), jnp.float32), 'k_scale': jnp.ones((DEPTH, DIM_HEAD), jnp.float32), 'wo': jax.random.normal(ks[2], (DEPTH, INNER, DIM), jnp.float32) * 0.02, 'ln_g': jnp.ones((DEPTH, DIM), jnp.float32), 'ln_b': jnp.zeros((DEPTH, DIM), jnp.float32), 'w1': jax.random.normal(ks[3], (DEPTH, DIM, 2 * HID), jnp.float32) * 0.02, 'b1': jnp.zeros((DEPTH, 2 * HID), jnp.float32), 'w2': jax.random.normal(ks[4], (DEPTH, HID, DIM), jnp.float32) * 0.02, 'b2': jnp.zeros((DEPTH, DIM), jnp.float32)}
    _L0_ffn_in = _L0_ffn_setup()
    _d = {'L0_attn_x': _L0_attn_in['x'], 'L0_attn_Wqkv': _L0_attn_in['Wqkv'], 'L0_attn_bqkv': _L0_attn_in['bqkv'], 'L0_attn_Wout': _L0_attn_in['Wout'], 'L0_attn_bout': _L0_attn_in['bout'], 'L0_attn_omega': _L0_attn_in['omega'], 'L0_attn_quad_nodes': _L0_attn_in['quad_nodes'], 'L0_attn_quad_weights': _L0_attn_in['quad_weights'], 'L0_ffn_wqkv': _L0_ffn_in['wqkv'], 'L0_ffn_q_scale': _L0_ffn_in['q_scale'], 'L0_ffn_k_scale': _L0_ffn_in['k_scale'], 'L0_ffn_wo': _L0_ffn_in['wo'], 'L0_ffn_ln_g': _L0_ffn_in['ln_g'], 'L0_ffn_ln_b': _L0_ffn_in['ln_b'], 'L0_ffn_w1': _L0_ffn_in['w1'], 'L0_ffn_b1': _L0_ffn_in['b1'], 'L0_ffn_w2': _L0_ffn_in['w2'], 'L0_ffn_b2': _L0_ffn_in['b2']}
    _x0 = _d['L0_attn_x']
    _d['L0_attn_x'] = jax.random.normal(jax.random.fold_in(jax.random.key(seed), 1), (8, 256, 128), dtype=_x0.dtype)
    del _x0
    return _d

def reference(L0_attn_x, L0_attn_Wqkv, L0_attn_bqkv, L0_attn_Wout, L0_attn_bout, L0_attn_omega, L0_attn_quad_nodes, L0_attn_quad_weights, L0_ffn_wqkv, L0_ffn_q_scale, L0_ffn_k_scale, L0_ffn_wo, L0_ffn_ln_g, L0_ffn_ln_b, L0_ffn_w1, L0_ffn_b1, L0_ffn_w2, L0_ffn_b2):

    def _L0_attn_ref(x, Wqkv, bqkv, Wout, bout, omega, quad_nodes, quad_weights):
        import jax, jax.numpy as jnp
        import numpy as np
        EMBED = 128
        HEADS = 16
        HD = EMBED // HEADS
        M = 32
        R = 2
        EPS = 1e-06
        C_CONST = 2.0 + EPS
        CHUNK = 64

        def _features(x, omega, quad_nodes, quad_weights):
            B, H, T, D = x.shape
            xn = x / jnp.maximum(jnp.linalg.norm(x, axis=-1, keepdims=True), 1e-12)
            proj = jnp.einsum('bhtd,rhdm->rbhtm', xn, omega)
            s = quad_nodes[:, None, None, None, None]
            sqrt_2s = jnp.sqrt(2.0 * jnp.maximum(s, 0.0))
            arg = jnp.clip(proj * sqrt_2s - s, -20.0, 20.0)
            feat = jnp.exp(arg) / np.sqrt(M).astype(np.float32)
            feat = feat * jnp.sqrt(jnp.maximum(quad_weights, 0.0))[:, None, None, None, None]
            return jnp.transpose(feat, (1, 2, 3, 0, 4)).reshape(B, H, T, R * M)
        B, T, C = x.shape
        qkv = x @ Wqkv + bqkv
        q, k, v = jnp.split(qkv, 3, axis=-1)
        resh = lambda t: t.reshape(B, T, HEADS, HD).transpose(0, 2, 1, 3)
        q, k, v = (resh(q), resh(k), resh(v))
        qf = _features(q, omega, quad_nodes, quad_weights)
        kf = _features(k, omega, quad_nodes, quad_weights)
        Fd = R * M
        nc = T // CHUNK
        to_chunks = lambda t, last: t.reshape(B, HEADS, nc, CHUNK, last).transpose(2, 0, 1, 3, 4)
        qc = to_chunks(qf, Fd)
        kc = to_chunks(kf, Fd)
        vc = to_chunks(v, HD)

        def step(carry, inp):
            kv_state, k_state = carry
            q_ch, k_ch, v_ch = inp
            kv_prod = jnp.einsum('bhtf,bhtd->bhtfd', k_ch, v_ch)
            kv_cur = jnp.cumsum(kv_prod, axis=2) + kv_state[:, :, None]
            k_cur = jnp.cumsum(k_ch, axis=2) + k_state[:, :, None]
            ctx = jnp.einsum('bhtf,bhtfd->bhtd', q_ch, kv_cur)
            den = jnp.maximum(jnp.einsum('bhtf,bhtf->bht', q_ch, k_cur), 1e-06)
            out_ch = ctx / den[..., None]
            return ((kv_cur[:, :, -1], k_cur[:, :, -1]), out_ch)
        init = (jnp.zeros((B, HEADS, Fd, HD), jnp.float32), jnp.zeros((B, HEADS, Fd), jnp.float32))
        _, outs = jax.lax.scan(step, init, (qc, kc, vc))
        out = outs.transpose(1, 2, 0, 3, 4).reshape(B, HEADS, T, HD)
        out = out.transpose(0, 2, 1, 3).reshape(B, T, C)
        return out @ Wout + bout

    def _L0_ffn_ref(x, wqkv, q_scale, k_scale, wo, ln_g, ln_b, w1, b1, w2, b2):
        import jax, jax.numpy as jnp
        import numpy as np
        DIM = 128
        DEPTH = 2
        HEADS = 8
        DIM_HEAD = 64
        WINDOW = 64
        INNER = HEADS * DIM_HEAD
        HID = int(DIM * 4 * 2 / 3)
        B, N = (2, 1024)
        QK_SCALE = 8.0

        def shift_token(t):
            t1, t2 = jnp.split(t, 2, axis=-1)
            t2 = jnp.pad(t2, ((0, 0), (1, 0), (0, 0)))[:, :-1]
            return jnp.concatenate([t1, t2], axis=-1)

        def l2norm(t):
            return t / jnp.clip(jnp.linalg.norm(t, axis=-1, keepdims=True), 1e-12)

        def rotate_half(x):
            x1, x2 = jnp.split(x, 2, axis=-1)
            return jnp.concatenate([-x2, x1], axis=-1)

        def rotary_xpos(q, k):
            n = q.shape[-2]
            half_idx = jnp.arange(0, DIM_HEAD, 2, dtype=jnp.float32)
            inv_freq = 1.0 / 10000.0 ** (half_idx / DIM_HEAD)
            t = jnp.arange(n, dtype=jnp.float32)
            freqs = t[:, None] * inv_freq[None, :]
            freqs = jnp.concatenate([freqs, freqs], axis=-1)
            base = (half_idx + 0.4 * DIM_HEAD) / (1.4 * DIM_HEAD)
            power = (t - n // 2) / float(WINDOW // 2)
            scale = base[None, :] ** power[:, None]
            scale = jnp.concatenate([scale, scale], axis=-1)
            cos, sin = (jnp.cos(freqs), jnp.sin(freqs))
            q = q * cos * scale + rotate_half(q) * sin * scale
            k = k * cos / scale + rotate_half(k) * sin / scale
            return (q, k)

        def local_attention(q, k, v):
            b, h, n, d = q.shape
            w = n // WINDOW
            bq = q.reshape(b, h, w, WINDOW, d) * QK_SCALE
            bk = k.reshape(b, h, w, WINDOW, d)
            bv = v.reshape(b, h, w, WINDOW, d)

            def look_around(t):
                p = jnp.pad(t, ((0, 0), (0, 0), (1, 0), (0, 0), (0, 0)))
                return jnp.concatenate([p[:, :, :w], p[:, :, 1:]], axis=3)
            bk, bv = (look_around(bk), look_around(bv))
            bt = jnp.arange(n).reshape(w, WINDOW)
            btp = jnp.pad(bt, ((1, 0), (0, 0)), constant_values=-1)
            btk = jnp.concatenate([btp[:w], btp[1:]], axis=1)
            sim = jnp.einsum('bhwid,bhwjd->bhwij', bq, bk)
            i = bt[:, :, None]
            j = btk[:, None, :]
            mask = (i < j) | (i > j + WINDOW) | (j == -1)
            sim = jnp.where(mask, -jnp.finfo(sim.dtype).max, sim)
            attn = jax.nn.softmax(sim, axis=-1)
            out = jnp.einsum('bhwij,bhwjd->bhwid', attn, bv)
            return out.reshape(b, h, n, d)

        def _layer(x, wqkv, qs, ksc, wo, lg, lb, w1, b1, w2, b2):
            b, n, _ = x.shape
            h = shift_token(x)
            qkv = h @ wqkv
            q, k, v = jnp.split(qkv, 3, axis=-1)
            to_heads = lambda t: t.reshape(b, n, HEADS, DIM_HEAD).transpose(0, 2, 1, 3)
            q, k, v = (to_heads(q), to_heads(k), to_heads(v))
            q = l2norm(q) * qs
            k = l2norm(k) * ksc
            q, k = rotary_xpos(q, k)
            o = local_attention(q, k, v)
            o = o.transpose(0, 2, 1, 3).reshape(b, n, INNER)
            x = x + o @ wo
            h = shift_token(x)
            mu = h.mean(-1, keepdims=True)
            var = h.var(-1, keepdims=True)
            h = (h - mu) / jnp.sqrt(var + 1e-05) * lg + lb
            h = h @ w1 + b1
            a, g = jnp.split(h, 2, axis=-1)
            h = a * jax.nn.gelu(g, approximate=False)
            x = x + h @ w2 + b2
            return x
        for l in range(DEPTH):
            x = _layer(x, wqkv[l], q_scale[l], k_scale[l], wo[l], ln_g[l], ln_b[l], w1[l], b1[l], w2[l], b2[l])
        return x
    x = L0_attn_x
    x = x + _layernorm(_L0_attn_ref(_layernorm(x, axis=-1), L0_attn_Wqkv, L0_attn_bqkv, L0_attn_Wout, L0_attn_bout, L0_attn_omega, L0_attn_quad_nodes, L0_attn_quad_weights), axis=-1)
    x = x + _layernorm(_L0_ffn_ref(_layernorm(x, axis=-1), L0_ffn_wqkv, L0_ffn_q_scale, L0_ffn_k_scale, L0_ffn_wo, L0_ffn_ln_g, L0_ffn_ln_b, L0_ffn_w1, L0_ffn_b1, L0_ffn_w2, L0_ffn_b2), axis=-1)
    return x

_drawn_inputs = setup_inputs


def setup_inputs(seed=0):
    import zlib

    import numpy as np

    out = dict(_drawn_inputs(seed))
    spreads = {'L0_attn_bqkv': (0.0, 0.1),
     'L0_attn_bout': (0.0, 0.1),
     'L0_ffn_q_scale': (1.0, 0.6),
     'L0_ffn_k_scale': (1.0, 0.6),
     'L0_ffn_ln_g': (1.0, 0.6),
     'L0_ffn_ln_b': (0.0, 0.8),
     'L0_ffn_b1': (0.0, 0.8),
     'L0_ffn_b2': (0.0, 0.8)}
    factors = {'L0_ffn_w1': 7.126, 'L0_ffn_w2': 6.97}
    for name, (base, spread) in spreads.items():
        noise = np.random.default_rng([zlib.crc32(name.encode()), seed]).standard_normal(out[name].shape)
        drawn = base * np.exp(spread * noise) if base else spread * noise
        out[name] = jnp.asarray(drawn.astype(out[name].dtype))
    for name, factor in factors.items():
        out[name] = (out[name] * factor).astype(out[name].dtype)
    return out
```

```python
from contextlib import ExitStack

import concourse.bass as bass
import numpy as np
from concourse import mybir

P = 128
F32 = mybir.dt.float32
BF16 = mybir.dt.bfloat16
ALU = mybir.AluOpType
ACT = mybir.ActivationFunctionType
AXX = mybir.AxisListType.X

BATCH, SEQ, CH = 8, 256, 128
TILES = BATCH * SEQ // P
UPS = SEQ // P
DEPTH = 2
A_HEADS, A_DIM, A_M, A_R = 16, 8, 32, 2
A_FEAT = A_R * A_M
PAIRS = A_HEADS // 2
GROUPS = 2
GH = A_HEADS // GROUPS
GROWS = GH * A_DIM + GH
CLIP = 20.0
HEADS, DIM, WIN = 8, 64, 64
INNER = HEADS * DIM
HP = HEADS // 2
QK_SCALE = 8.0
KEYS = 2 * WIN
VCOL = DIM + 1
MASKED = -1e30
HID = CH * 4 * 2 // 3
HCH = -(-HID // P)
HLAST = HID - (HCH - 1) * P
EPS = 1e-5


def shape_constants():
    half = np.arange(0, DIM, 2, dtype=np.float32)
    inv_freq = (np.float32(1.0) / np.float32(10000.0) ** (half / np.float32(DIM))).astype(np.float32)
    t = np.arange(SEQ, dtype=np.float32)
    freqs = t[:, None] * inv_freq[None, :]
    base = ((half + np.float32(0.4 * DIM)) / np.float32(1.4 * DIM)).astype(np.float32)
    power = (t - SEQ // 2) / np.float32(WIN // 2)
    scale = base[None, :] ** power[:, None]
    cos, sin = np.cos(freqs), np.sin(freqs)
    cos, sin = np.concatenate([cos, cos], 1), np.concatenate([-sin, sin], 1)
    scale = np.concatenate([scale, scale], 1)
    rot = np.stack([np.stack([cos * scale * QK_SCALE, cos / scale], 1),
                    np.stack([sin * scale * QK_SCALE, sin / scale], 1)], 0)
    rot = rot.reshape(2, UPS, P, 2, DIM).transpose(0, 2, 1, 3, 4).astype(np.float32)
    q = np.arange(WIN)[:, None] + WIN
    k = np.arange(KEYS)[None, :]
    seen = (k <= q) & (q <= k + WIN)
    mask = np.where(seen, 0.0, MASKED)
    first = np.where(seen & (k >= WIN), 0.0, MASKED)
    masks = np.stack([np.concatenate([first, mask]), np.concatenate([mask, mask])], 1)
    s = np.arange(P)
    causal = (s[:, None] <= s[None, :]).astype(np.float32)
    owner = (s[:, None] // A_DIM == np.arange(A_HEADS)[None, :]).astype(np.float32)
    node = ((s[:, None] // A_M) % A_R == np.arange(A_R)[None, :]).astype(np.float32)
    return {
        "c_rot_cos": np.ascontiguousarray(rot[0]), "c_rot_sin": np.ascontiguousarray(rot[1]),
        "c_masks": masks.astype(np.float32), "c_ident": np.eye(P, dtype=np.float32),
        "c_causal": causal, "c_owner": owner, "c_node": node,
    }


def build(nc, x, Wqkv, bqkv, Wout, bout, omega, nodes, weights, wqkv, q_scale, k_scale, wo, ln_g, ln_b,
          w1, b1, w2, b2, c_rot_cos, c_rot_sin, c_masks, c_ident, c_causal, c_owner, c_node, out):
    with ExitStack() as ctx:
        def sb(name, shape, dt=F32):
            return ctx.enter_context(nc.sbuf_tensor(name, shape, dt))

        def sem(name):
            return ctx.enter_context(nc.semaphore(name))

        x1 = sb("x1", [P, TILES, CH])
        xc = sb("xc", [P, TILES, CH])
        ident = sb("ident", [P, P])
        ident_bf = sb("ident_bf", [P, P], BF16)
        causal = sb("causal", [P, P])
        owner = sb("owner", [P, A_HEADS])
        node_sel = sb("node_sel", [P, A_R])
        rot_cos = sb("rot_cos", [P, UPS, 2, DIM])
        rot_sin = sb("rot_sin", [P, UPS, 2, DIM])
        masks_f = sb("masks_f", [P, 2, KEYS])
        masks = sb("masks", [P, 2, 4, KEYS], BF16)
        a_wqkv = sb("a_wqkv", [P, 3 * CH])
        a_bqkv = sb("a_bqkv", [P, 3 * CH])
        a_wout = sb("a_wout", [P, CH])
        a_bout = sb("a_bout", [P, CH])
        omega_rows = sb("omega_rows", [P, A_R, A_M])
        omega_pad = sb("omega_pad", [P, A_HEADS, A_FEAT])
        quad = sb("quad", [P, 2, A_R])
        quad_t = sb("quad_t", [P, 8, A_R])
        feat_sel = sb("feat_sel", [P, 2, A_R])
        feat_bias = sb("feat_bias", [P, 2])
        feat_ends = sb("feat_ends", [P, 2])
        power = sb("power", [P, 4])
        st6 = sb("st6", [P, 3, UPS, 6])
        st2 = sb("st2", [P, 3, UPS, 2])
        rstd = sb("rstd", [P, 3, UPS])
        a_ss = sb("a_ss", [P, UPS * 2 * A_HEADS])
        a_rn = sb("a_rn", [P, UPS * 2 * A_HEADS])
        xn = sb("xn", [P, UPS, CH])
        xnT = sb("xnT", [P, SEQ])
        a_qkv = sb("a_qkv", [P, UPS, 3 * CH])
        a_sq = sb("a_sq", [P, UPS, 2 * CH])
        a_qkn = sb("a_qkn", [P, UPS, 2 * CH])
        a_qkT = sb("a_qkT", [P, 2, SEQ])
        a_exp = sb("a_exp", [P, 2, 2, SEQ])
        a_qf = sb("a_qf", [P, 2, SEQ])
        a_kz = sb("a_kz", [P, 2, 2, SEQ])
        a_S = sb("a_S", [P, 2, SEQ + P])
        a_vz = sb("a_vz", [P, UPS, GROUPS, GH * (GROWS + A_DIM)])
        a_oT = sb("a_oT", [GROWS, GROUPS, SEQ])
        a_den = sb("a_den", [P, 2, UPS * GROUPS * GH])
        a_o = sb("a_o", [P, UPS, CH])
        a_oT2 = sb("a_oT2", [P, SEQ])
        a_y = sb("a_y", [P, UPS, CH])
        b_wqkv = sb("b_wqkv", [P, 3 * INNER])
        b_wo = sb("b_wo", [P, HP, CH])
        qk_scale = sb("qk_scale", [P, 2, DIM])
        t_cos = sb("t_cos", [P, UPS, 2, DIM])
        t_sin = sb("t_sin", [P, UPS, 2, DIM])
        hT = sb("hT", [P, WIN + SEQ + 1])
        b_x = sb("b_x", [P, CH])
        b_sq = sb("b_sq", [P, 2 * INNER])
        b_ss = sb("b_ss", [P, 2 * HEADS])
        b_rn = sb("b_rn", [P, 2 * HEADS])
        b_qkn = sb("b_qkn", [P, 2 * INNER])
        b_ra = sb("b_ra", [P, 2 * INNER])
        b_rb = sb("b_rb", [P, 2 * INNER])
        b_qT = sb("b_qT", [P, HP, P])
        b_kz = sb("b_kz", [P, HP, 2, WIN + SEQ])
        b_v = sb("b_v", [P, 2, 2, HEADS, VCOL])
        b_mx = sb("b_mx", [P, HEADS])
        b_p = sb("b_p", [P, HEADS, KEYS])
        b_pT = sb("b_pT", [P, HEADS, P])
        b_rs = sb("b_rs", [P, HEADS])
        b_o = sb("b_o", [P, HEADS, DIM])
        b_oT = sb("b_oT", [P, HP, P])
        c_w1 = sb("c_w1", [P, 2, HCH * P])
        c_w2 = sb("c_w2", [P, HCH, CH])
        c_b1 = sb("c_b1", [P, 2, HCH])
        c_b2 = sb("c_b2", [P, CH])
        c_lg = sb("c_lg", [P, 1])
        c_lb = sb("c_lb", [P, 1])
        c_x = sb("c_x", [P, UPS, CH])
        c_hn = sb("c_hn", [P, UPS, CH])
        c_hT = sb("c_hT", [P, SEQ])
        c_st6 = sb("c_st6", [P, UPS, 6])
        c_st2 = sb("c_st2", [P, UPS, 2])
        c_rstd = sb("c_rstd", [P, UPS])
        c_gelu = sb("c_gelu", [P, HCH, SEQ])
        c_act = sb("c_act", [P, HCH, SEQ])
        c_xb = sb("c_xb", [P, UPS, CH])
        f_y = sb("f_y", [P, TILES, CH])
        f_st6 = sb("f_st6", [P, TILES // 4, 6])
        f_st2 = sb("f_st2", [P, TILES // 4, 2])
        f_rstd = sb("f_rstd", [P, TILES // 4])

        wide = [ctx.enter_context(nc.psum_tensor(f"wide{i}", [P, 1024], F32)) for i in range(3)]
        bank = [ctx.enter_context(nc.psum_tensor(f"bank{i}", [P, 512], F32)) for i in range(2)]

        x_loaded = sem("x_loaded")
        const_loaded = sem("const_loaded")
        attn_w_loaded = sem("attn_w_loaded")
        ffn_w_loaded = sem("ffn_w_loaded")
        out_stored = sem("out_stored")
        zeroed = sem("zeroed")
        prep_dve = sem("prep_dve")
        root_in = sem("root_in")
        root_ready = sem("root_ready")
        pool_eps = sem("pool_eps")
        quad_logs_in = sem("quad_logs_in")
        quad_logs = sem("quad_logs")
        feat_bias_ready = sem("feat_bias_ready")
        feat_ends_exp = sem("feat_ends_exp")
        prep_done = sem("prep_done")
        masks_ready = sem("masks_ready")
        a_var = [sem(f"a_var{i}") for i in range(3)]
        a_rstd = [sem(f"a_rstd{i}") for i in range(3)]
        a_ss_ready = sem("a_ss_ready")
        a_rn_ready = sem("a_rn_ready")
        den_ready = sem("den_ready")
        xc_part = sem("xc_part")
        xn_ready = sem("xn_ready")
        xnT_ps = sem("xnT_ps")
        xnT_sb = sem("xnT_sb")
        aqkv_ps = sem("aqkv_ps")
        aqkv_sb = sem("aqkv_sb")
        asq_sb = sem("asq_sb")
        vz_ready = sem("vz_ready")
        aqkn_ready = sem("aqkn_ready")
        aqkT_ps = sem("aqkT_ps")
        aqkT_sb = sem("aqkT_sb")
        feat_ps = sem("feat_ps")
        feat_exp = sem("feat_exp")
        feat_clip = sem("feat_clip")
        aS_ps = sem("aS_ps")
        aS_diag = sem("aS_diag")
        aS_off = sem("aS_off")
        av_done = sem("av_done")
        aoT_sb = sem("aoT_sb")
        ao_ps = sem("ao_ps")
        ao_ready = sem("ao_ready")
        ao2_ps = sem("ao2_ps")
        ao2_sb = sem("ao2_sb")
        ay_ps = sem("ay_ps")
        xc_ready = sem("xc_ready")
        tables_dve = sem("tables_dve")
        tables_ready = sem("tables_ready")
        b_ss_ready = sem("b_ss_ready")
        b_rn_ready = sem("b_rn_ready")
        rot_a = sem("rot_a")
        mx_ready = sem("mx_ready")
        rs_ready = sem("rs_ready")
        bx_ready = sem("bx_ready")
        hT_ps = sem("hT_ps")
        hT_sb = sem("hT_sb")
        qk_ps = sem("qk_ps")
        sq_sb = sem("sq_sb")
        v_ps = sem("v_ps")
        v_sb = sem("v_sb")
        qkn_ready = sem("qkn_ready")
        rot_b = sem("rot_b")
        rot_ready = sem("rot_ready")
        qkT_ps = sem("qkT_ps")
        qT_sb = sem("qT_sb")
        kz_sb = sem("kz_sb")
        s_ps = sem("s_ps")
        p_in = sem("p_in")
        p_exp = sem("p_exp")
        pT_ps = sem("pT_ps")
        pT_sb = sem("pT_sb")
        o_ps = sem("o_ps")
        o_ready = sem("o_ready")
        oT_ps = sem("oT_ps")
        oT_sb = sem("oT_sb")
        wo_ps = sem("wo_ps")
        attn_added = sem("attn_added")
        c_var = sem("c_var")
        c_rstd_ready = sem("c_rstd_ready")
        cx_ready = sem("cx_ready")
        fT_ps = sem("fT_ps")
        fT_sb = sem("fT_sb")
        fh_ps = sem("fh_ps")
        fhn_ready = sem("fhn_ready")
        fhnT_ps = sem("fhnT_ps")
        fhnT_sb = sem("fhnT_sb")
        w1_ps = sem("w1_ps")
        gelu_sb = sem("gelu_sb")
        act_ready = sem("act_ready")
        xb_ready = sem("xb_ready")
        w2_ps = sem("w2_ps")
        f_var = sem("f_var")
        f_rstd_ready = sem("f_rstd_ready")
        f_ready = sem("f_ready")

        CONST_LOADS = 15
        ATTN_LOADS = 4
        FFN_LOADS = 13
        TABLE_OPS = 3 * UPS
        STEPS_B = TILES
        STEPS_C = BATCH

        block = ctx.enter_context(nc.Block())

        def xt(buf, b, u=0, n=1):
            return buf[:, bass.ds(b * UPS + u, n), :]

        def flat(t):
            return t.rearrange("p a c -> p (a c)")

        def one(buf, b, u):
            return flat(xt(buf, b, u))

        @block.sync
        def _(sp):
            xv = x.rearrange("b (u p) c -> p (b u) c", p=P)
            for part in range(4):
                lo = part * TILES // 4
                sp.dma_start(x1[:, lo:lo + TILES // 4, :], xv[:, lo:lo + TILES // 4, :]).then_inc(x_loaded, 16)
            for dst, src in ((ident, c_ident), (causal, c_causal), (owner, c_owner), (node_sel, c_node),
                             (rot_cos, c_rot_cos), (rot_sin, c_rot_sin), (masks_f, c_masks),
                             (a_wqkv, Wqkv), (a_wout, Wout)):
                sp.dma_start(dst[:], src).then_inc(const_loaded, 16)
            sp.dma_start(a_bqkv[:], bqkv.partition_broadcast(P)).then_inc(const_loaded, 16)
            sp.dma_start(a_bout[:], bout.partition_broadcast(P)).then_inc(const_loaded, 16)
            for r in range(A_R):
                sp.dma_start(omega_rows[:, r, :], omega[r].rearrange("h d m -> (h d) m")).then_inc(const_loaded, 16)
            sp.dma_start(quad[:, 0, :], nodes.partition_broadcast(P)).then_inc(const_loaded, 16)
            sp.dma_start(quad[:, 1, :], weights.partition_broadcast(P)).then_inc(const_loaded, 16)
            for l in range(DEPTH):
                if l:
                    sp.wait_ge(wo_ps, l * STEPS_B)
                    sp.wait_ge(tables_ready, l * TABLE_OPS)
                sp.dma_start(b_wqkv[:], wqkv[l]).then_inc(attn_w_loaded, 16)
                sp.dma_start(b_wo[:], wo[l].rearrange("(k p) n -> p k n", p=P)).then_inc(attn_w_loaded, 16)
                sp.dma_start(qk_scale[:, 0, :], q_scale[l].partition_broadcast(P)).then_inc(attn_w_loaded, 16)
                sp.dma_start(qk_scale[:, 1, :], k_scale[l].partition_broadcast(P)).then_inc(attn_w_loaded, 16)
                if l:
                    sp.wait_ge(xc_ready, (l + 1) * STEPS_C)
                    sp.wait_ge(fhnT_sb, l * STEPS_C)
                    sp.wait_ge(gelu_sb, l * STEPS_C)
                    sp.wait_ge(xb_ready, l * STEPS_C)
                else:
                    sp.wait_ge(zeroed, 7)
                for g in range(2):
                    sp.dma_start(c_w1[:, g, 0:HID], w1[l][:, g * HID:(g + 1) * HID]).then_inc(ffn_w_loaded, 16)
                    for c in range(HCH):
                        n = P if c < HCH - 1 else HLAST
                        at = g * HID + c * P
                        sp.dma_start(c_b1[0:n, g, c:c + 1], b1[l][at:at + n].unsqueeze(1)).then_inc(ffn_w_loaded, 16)
                sp.dma_start(c_w2[:, 0:HCH - 1, :],
                             w2[l][0:(HCH - 1) * P].rearrange("(k p) n -> p k n", p=P)).then_inc(ffn_w_loaded, 16)
                sp.dma_start(c_w2[0:HLAST, HCH - 1, :], w2[l][(HCH - 1) * P:HID]).then_inc(ffn_w_loaded, 16)
                sp.dma_start(c_b2[:], b2[l].partition_broadcast(P)).then_inc(ffn_w_loaded, 16)
                sp.dma_start(c_lg[:], ln_g[l].unsqueeze(1)).then_inc(ffn_w_loaded, 16)
                sp.dma_start(c_lb[:], ln_b[l].unsqueeze(1)).then_inc(ffn_w_loaded, 16)
            ov = out.rearrange("b (u p) c -> p (b u) c", p=P)
            for part in range(4):
                lo = part * TILES // 4
                sp.wait_ge(f_ready, part + 1)
                sp.dma_start(ov[:, lo:lo + TILES // 4, :], f_y[:, lo:lo + TILES // 4, :]).then_inc(out_stored, 16)
            sp.wait_ge(out_stored, 4 * 16)

        ZEROED = 7
        SET = UPS * GROUPS + 5

        @block.gpsimd
        def _(pool):
            G = nc.gpsimd
            for buf in (c_w1, c_w2, c_b1, a_kz, a_vz, hT, b_kz):
                G.memset(buf[:], 0.0).then_inc(zeroed, 1)
            pool.wait_ge(zeroed, ZEROED)
            for u in range(UPS):
                for g in range(GROUPS):
                    first = GH * A_DIM
                    G.memset(a_vz[:, u, g, first:first + (GH - 1) * (GROWS + 1) + 1:GROWS + 1],
                             1.0).then_inc(zeroed, 1)
            G.memset(b_v[:], 1.0).then_inc(zeroed, 1)
            G.memset(power[:, 0:1], -0.5).then_inc(zeroed, 1)
            G.memset(power[:, 1:2], 0.5).then_inc(zeroed, 1)
            G.memset(power[:, 2:3], EPS).then_inc(zeroed, 1)
            G.memset(power[:, 3:4], 0.0).then_inc(zeroed, 1)
            pool.wait_ge(zeroed, ZEROED + SET)

            def inverse_root(out, x):
                shape = list(out.shape)
                G.tensor_tensor(x, x, power[:, 2:3].broadcast_to(shape), ALU.add)
                pool.drain()
                return G.tensor_tensor(out, x, power[:, 0:1].broadcast_to(shape), ALU.pow)

            def inverse_norm(out, x):
                G.tensor_tensor(out, x, power[:, 0:1].broadcast_to(list(out.shape)), ALU.pow)
                pool.drain()
                return G.tensor_scalar(out, out, 1e12, None, ALU.min)

            pool.wait_ge(root_in, 1)
            G.tensor_tensor(quad_t[:, 4], quad_t[:, 3], power[:, 1:2].broadcast_to([P, A_R]),
                            ALU.pow).then_inc(root_ready, 1)

            def a_rstds(i, g):
                pool.wait_ge(a_var[i], g + 1)
                inverse_root(rstd[:, i], st2[:, i, :, 1]).then_inc(a_rstd[i], 1)

            def a_head_norms(g):
                pool.wait_ge(a_ss_ready, g + 1)
                inverse_norm(a_rn[:], a_ss[:]).then_inc(a_rn_ready, 1)

            def a_step(g, more):
                if more:
                    a_rstds(0, g + 1)
                    a_head_norms(g + 1)
                a_rstds(1, g)
                a_rstds(2, g)

            a_rstds(0, 0)
            a_head_norms(0)
            with pool.Fori(0, BATCH - 1) as g:
                a_step(g, True)
            a_step(BATCH - 1, False)
            with pool.Fori(0, DEPTH) as l:
                pool.wait_ge(attn_w_loaded, (l + 1) * (ATTN_LOADS * 16))
                pool.wait_ge(const_loaded, CONST_LOADS * 16)
                pool.wait_ge(xc_ready, l * STEPS_C + 1)
                for u in range(UPS):
                    G.tensor_tensor(t_cos[:, u], rot_cos[:, u], qk_scale[:], ALU.mult).then_inc(tables_ready, 1)
                    for half in range(2):
                        here = slice(half * DIM // 2, (half + 1) * DIM // 2)
                        there = slice((1 - half) * DIM // 2, (2 - half) * DIM // 2)
                        G.tensor_tensor(t_sin[:, u, :, here], rot_sin[:, u, :, here],
                                        qk_scale[:, :, there], ALU.mult).then_inc(tables_ready, 1)

                def taken(b, u):
                    G.tensor_copy(b_x[:], one(xc, b, u)).then_inc(bx_ready, 1)

                def turned(m, u):
                    pool.wait_ge(b_ss_ready, m + 1)
                    inverse_norm(b_rn[:], b_ss[:]).then_inc(b_rn_ready, 1)
                    pool.wait_ge(qkn_ready, m + 1)
                    src = b_qkn[:].rearrange("p (a h b d) -> p a h b d", a=2, h=HEADS, b=2)
                    dst = b_rb[:].rearrange("p (a h b d) -> p a h b d", a=2, h=HEADS, b=2)
                    for half in range(2):
                        sin = t_sin[:, u, :, half * DIM // 2:(half + 1) * DIM // 2]
                        sin = sin.unsqueeze(2).broadcast_to([P, 2, HEADS, DIM // 2])
                        G.tensor_tensor(dst[:, :, :, half, :], src[:, :, :, 1 - half, :], sin,
                                        ALU.mult).then_inc(rot_b, 1)

                m0 = l * STEPS_B
                taken(0, 0)
                pool.wait_ge(tables_ready, (l + 1) * TABLE_OPS)
                turned(m0, 0)
                with pool.Fori(0, BATCH - 1) as b:
                    taken(b, 1)
                    turned(m0 + b * UPS + 1, 1)
                    pool.wait_ge(xc_ready, l * STEPS_C + b + 2)
                    taken(b + 1, 0)
                    turned(m0 + b * UPS + 2, 0)
                taken(BATCH - 1, 1)
                turned(m0 + TILES - 1, 1)
                pool.wait_ge(rot_ready, (l + 1) * STEPS_B)

                def stream_out(b):
                    if isinstance(b, int):
                        ins = G.tensor_tensor(c_x[:], xt(xc, b, 0, UPS),
                                              power[:, 3:4].unsqueeze(2).broadcast_to([P, UPS, CH]), ALU.add)
                    else:
                        ins = G.tensor_copy(c_x[:], xt(xc, b, 0, UPS))
                    ins.then_inc(cx_ready, 1)

                def stream_biased(m):
                    pool.wait_ge(cx_ready, m + 1)
                    G.tensor_tensor(c_xb[:], c_x[:], c_b2[:].unsqueeze(1).broadcast_to([P, UPS, CH]),
                                    ALU.add).then_inc(xb_ready, 1)

                def rstds(m):
                    pool.wait_ge(c_var, m + 1)
                    inverse_root(c_rstd[:], c_st2[:, :, 1]).then_inc(c_rstd_ready, 1)

                m1 = l * STEPS_C
                pool.wait_ge(attn_added, l * STEPS_B + UPS)
                stream_out(0)
                pool.wait_ge(ffn_w_loaded, (l + 1) * (FFN_LOADS * 16))
                stream_biased(m1)
                rstds(m1)
                with pool.Fori(0, BATCH - 1) as b:
                    pool.wait_ge(attn_added, l * STEPS_B + b * UPS + 2 * UPS)
                    pool.wait_ge(fT_ps, m1 + b + 1)
                    pool.wait_ge(xb_ready, m1 + b + 1)
                    stream_out(b + 1)
                    rstds(m1 + b + 1)
                    pool.wait_ge(xc_ready, m1 + STEPS_C + b + 1)
                    stream_biased(m1 + b + 1)

            with pool.Fori(0, 4) as f:
                pool.wait_ge(f_var, f + 1)
                inverse_root(f_rstd[:], f_st2[:, :, 1]).then_inc(f_rstd_ready, 1)

        @block.scalar
        def _(act):
            def copy(dst, src):
                return nc.scalar.activation(dst, src, ACT.Copy)

            act.wait_ge(quad_logs_in, 1)
            nc.scalar.activation(quad_t[:, 1], quad_t[:, 0], ACT.Ln).then_inc(quad_logs, 1)
            act.wait_ge(feat_bias_ready, 1)
            nc.scalar.activation(feat_ends[:], quad_t[:, 7], ACT.Exp).then_inc(feat_ends_exp, 1)

            def a_front1(g):
                act.wait_ge(xnT_ps, g + 1)
                copy(xnT[:], bank[0][:, 0:SEQ]).then_inc(xnT_sb, 1)

            def a_front2(g):
                act.wait_ge(aqkv_sb, (g + 1) * UPS)
                nc.scalar.activation(a_sq[:], a_qkv[:, :, 0:2 * CH], ACT.Square).then_inc(asq_sb, 1)

            def a_front3(g):
                act.wait_ge(aqkT_ps, g + 1)
                copy(a_qkT[:], bank[0][:].rearrange("p (a t) -> p a t", a=2)).then_inc(aqkT_sb, 1)

            def a_pair_exp(g, p):
                act.wait_ge(feat_ps, g * PAIRS + p + 1)
                at = p % 2 * 512
                nc.scalar.activation(a_exp[:, p % 2], wide[0][:, at:at + 512].rearrange("p (a t) -> p a t", a=2),
                                     ACT.Exp, bias=feat_bias[:, 0:1]).then_inc(feat_exp, 1)

            def a_pair_off(g, p):
                act.wait_ge(aS_ps, g * PAIRS + p + 1)
                copy(a_S[:, :, SEQ:SEQ + P],
                     wide[1][:, 512:512 + SEQ].rearrange("p (h t) -> p h t", t=P)).then_inc(aS_off, 1)

            def a_step(g, more):
                for k in range(PAIRS + 1):
                    if k < PAIRS:
                        a_pair_exp(g, k)
                    if k == 2 and more:
                        a_front1(g + 1)
                    if k >= 1:
                        a_pair_off(g, k - 1)
                    if k == 5 and more:
                        a_front2(g + 1)
                if more:
                    a_front3(g + 1)
                act.wait_ge(av_done, g + 1)
                copy(a_oT[:], wide[2][0:GROWS].rearrange("p (g c) -> p g c", c=512)[:, :, 0:SEQ]).then_inc(aoT_sb, 1)
                act.wait_ge(ao2_ps, g + 1)
                copy(a_oT2[:], bank[1][:, 0:SEQ]).then_inc(ao2_sb, 1)

            a_front1(0)
            a_front2(0)
            a_front3(0)
            act.wait_ge(prep_done, 1)
            with act.Fori(0, BATCH - 1) as g:
                a_step(g, True)
            a_step(BATCH - 1, False)

            with act.Fori(0, DEPTH) as l:
                def b_front1(m, u):
                    act.wait_ge(hT_ps, m + 1)
                    at = WIN + u * P
                    copy(hT[0:64, at:at + P], bank[1][0:64, 0:P]).then_inc(hT_sb, 1)
                    copy(hT[64:P, at + 1:at + 1 + P], bank[1][64:P, 0:P]).then_inc(hT_sb, 1)

                def b_front2(m, u):
                    act.wait_ge(qk_ps, m + 1)
                    nc.scalar.activation(b_sq[:], wide[1][:], ACT.Square).then_inc(sq_sb, 1)

                def b_front3(m, u):
                    act.wait_ge(v_ps, m + 1)
                    copy(b_v[:, u, :, :, 0:DIM],
                         wide[2][:].rearrange("p (w h d) -> p w h d", w=2, h=HEADS)).then_inc(v_sb, 1)

                def b_front4(m, u):
                    act.wait_ge(qkT_ps, m + 1)
                    copy(b_qT[:], wide[1][:, 0:512].rearrange("p (k t) -> p k t", t=P)).then_inc(qT_sb, 1)

                def b_step(m, u, more):
                    if more:
                        b_front1(m + 1, 1 - u)
                        b_front2(m + 1, 1 - u)
                    act.wait_ge(p_in, m + 1)
                    nc.scalar.activation(b_p[:], b_p[:], ACT.Exp).then_inc(p_exp, 1)
                    if more:
                        b_front3(m + 1, 1 - u)
                    act.wait_ge(pT_ps, m + 1)
                    copy(b_pT[:], wide[0][:].rearrange("p (h t) -> p h t", t=P)).then_inc(pT_sb, 1)
                    act.wait_ge(oT_ps, m + 1)
                    copy(b_oT[:], bank[0][:].rearrange("p (k t) -> p k t", t=P)).then_inc(oT_sb, 1)
                    if more:
                        b_front4(m + 1, 1 - u)

                m0 = l * STEPS_B
                for front in (b_front1, b_front2, b_front3, b_front4):
                    front(m0, 0)
                with act.Fori(0, BATCH - 1) as b:
                    for u in range(UPS):
                        b_step(m0 + b * UPS + u, u, True)
                b_step(m0 + TILES - 2, 0, True)
                b_step(m0 + TILES - 1, 1, False)

                def c_front1(m):
                    act.wait_ge(fT_ps, m + 1)
                    copy(hT[0:64, WIN:WIN + SEQ], bank[0][0:64, 0:SEQ]).then_inc(fT_sb, 1)
                    copy(hT[64:P, WIN + 1:WIN + 1 + SEQ], bank[0][64:P, 0:SEQ]).then_inc(fT_sb, 1)

                def c_front2(m):
                    act.wait_ge(fhnT_ps, m + 1)
                    nc.scalar.activation(c_hT[:], bank[0][:, 0:SEQ], ACT.Identity, bias=c_lb[:],
                                         scale=c_lg[:]).then_inc(fhnT_sb, 1)

                def c_step(m, more):
                    if more:
                        c_front1(m + 1)
                    act.wait_ge(w1_ps, m + 1)
                    for c in range(HCH):
                        last = nc.scalar.activation(c_gelu[:, c], wide[1][:, c * SEQ:(c + 1) * SEQ], ACT.Gelu,
                                                    bias=c_b1[:, 1, c:c + 1])
                    last.then_inc(gelu_sb, 1)
                    if more:
                        c_front2(m + 1)

                act.wait_ge(ffn_w_loaded, (l + 1) * (FFN_LOADS * 16))
                m1 = l * STEPS_C
                c_front1(m1)
                c_front2(m1)
                with act.Fori(0, BATCH - 1) as b:
                    c_step(m1 + b, True)
                c_step(m1 + BATCH - 1, False)

        @block.vector
        def _(dve):
            V = nc.vector

            def mult(out, a, b):
                return V.tensor_tensor(out, a, b, ALU.mult)

            def stats(tiles, st6, st2, own=True):
                if own:
                    dve.drain()
                for i, t in enumerate(tiles):
                    V.bn_stats(st6[:, i], t)
                dve.drain()
                for i in range(len(tiles)):
                    last = V.bn_aggr(st2[:, i], st6[:, i])
                return last

            def normalised(out, t, i, st2, rstd):
                return V.tensor_scalar(out, t, st2[:, i, 0:1], rstd[:, i:i + 1], ALU.subtract, ALU.mult)

            def then(ins):
                ins.then_inc(prep_dve, 1)
                prep_count[0] += 1
                dve.wait_ge(prep_dve, prep_count[0])

            prep_count = [0]

            dve.wait_ge(const_loaded, CONST_LOADS * 16)
            V.tensor_scalar(quad_t[:, 0], quad[:, 1], 1.0 / A_M, 2.0 ** -63, ALU.mult, ALU.max).then_inc(quad_logs_in, 1)
            V.tensor_copy(masks[:], masks_f[:].unsqueeze(2).broadcast_to([P, 2, 4, KEYS])).then_inc(masks_ready, 1)
            V.tensor_copy(ident_bf[:], ident[:]).then_inc(masks_ready, 1)
            then(V.tensor_scalar(quad_t[:, 2], quad[:, 1], 0.0, None, ALU.is_gt))
            V.tensor_scalar(quad_t[:, 3], quad[:, 0], 0.0, 2.0, ALU.max, ALU.mult).then_inc(root_in, 1)
            dve.wait_ge(root_ready, 1)
            then(mult(omega_rows[:], omega_rows[:], quad_t[:, 4].unsqueeze(2).broadcast_to([P, A_R, A_M])))
            then(mult(omega_pad[:],
                           omega_rows[:].rearrange("p r m -> p (r m)").unsqueeze(1).broadcast_to([P, A_HEADS, A_FEAT]),
                           owner[:].unsqueeze(2).broadcast_to([P, A_HEADS, A_FEAT])))
            dve.wait_ge(quad_logs, 1)
            then(V.tensor_scalar(quad_t[:, 1], quad_t[:, 1], 0.5, None, ALU.mult))
            then(V.tensor_tensor(quad_t[:, 5], quad_t[:, 1], quad[:, 0], ALU.subtract))
            then(mult(feat_sel[:, 0], quad_t[:, 5], node_sel[:]))
            then(mult(feat_sel[:, 1], quad_t[:, 1], node_sel[:]))
            then(V.tensor_reduce(out=feat_bias[:], in_=feat_sel[:], axis=AXX, op=ALU.add))
            then(V.tensor_scalar(quad_t[:, 7, 0:1], feat_bias[:, 1:2], -CLIP, None, ALU.add))
            V.tensor_scalar(quad_t[:, 7, 1:2], feat_bias[:, 1:2], CLIP, None, ALU.add).then_inc(feat_bias_ready, 1)
            then(mult(feat_sel[:, 0], quad_t[:, 2], node_sel[:]))
            then(V.tensor_reduce(out=feat_sel[:, 1, 0:1], in_=feat_sel[:, 0], axis=AXX, op=ALU.add))
            dve.wait_ge(feat_ends_exp, 1)
            then(mult(feat_ends[:], feat_ends[:], feat_sel[:, 1, 0:1].broadcast_to([P, 2])))
            V.tensor_copy(quad_t[:, 5], quad_t[:, 4]).then_inc(prep_done, 1)

            def a_front1(g):
                stats([one(x1, g, u) for u in range(UPS)], st6[:, 0], st2[:, 0]).then_inc(a_var[0], 1)

            def a_front1b(g):
                dve.wait_ge(a_rstd[0], g + 1)
                for u in range(UPS):
                    normalised(xn[:, u], one(x1, g, u), u, st2[:, 0], rstd[:, 0]).then_inc(xn_ready, 1)

            def a_front2(g):
                dve.wait_ge(aqkv_ps, g + 1)
                for u in range(UPS):
                    V.tensor_tensor(a_qkv[:, u], bank[u][:, 0:3 * CH], a_bqkv[:], ALU.add).then_inc(aqkv_sb, 1)

            def a_front3(g):
                dve.wait_ge(asq_sb, g + 1)
                V.tensor_reduce(out=a_ss[:], in_=a_sq[:].rearrange("p u (h d) -> p (u h) d", d=A_DIM),
                                axis=AXX, op=ALU.add).then_inc(a_ss_ready, 1)

            def a_front3b(g):
                dve.wait_ge(a_rn_ready, g + 1)
                dve.wait_ge(aqkv_sb, (g + 1) * UPS)
                for u in range(UPS):
                    r = a_rn[:, u * 2 * A_HEADS:(u + 1) * 2 * A_HEADS].unsqueeze(2)
                    mult(a_qkn[:, u].rearrange("p (h d) -> p h d", d=A_DIM),
                         a_qkv[:, u, 0:2 * CH].rearrange("p (h d) -> p h d", d=A_DIM),
                         r.broadcast_to([P, 2 * A_HEADS, A_DIM])).then_inc(aqkn_ready, 1)

            def a_front4(g):
                for u in range(UPS):
                    V.tensor_copy(
                        a_vz[:, u].rearrange("p g (h c) -> p g h c", c=GROWS + A_DIM)[:, :, :, 0:A_DIM],
                        a_qkv[:, u, 2 * CH:3 * CH].rearrange("p (g h d) -> p g h d", g=GROUPS, d=A_DIM)
                    ).then_inc(vz_ready, 1)

            def a_pair_clip(g, p):
                dve.wait_ge(feat_exp, g * PAIRS + p + 1)
                V.tensor_scalar(a_qf[:, p % 2], a_exp[:, p % 2, 0], feat_ends[:, 0:1], feat_ends[:, 1:2],
                                ALU.max, ALU.min).then_inc(feat_clip, 1)
                for hh in range(2):
                    rows = slice(64 * hh, 64 * hh + 64)
                    V.tensor_scalar(a_kz[rows, p % 2, hh], a_exp[rows, p % 2, 1], feat_ends[rows, 0:1],
                                    feat_ends[rows, 1:2], ALU.max, ALU.min).then_inc(feat_clip, 1)

            def a_pair_diag(g, p):
                dve.wait_ge(aS_ps, g * PAIRS + p + 1)
                mult(a_S[:, :, 0:SEQ].rearrange("p h (a t) -> p h a t", t=P),
                     wide[1][:, 0:512].rearrange("p (h a t) -> p h a t", h=2, t=P),
                     causal[:].unsqueeze(1).unsqueeze(1).broadcast_to([P, 2, 2, P])).then_inc(aS_diag, 1)

            def a_step(g, more):
                for k in range(PAIRS + 1):
                    if k < PAIRS:
                        a_pair_clip(g, k)
                    if k == 0 and more:
                        a_front1(g + 1)
                    if k == 1 and more:
                        a_front1b(g + 1)
                    if k >= 1:
                        a_pair_diag(g, k - 1)
                    if k == 3 and more:
                        a_front2(g + 1)
                    if k == 4 and more:
                        a_front3(g + 1)
                if more:
                    a_front3b(g + 1)
                dve.wait_ge(av_done, g + 1)
                if more:
                    a_front4(g + 1)
                dve.wait_ge(ao_ps, g + 1)
                o_v = bank[1][:, 0:UPS * GROUPS * GROWS].rearrange("p (a c) -> p a c", c=GROWS)
                V.tensor_scalar(a_den[:, 0].rearrange("p (a h) -> p a h", h=GH), o_v[:, :, GH * A_DIM:GROWS],
                                1e-6, None, ALU.max).then_inc(den_ready, 1)
                dve.wait_ge(den_ready, g * 2 + 1)
                V.reciprocal(a_den[:, 1], a_den[:, 0]).then_inc(den_ready, 1)
                dve.wait_ge(den_ready, g * 2 + 2)
                mult(a_o[:].rearrange("p u (g h d) -> p (u g) h d", g=GROUPS, d=A_DIM),
                     o_v[:, :, 0:GH * A_DIM].rearrange("p a (h d) -> p a h d", d=A_DIM),
                     a_den[:, 1].rearrange("p (a h) -> p a h", h=GH).unsqueeze(3)
                     .broadcast_to([P, UPS * GROUPS, GH, A_DIM])).then_inc(ao_ready, 1)
                dve.wait_ge(ay_ps, g + 1)
                V.tensor_tensor(a_y[:], bank[1][:, 0:SEQ].rearrange("p (u c) -> p u c", u=UPS),
                                a_bout[:].unsqueeze(1).broadcast_to([P, UPS, CH]), ALU.add)
                stats([a_y[:, u] for u in range(UPS)], st6[:, 1], st2[:, 1]).then_inc(a_var[1], 1)
                dve.wait_ge(a_rstd[1], g + 1)
                for u in range(UPS):
                    normalised(a_y[:, u], a_y[:, u], u, st2[:, 1], rstd[:, 1])
                dve.drain()
                V.tensor_tensor(xt(x1, g, 0, UPS), xt(x1, g, 0, UPS), a_y[:], ALU.add)
                stats([one(x1, g, u) for u in range(UPS)], st6[:, 2], st2[:, 2]).then_inc(a_var[2], 1)
                dve.wait_ge(a_rstd[2], g + 1)
                for u in range(UPS):
                    ins = normalised(one(xc, g, u), one(x1, g, u), u, st2[:, 2], rstd[:, 2])
                ins.then_inc(xc_ready, 1)

            dve.wait_ge(x_loaded, 4 * 16)
            for front in (a_front1, a_front1b, a_front2, a_front3, a_front3b):
                front(0)
            dve.wait_ge(zeroed, ZEROED + SET)
            a_front4(0)
            with dve.Fori(0, BATCH - 1) as g:
                a_step(g, True)
            a_step(BATCH - 1, False)

            with dve.Fori(0, DEPTH) as l:
                def b_front1(m, u):
                    dve.wait_ge(sq_sb, m + 1)
                    V.tensor_reduce(out=b_ss[:], in_=b_sq[:].rearrange("p (h d) -> p h d", d=DIM),
                                    axis=AXX, op=ALU.add).then_inc(b_ss_ready, 1)
                    dve.wait_ge(b_rn_ready, m + 1)
                    heads = "p (h d) -> p h d"
                    mult(b_qkn[:].rearrange(heads, d=DIM), wide[1][:].rearrange(heads, d=DIM),
                         b_rn[:].unsqueeze(2).broadcast_to([P, 2 * HEADS, DIM])).then_inc(qkn_ready, 1)
                    dve.wait_ge(qkn_ready, m + 1)
                    each = "p (a h d) -> p a h d"
                    mult(b_ra[:].rearrange(each, a=2, d=DIM), b_qkn[:].rearrange(each, a=2, d=DIM),
                         t_cos[:, u].unsqueeze(2).broadcast_to([P, 2, HEADS, DIM])).then_inc(rot_a, 1)
                    dve.wait_ge(rot_a, m + 1)
                    dve.wait_ge(rot_b, m * 2 + 2)
                    V.tensor_tensor(b_ra[:], b_ra[:], b_rb[:], ALU.add).then_inc(rot_ready, 1)

                def b_front2(m, u):
                    dve.wait_ge(qkT_ps, m + 1)
                    src = wide[1][:, 512:1024].rearrange("p (k t) -> p k t", t=P)
                    at = WIN + u * P
                    for hh in range(2):
                        rows = slice(64 * hh, 64 * hh + 64)
                        V.tensor_copy(b_kz[rows, :, hh, at:at + P], src[rows]).then_inc(kz_sb, 1)

                def b_step(m, b, u, more):
                    dve.wait_ge(s_ps, m + 1)
                    s_v = wide[0][:].rearrange("p (h j) -> p h j", j=KEYS)
                    V.tensor_reduce(out=b_mx[:], in_=s_v, axis=AXX, op=ALU.max).then_inc(mx_ready, 1)
                    dve.wait_ge(mx_ready, m + 1)
                    V.tensor_tensor(b_p[:], s_v, b_mx[:].unsqueeze(2).broadcast_to([P, HEADS, KEYS]),
                                    ALU.subtract).then_inc(p_in, 1)
                    if more:
                        b_front1(m + 1, 1 - u)
                    dve.wait_ge(o_ps, m + 1)
                    o_v = wide[2][:].rearrange("p (g c) -> p g c", c=512)[:, :, 0:4 * VCOL]
                    o_v = o_v.rearrange("p g (h d) -> p g h d", d=VCOL)
                    rs = b_rs[:].rearrange("p (g h) -> p g h", g=2).unsqueeze(3)
                    V.reciprocal(rs, o_v[:, :, :, DIM:VCOL]).then_inc(rs_ready, 1)
                    dve.wait_ge(rs_ready, m + 1)
                    mult(b_o[:].rearrange("p (g h) d -> p g h d", g=2), o_v[:, :, :, 0:DIM],
                         rs.broadcast_to([P, 2, HEADS // 2, DIM])).then_inc(o_ready, 1)
                    dve.wait_ge(wo_ps, m + 1)
                    V.tensor_tensor(one(xc, b, u), one(xc, b, u), bank[1][:, P:P + CH],
                                    ALU.add).then_inc(attn_added, 1)
                    if more:
                        b_front2(m + 1, 1 - u)

                m0 = l * STEPS_B
                dve.wait_ge(tables_ready, (l + 1) * TABLE_OPS)
                b_front1(m0, 0)
                b_front2(m0, 0)
                with dve.Fori(0, BATCH - 1) as b:
                    for u in range(UPS):
                        b_step(m0 + b * UPS + u, b, u, True)
                b_step(m0 + TILES - 2, BATCH - 1, 0, True)
                b_step(m0 + TILES - 1, BATCH - 1, 1, False)

                def c_front1(m):
                    dve.wait_ge(fh_ps, m + 1)
                    tiles = [bank[1][:, u * CH:(u + 1) * CH] for u in range(UPS)]
                    stats(tiles, c_st6, c_st2, own=False).then_inc(c_var, 1)
                    dve.wait_ge(c_rstd_ready, m + 1)
                    for u in range(UPS):
                        normalised(c_hn[:, u], tiles[u], u, c_st2, c_rstd).then_inc(fhn_ready, 1)

                def c_step(m, b, more):
                    dve.wait_ge(gelu_sb, m + 1)
                    for c in range(HCH):
                        V.scalar_tensor_tensor(out=c_act[:, c], in0=wide[0][:, c * SEQ:(c + 1) * SEQ],
                                               scalar=c_b1[:, 0, c:c + 1], in1=c_gelu[:, c],
                                               op0=ALU.add, op1=ALU.mult).then_inc(act_ready, 1)
                    if more:
                        c_front1(m + 1)
                    dve.wait_ge(w2_ps, m + 1)
                    dve.wait_ge(xb_ready, m + 1)
                    V.tensor_tensor(xt(xc, b, 0, UPS), c_xb[:],
                                    wide[2][:, 0:SEQ].rearrange("p (u c) -> p u c", u=UPS),
                                    ALU.add).then_inc(xc_ready, 1)

                m1 = l * STEPS_C
                dve.wait_ge(ffn_w_loaded, (l + 1) * (FFN_LOADS * 16))
                c_front1(m1)
                with dve.Fori(0, BATCH - 1) as b:
                    c_step(m1 + b, b, True)
                c_step(m1 + BATCH - 1, BATCH - 1, False)

            part = TILES // 4
            dve.wait_ge(xc_ready, (DEPTH + 1) * STEPS_C)
            with dve.Fori(0, 4) as f:
                def tile(buf, i):
                    return flat(buf[:, bass.ds(f * part + i, 1), :])

                stats([tile(xc, i) for i in range(part)], f_st6, f_st2).then_inc(f_var, 1)
                dve.wait_ge(f_rstd_ready, f + 1)
                for i in range(part):
                    normalised(tile(f_y, i), tile(xc, i), i, f_st2, f_rstd)
                dve.drain()
                here = bass.ds(f * part, part)
                V.tensor_tensor(f_y[:, here, :], f_y[:, here, :], x1[:, here, :], ALU.add).then_inc(f_ready, 1)

        @block.tensor
        def _(pe):
            T = nc.tensor

            def a_front1(g):
                pe.wait_ge(xn_ready, (g + 1) * UPS)
                for u in range(UPS):
                    last = T.transpose(bank[0][:, u * P:(u + 1) * P], xn[:, u], ident[:])
                last.then_inc(xnT_ps, 1)

            def a_front2(g):
                pe.wait_ge(xnT_sb, g + 1)
                for u in range(UPS):
                    last = T.matmul(bank[u][:, 0:3 * CH], xnT[:, u * P:(u + 1) * P], a_wqkv[:], start=True, stop=True)
                last.then_inc(aqkv_ps, 1)

            def a_front3(g):
                pe.wait_ge(aqkn_ready, (g + 1) * UPS)
                for a in range(2):
                    for u in range(UPS):
                        last = T.transpose(bank[0][:, a * SEQ + u * P:a * SEQ + (u + 1) * P],
                                           a_qkn[:, u, a * CH:(a + 1) * CH], ident[:])
                last.then_inc(aqkT_ps, 1)

            def a_pair_feat(g, p):
                half = p % 2 * 512
                T.matmul(wide[0][:, half:half + 512], omega_pad[:, 2 * p:2 * p + 2, :].rearrange("p a f -> p (a f)"),
                         a_qkT[:].rearrange("p a t -> p (a t)"), start=True, stop=True).then_inc(feat_ps, 1)

            def a_pair_scores(g, p):
                pe.wait_ge(feat_clip, g * (3 * PAIRS) + 3 * p + 3)
                for hh in range(2):
                    for keys, queries, at in ((1, 1, hh * SEQ), (0, 0, hh * SEQ + P), (0, 1, 512 + hh * P)):
                        last = T.matmul(wide[1][:, at:at + P], a_kz[:, p % 2, hh, keys * P:(keys + 1) * P],
                                        a_qf[:, p % 2, queries * P:(queries + 1) * P], start=True, stop=True)
                last.then_inc(aS_ps, 1)

            def a_pair_values(g, p):
                pe.wait_ge(aS_diag, g * PAIRS + p + 1)
                pe.wait_ge(aS_off, g * PAIRS + p + 1)
                for hh in range(2):
                    grp, h = divmod(2 * p + hh, GH)
                    cols = slice(h * GROWS, (h + 1) * GROWS)
                    at = grp * 512
                    T.matmul(wide[2][0:GROWS, at:at + SEQ], a_vz[:, 0, grp, cols], a_S[:, hh, P:P + SEQ],
                             start=h == 0, stop=False)
                    last = T.matmul(wide[2][0:GROWS, at + P:at + SEQ], a_vz[:, 1, grp, cols], a_S[:, hh, 0:P],
                                    start=False, stop=h == GH - 1)
                if p == PAIRS - 1:
                    last.then_inc(av_done, 1)

            def a_step(g, more):
                pe.wait_ge(aqkT_sb, g + 1)
                for k in range(PAIRS + 2):
                    if k < PAIRS:
                        a_pair_feat(g, k)
                    if k == 2 and more:
                        a_front1(g + 1)
                    if k == 4 and more:
                        a_front2(g + 1)
                    if k == 2:
                        pe.wait_ge(vz_ready, (g + 1) * UPS)
                    if k >= 2:
                        a_pair_values(g, k - 2)
                    if 1 <= k <= PAIRS:
                        a_pair_scores(g, k - 1)
                if more:
                    a_front3(g + 1)
                pe.wait_ge(aoT_sb, g + 1)
                for u in range(UPS):
                    for grp in range(GROUPS):
                        at = (u * GROUPS + grp) * GROWS
                        last = T.transpose(bank[1][:, at:at + GROWS], a_oT[:, grp, u * P:(u + 1) * P],
                                           ident[0:GROWS, 0:GROWS])
                last.then_inc(ao_ps, 1)
                pe.wait_ge(ao_ready, g + 1)
                for u in range(UPS):
                    last = T.transpose(bank[1][:, u * P:(u + 1) * P], a_o[:, u], ident[:])
                last.then_inc(ao2_ps, 1)
                pe.wait_ge(ao2_sb, g + 1)
                for u in range(UPS):
                    last = T.matmul(bank[1][:, u * CH:(u + 1) * CH], a_oT2[:, u * P:(u + 1) * P], a_wout[:],
                                    start=True, stop=True)
                last.then_inc(ay_ps, 1)

            pe.wait_ge(const_loaded, CONST_LOADS * 16)
            a_front1(0)
            a_front2(0)
            a_front3(0)
            pe.wait_ge(prep_done, 1)
            with pe.Fori(0, BATCH - 1) as g:
                a_step(g, True)
            a_step(BATCH - 1, False)

            pe.wait_ge(masks_ready, 2)
            with pe.Fori(0, DEPTH) as l:
                def b_front1(m, u):
                    pe.wait_ge(bx_ready, m + 1)
                    T.transpose(bank[1][:, 0:P], b_x[:], ident[:]).then_inc(hT_ps, 1)

                def b_front2(m, u):
                    pe.wait_ge(hT_sb, m * 2 + 2)
                    at = WIN + u * P
                    for a in range(2):
                        last = T.matmul(wide[1][:, a * INNER:(a + 1) * INNER], hT[:, at:at + P],
                                        b_wqkv[:, a * INNER:(a + 1) * INNER], start=True, stop=True)
                    last.then_inc(qk_ps, 1)
                    for w in range(2):
                        at = u * P + w * WIN
                        last = T.matmul(wide[2][:, w * INNER:(w + 1) * INNER], hT[:, at:at + KEYS],
                                        b_wqkv[:, 2 * INNER:3 * INNER], start=True, stop=True)
                    last.then_inc(v_ps, 1)

                def b_front3(m, u):
                    pe.wait_ge(rot_ready, m + 1)
                    for c in range(2 * HP):
                        last = T.transpose(wide[1][:, c * P:(c + 1) * P], b_ra[:, c * P:(c + 1) * P], ident[:])
                    last.then_inc(qkT_ps, 1)

                def b_scores(m, u):
                    kind = 0 if u == 0 else 1
                    for half in range(2):
                        T.matmul(wide[0][:, half * 512:half * 512 + 512], ident_bf[:],
                                 masks[:, kind].rearrange("p h j -> p (h j)"), start=True, stop=False)
                        for k in range(half * HP // 2, (half + 1) * HP // 2):
                            for w in range(2):
                                at = u * P + w * WIN
                                last = T.matmul(wide[0][w * WIN:(w + 1) * WIN, k * 2 * KEYS:(k + 1) * 2 * KEYS],
                                                b_qT[:, k, w * WIN:(w + 1) * WIN], b_kz[:, k, :, at:at + KEYS],
                                                start=False, stop=k % 2 == 1)
                    last.then_inc(s_ps, 1)

                def b_step(m, u, more):
                    pe.wait_ge(qT_sb, m + 1)
                    pe.wait_ge(kz_sb, m * 2 + 2)
                    if more:
                        b_front1(m + 1, 1 - u)
                    b_scores(m, u)
                    if more:
                        b_front2(m + 1, 1 - u)
                    pe.wait_ge(p_exp, m + 1)
                    for h in range(HEADS):
                        last = T.transpose(wide[0][:, h * P:(h + 1) * P], b_p[:, h], ident[:])
                    last.then_inc(pT_ps, 1)
                    pe.wait_ge(pT_sb, m + 1)
                    pe.wait_ge(v_sb, m + 2 if more else m + 1)
                    for h in range(HEADS):
                        for w in range(2):
                            at = h // 4 * 512 + h % 4 * VCOL
                            last = T.matmul(wide[2][w * WIN:(w + 1) * WIN, at:at + VCOL],
                                            b_pT[:, h, w * WIN:(w + 1) * WIN], b_v[:, u, w, h, :],
                                            start=True, stop=True)
                    last.then_inc(o_ps, 1)
                    pe.wait_ge(o_ready, m + 1)
                    for k in range(HP):
                        last = T.transpose(bank[0][:, k * P:(k + 1) * P],
                                           b_o[:, 2 * k:2 * k + 2].rearrange("p h d -> p (h d)"), ident[:])
                    last.then_inc(oT_ps, 1)
                    pe.wait_ge(oT_sb, m + 1)
                    for k in range(HP):
                        last = T.matmul(bank[1][:, P:P + CH], b_oT[:, k], b_wo[:, k], start=k == 0, stop=k == HP - 1)
                    last.then_inc(wo_ps, 1)
                    if more:
                        b_front3(m + 1, 1 - u)

                m0 = l * STEPS_B
                pe.wait_ge(attn_w_loaded, (l + 1) * (ATTN_LOADS * 16))
                pe.wait_ge(xc_ready, (l + 1) * STEPS_C)
                for front in (b_front1, b_front2, b_front3):
                    front(m0, 0)
                with pe.Fori(0, BATCH - 1) as b:
                    for u in range(UPS):
                        b_step(m0 + b * UPS + u, u, True)
                b_step(m0 + TILES - 2, 0, True)
                b_step(m0 + TILES - 1, 1, False)

                def c_front1(m):
                    pe.wait_ge(cx_ready, m + 1)
                    for u in range(UPS):
                        last = T.transpose(bank[0][:, u * P:(u + 1) * P], c_x[:, u], ident[:])
                    last.then_inc(fT_ps, 1)

                def c_front2(m):
                    pe.wait_ge(fT_sb, m * 2 + 2)
                    for u in range(UPS):
                        at = WIN + u * P
                        last = T.transpose(bank[1][:, u * P:(u + 1) * P], hT[:, at:at + P], ident[:])
                    last.then_inc(fh_ps, 1)

                def c_front3(m):
                    pe.wait_ge(fhn_ready, (m + 1) * UPS)
                    for u in range(UPS):
                        last = T.transpose(bank[0][:, u * P:(u + 1) * P], c_hn[:, u], ident[:])
                    last.then_inc(fhnT_ps, 1)

                def c_step(m, more):
                    pe.wait_ge(fhnT_sb, m + 1)
                    if more:
                        c_front1(m + 1)
                    for g in (1, 0):
                        for c in range(HCH):
                            last = T.matmul(wide[g][:, c * SEQ:(c + 1) * SEQ], c_w1[:, g, c * P:(c + 1) * P],
                                            c_hT[:], start=True, stop=True)
                    last.then_inc(w1_ps, 1)
                    if more:
                        c_front2(m + 1)
                    pe.wait_ge(act_ready, (m + 1) * HCH)
                    for u in range(UPS):
                        for c in range(HCH):
                            last = T.matmul(wide[2][:, u * CH:(u + 1) * CH], c_act[:, c, u * P:(u + 1) * P],
                                            c_w2[:, c], start=c == 0, stop=c == HCH - 1)
                    last.then_inc(w2_ps, 1)
                    if more:
                        c_front3(m + 1)

                m1 = l * STEPS_C
                pe.wait_ge(ffn_w_loaded, (l + 1) * (FFN_LOADS * 16))
                c_front1(m1)
                pe.wait_ge(attn_added, (l + 1) * STEPS_B)
                c_front2(m1)
                c_front3(m1)
                with pe.Fori(0, BATCH - 1) as b:
                    c_step(m1 + b, True)
                c_step(m1 + BATCH - 1, False)


_INS = ['L0_attn_x', 'L0_attn_Wqkv', 'L0_attn_bqkv', 'L0_attn_Wout', 'L0_attn_bout', 'L0_attn_omega',
        'L0_attn_quad_nodes', 'L0_attn_quad_weights', 'L0_ffn_wqkv', 'L0_ffn_q_scale', 'L0_ffn_k_scale',
        'L0_ffn_wo', 'L0_ffn_ln_g', 'L0_ffn_ln_b', 'L0_ffn_w1', 'L0_ffn_b1', 'L0_ffn_w2', 'L0_ffn_b2']


def kernel(**inputs):
    import concourse.bacc as bacc
    from concourse.bass_utils import run_bass_kernel_spmd

    nc = bacc.Bacc("TRN2", target_bir_lowering=False, num_devices=1)
    arrays, args = {}, []
    constants = shape_constants()
    for name, a in [(n, inputs[n]) for n in _INS] + list(constants.items()):
        a = np.ascontiguousarray(a)
        arrays[name] = a
        args.append(nc.dram_tensor(name, a.shape, mybir.dt.from_np(a.dtype), kind="ExternalInput").ap())
    result = nc.dram_tensor("result", (BATCH, SEQ, CH), F32, kind="ExternalOutput").ap()
    build(nc, *args, result)
    r = run_bass_kernel_spmd(nc, [arrays], core_ids=[0])
    return r.results[0]["result"]
```

```python
from contextlib import ExitStack

import concourse.bass as bass
import numpy as np
from concourse import mybir

P = 128
F32 = mybir.dt.float32
BF16 = mybir.dt.bfloat16
ALU = mybir.AluOpType
ACT = mybir.ActivationFunctionType
AXX = mybir.AxisListType.X

BATCH, SEQ, CH = 8, 256, 128
TILES = BATCH * SEQ // P
UPS = SEQ // P
DEPTH = 2
A_HEADS, A_DIM, A_M, A_R = 16, 8, 32, 2
A_FEAT = A_R * A_M
PAIRS = A_HEADS // 2
GROUPS = 2
GH = A_HEADS // GROUPS
GROWS = GH * A_DIM + GH
CLIP = 20.0
HEADS, DIM, WIN = 8, 64, 64
INNER = HEADS * DIM
HP = HEADS // 2
QK_SCALE = -8.0
KEYS = 2 * WIN
VCOL = DIM + 1
MASKED = 1e30
HID = CH * 4 * 2 // 3
HCH = -(-HID // P)
HLAST = HID - (HCH - 1) * P
EPS = 1e-5


def shape_constants():
    half = np.arange(0, DIM, 2, dtype=np.float32)
    inv_freq = (np.float32(1.0) / np.float32(10000.0) ** (half / np.float32(DIM))).astype(np.float32)
    t = np.arange(SEQ, dtype=np.float32)
    freqs = t[:, None] * inv_freq[None, :]
    base = ((half + np.float32(0.4 * DIM)) / np.float32(1.4 * DIM)).astype(np.float32)
    power = (t - SEQ // 2) / np.float32(WIN // 2)
    scale = base[None, :] ** power[:, None]
    cos, sin = np.cos(freqs), np.sin(freqs)
    cos, sin = np.concatenate([cos, cos], 1), np.concatenate([-sin, sin], 1)
    scale = np.concatenate([scale, scale], 1)
    rot = np.stack([np.stack([cos * scale * QK_SCALE, cos / scale], 1),
                    np.stack([sin * scale * QK_SCALE, sin / scale], 1)], 0)
    rot = rot.reshape(2, UPS, P, 2, DIM).transpose(0, 2, 1, 3, 4).astype(np.float32)
    q = np.arange(WIN)[:, None] + WIN
    k = np.arange(KEYS)[None, :]
    seen = (k <= q) & (q <= k + WIN)
    mask = np.where(seen, 0.0, MASKED)
    first = np.where(seen & (k >= WIN), 0.0, MASKED)
    masks = np.stack([np.concatenate([first, mask]), np.concatenate([mask, mask])], 1)
    s = np.arange(P)
    causal = (s[:, None] <= s[None, :]).astype(np.float32)
    owner = (s[:, None] // A_DIM == np.arange(A_HEADS)[None, :]).astype(np.float32)
    node = ((s[:, None] // A_M) % A_R == np.arange(A_R)[None, :]).astype(np.float32)
    return {
        "c_rot_cos": np.ascontiguousarray(rot[0]), "c_rot_sin": np.ascontiguousarray(rot[1]),
        "c_masks": masks.astype(np.float32), "c_ident": np.eye(P, dtype=np.float32),
        "c_causal": causal, "c_owner": owner, "c_node": node,
    }


def build(nc, x, Wqkv, bqkv, Wout, bout, omega, nodes, weights, wqkv, q_scale, k_scale, wo, ln_g, ln_b,
          w1, b1, w2, b2, c_rot_cos, c_rot_sin, c_masks, c_ident, c_causal, c_owner, c_node, out):
    with ExitStack() as ctx:
        def sb(name, shape, dt=F32):
            return ctx.enter_context(nc.sbuf_tensor(name, shape, dt))

        def sem(name):
            return ctx.enter_context(nc.semaphore(name))

        x1 = sb("x1", [P, TILES, CH])
        xc = sb("xc", [P, TILES, CH])
        ident = sb("ident", [P, P])
        ident_bf = sb("ident_bf", [P, P], BF16)
        causal = sb("causal", [P, P])
        owner = sb("owner", [P, A_HEADS])
        node_sel = sb("node_sel", [P, A_R])
        rot_cos = sb("rot_cos", [P, UPS, 2, DIM])
        rot_sin = sb("rot_sin", [P, UPS, 2, DIM])
        masks_f = sb("masks_f", [P, 2, KEYS])
        masks = sb("masks", [P, 2, 4, KEYS], BF16)
        a_wqkv = sb("a_wqkv", [P, 3 * CH])
        a_bqkv = sb("a_bqkv", [P, 3 * CH])
        a_wout = sb("a_wout", [P, CH])
        a_bout = sb("a_bout", [P, CH])
        omega_rows = sb("omega_rows", [P, A_R, A_M])
        omega_pad = sb("omega_pad", [P, A_HEADS, A_FEAT])
        quad = sb("quad", [P, 2, A_R])
        quad_t = sb("quad_t", [P, 8, A_R])
        feat_sel = sb("feat_sel", [P, 2, A_R])
        feat_bias = sb("feat_bias", [P, 2])
        feat_ends = sb("feat_ends", [P, 2])
        power = sb("power", [P, 4])
        st6 = sb("st6", [P, 3, UPS, 6])
        st2 = sb("st2", [P, 3, UPS, 2])
        rstd = sb("rstd", [P, 3, UPS])
        a_ss = sb("a_ss", [P, UPS * 2 * A_HEADS])
        a_rn = sb("a_rn", [P, UPS * 2 * A_HEADS])
        xn = sb("xn", [P, UPS, CH])
        xnT = sb("xnT", [P, SEQ])
        a_qkv = sb("a_qkv", [P, UPS, 3 * CH])
        a_sq = sb("a_sq", [P, UPS, 2 * CH])
        a_qkn = sb("a_qkn", [P, UPS, 2 * CH])
        a_qkT = sb("a_qkT", [P, 2, SEQ])
        a_exp = sb("a_exp", [P, 2, 2, SEQ])
        a_qf = sb("a_qf", [P, 2, SEQ])
        a_kz = sb("a_kz", [P, 2, 2, SEQ])
        a_S = sb("a_S", [P, 2, SEQ + P])
        a_vz = sb("a_vz", [P, UPS, GROUPS, GH * (GROWS + A_DIM)])
        a_oT = sb("a_oT", [GROWS, GROUPS, SEQ])
        a_den = sb("a_den", [P, 2, UPS * GROUPS * GH])
        a_o = sb("a_o", [P, UPS, CH])
        a_oT2 = sb("a_oT2", [P, SEQ])
        a_y = sb("a_y", [P, UPS, CH])
        b_wqkv = sb("b_wqkv", [P, 3 * INNER])
        b_wo = sb("b_wo", [P, HP, CH])
        qk_scale = sb("qk_scale", [P, 2, DIM])
        t_cos = sb("t_cos", [P, UPS, 2, DIM])
        t_sin = sb("t_sin", [P, UPS, 2, DIM])
        hT = sb("hT", [P, WIN + SEQ + 1])
        b_x = sb("b_x", [P, CH])
        b_sq = sb("b_sq", [P, 2 * INNER])
        b_ss = sb("b_ss", [P, 2 * HEADS])
        b_rn = sb("b_rn", [P, 2 * HEADS])
        b_qk_rot = sb("b_qk_rot", [P, 2 * INNER])
        b_ra = sb("b_ra", [P, 2 * INNER])
        b_rb = sb("b_rb", [P, 2 * INNER])
        b_qT = sb("b_qT", [P, HP, P])
        b_kz = sb("b_kz", [P, HP, 2, WIN + SEQ])
        b_v = sb("b_v", [P, 2, 2, HEADS, VCOL])
        b_mx = sb("b_mx", [P, HEADS])
        b_p = sb("b_p", [P, HEADS, KEYS])
        b_pT = sb("b_pT", [P, HEADS, P])
        b_rs = sb("b_rs", [P, HEADS])
        b_o = sb("b_o", [P, HEADS, DIM])
        b_oT = sb("b_oT", [P, HP, P])
        c_w1 = sb("c_w1", [P, 2, HCH * P])
        c_w2 = sb("c_w2", [P, HCH, CH])
        c_b1 = sb("c_b1", [P, 2, HCH])
        c_b2 = sb("c_b2", [P, CH])
        c_lg = sb("c_lg", [P, 1])
        c_lb = sb("c_lb", [P, 1])
        c_x = sb("c_x", [P, UPS, CH])
        c_hn = sb("c_hn", [P, UPS, CH])
        c_hT = sb("c_hT", [P, SEQ])
        c_st6 = sb("c_st6", [P, UPS, 6])
        c_st2 = sb("c_st2", [P, UPS, 2])
        c_rstd = sb("c_rstd", [P, UPS])
        c_gelu = sb("c_gelu", [P, HCH, SEQ])
        c_act = sb("c_act", [P, HCH, SEQ])
        c_xb = sb("c_xb", [P, UPS, CH])
        f_y = sb("f_y", [P, TILES, CH])
        f_st6 = sb("f_st6", [P, TILES // 4, 6])
        f_st2 = sb("f_st2", [P, TILES // 4, 2])
        f_rstd = sb("f_rstd", [P, TILES // 4])

        wide = [ctx.enter_context(nc.psum_tensor(f"wide{i}", [P, 1024], F32)) for i in range(3)]
        bank = [ctx.enter_context(nc.psum_tensor(f"bank{i}", [P, 512], F32)) for i in range(2)]

        x_loaded = sem("x_loaded")
        const_loaded = sem("const_loaded")
        attn_w_loaded = sem("attn_w_loaded")
        ffn_w_loaded = sem("ffn_w_loaded")
        out_stored = sem("out_stored")
        zeroed = sem("zeroed")
        prep_dve = sem("prep_dve")
        root_in = sem("root_in")
        root_ready = sem("root_ready")
        pool_eps = sem("pool_eps")
        quad_logs_in = sem("quad_logs_in")
        quad_logs = sem("quad_logs")
        feat_bias_ready = sem("feat_bias_ready")
        feat_ends_exp = sem("feat_ends_exp")
        prep_done = sem("prep_done")
        masks_ready = sem("masks_ready")
        a_var = [sem(f"a_var{i}") for i in range(3)]
        a_rstd = [sem(f"a_rstd{i}") for i in range(3)]
        a_ss_ready = sem("a_ss_ready")
        a_rn_ready = sem("a_rn_ready")
        den_ready = sem("den_ready")
        xc_part = sem("xc_part")
        xn_ready = sem("xn_ready")
        xnT_ps = sem("xnT_ps")
        xnT_sb = sem("xnT_sb")
        aqkv_ps = sem("aqkv_ps")
        aqkv_sb = sem("aqkv_sb")
        asq_sb = sem("asq_sb")
        vz_ready = sem("vz_ready")
        aqkn_ready = sem("aqkn_ready")
        aqkT_ps = sem("aqkT_ps")
        aqkT_sb = sem("aqkT_sb")
        feat_ps = sem("feat_ps")
        feat_exp = sem("feat_exp")
        feat_clip = sem("feat_clip")
        aS_ps = sem("aS_ps")
        aS_diag = sem("aS_diag")
        aS_off = sem("aS_off")
        av_done = sem("av_done")
        aoT_sb = sem("aoT_sb")
        ao_ps = sem("ao_ps")
        ao_ready = sem("ao_ready")
        ao2_ps = sem("ao2_ps")
        ao2_sb = sem("ao2_sb")
        ay_ps = sem("ay_ps")
        xc_ready = sem("xc_ready")
        tables_dve = sem("tables_dve")
        tables_ready = sem("tables_ready")
        b_ss_ready = sem("b_ss_ready")
        b_rn_ready = sem("b_rn_ready")
        rot_a = sem("rot_a")
        rot_sum = sem("rot_sum")
        mx_ready = sem("mx_ready")
        rs_ready = sem("rs_ready")
        bx_ready = sem("bx_ready")
        hT_ps = sem("hT_ps")
        hT_sb = sem("hT_sb")
        qk_ps = sem("qk_ps")
        sq_sb = sem("sq_sb")
        v_ps = sem("v_ps")
        v_sb = sem("v_sb")
        rot_ready = sem("rot_ready")
        qkT_ps = sem("qkT_ps")
        qT_sb = sem("qT_sb")
        kz_sb = sem("kz_sb")
        s_ps = sem("s_ps")
        p_exp = sem("p_exp")
        pT_ps = sem("pT_ps")
        pT_sb = sem("pT_sb")
        o_ps = sem("o_ps")
        o_ready = sem("o_ready")
        oT_ps = sem("oT_ps")
        oT_sb = sem("oT_sb")
        wo_ps = sem("wo_ps")
        attn_added = sem("attn_added")
        c_var = sem("c_var")
        c_rstd_ready = sem("c_rstd_ready")
        cx_ready = sem("cx_ready")
        fT_ps = sem("fT_ps")
        fT_sb = sem("fT_sb")
        fh_ps = sem("fh_ps")
        fhn_ready = sem("fhn_ready")
        fhnT_ps = sem("fhnT_ps")
        fhnT_sb = sem("fhnT_sb")
        w1_ps = sem("w1_ps")
        gelu_sb = sem("gelu_sb")
        act_ready = sem("act_ready")
        xb_ready = sem("xb_ready")
        w2_ps = sem("w2_ps")
        f_var = sem("f_var")
        f_rstd_ready = sem("f_rstd_ready")
        f_ready = sem("f_ready")

        CONST_LOADS = 15
        ATTN_LOADS = 4
        FFN_LOADS = 13
        TABLE_OPS = 3 * UPS
        STEPS_B = TILES
        STEPS_C = BATCH

        block = ctx.enter_context(nc.Block())

        def xt(buf, b, u=0, n=1):
            return buf[:, bass.ds(b * UPS + u, n), :]

        def flat(t):
            return t.rearrange("p a c -> p (a c)")

        def one(buf, b, u):
            return flat(xt(buf, b, u))

        @block.sync
        def _(sp):
            xv = x.rearrange("b (u p) c -> p (b u) c", p=P)
            for part in range(4):
                lo = part * TILES // 4
                sp.dma_start(x1[:, lo:lo + TILES // 4, :], xv[:, lo:lo + TILES // 4, :]).then_inc(x_loaded, 16)
            for dst, src in ((ident, c_ident), (causal, c_causal), (owner, c_owner), (node_sel, c_node),
                             (rot_cos, c_rot_cos), (rot_sin, c_rot_sin), (masks_f, c_masks),
                             (a_wqkv, Wqkv), (a_wout, Wout)):
                sp.dma_start(dst[:], src).then_inc(const_loaded, 16)
            sp.dma_start(a_bqkv[:], bqkv.partition_broadcast(P)).then_inc(const_loaded, 16)
            sp.dma_start(a_bout[:], bout.partition_broadcast(P)).then_inc(const_loaded, 16)
            for r in range(A_R):
                sp.dma_start(omega_rows[:, r, :], omega[r].rearrange("h d m -> (h d) m")).then_inc(const_loaded, 16)
            sp.dma_start(quad[:, 0, :], nodes.partition_broadcast(P)).then_inc(const_loaded, 16)
            sp.dma_start(quad[:, 1, :], weights.partition_broadcast(P)).then_inc(const_loaded, 16)
            for l in range(DEPTH):
                if l:
                    sp.wait_ge(wo_ps, l * STEPS_B)
                    sp.wait_ge(tables_ready, l * TABLE_OPS)
                sp.dma_start(b_wqkv[:], wqkv[l]).then_inc(attn_w_loaded, 16)
                sp.dma_start(b_wo[:], wo[l].rearrange("(k p) n -> p k n", p=P)).then_inc(attn_w_loaded, 16)
                sp.dma_start(qk_scale[:, 0, :], q_scale[l].partition_broadcast(P)).then_inc(attn_w_loaded, 16)
                sp.dma_start(qk_scale[:, 1, :], k_scale[l].partition_broadcast(P)).then_inc(attn_w_loaded, 16)
                if l:
                    sp.wait_ge(xc_ready, (l + 1) * STEPS_C)
                    sp.wait_ge(fhnT_sb, l * STEPS_C)
                    sp.wait_ge(gelu_sb, l * STEPS_C)
                    sp.wait_ge(xb_ready, l * STEPS_C)
                else:
                    sp.wait_ge(zeroed, 7)
                for g in range(2):
                    sp.dma_start(c_w1[:, g, 0:HID], w1[l][:, g * HID:(g + 1) * HID]).then_inc(ffn_w_loaded, 16)
                    for c in range(HCH):
                        n = P if c < HCH - 1 else HLAST
                        at = g * HID + c * P
                        sp.dma_start(c_b1[0:n, g, c:c + 1], b1[l][at:at + n].unsqueeze(1)).then_inc(ffn_w_loaded, 16)
                sp.dma_start(c_w2[:, 0:HCH - 1, :],
                             w2[l][0:(HCH - 1) * P].rearrange("(k p) n -> p k n", p=P)).then_inc(ffn_w_loaded, 16)
                sp.dma_start(c_w2[0:HLAST, HCH - 1, :], w2[l][(HCH - 1) * P:HID]).then_inc(ffn_w_loaded, 16)
                sp.dma_start(c_b2[:], b2[l].partition_broadcast(P)).then_inc(ffn_w_loaded, 16)
                sp.dma_start(c_lg[:], ln_g[l].unsqueeze(1)).then_inc(ffn_w_loaded, 16)
                sp.dma_start(c_lb[:], ln_b[l].unsqueeze(1)).then_inc(ffn_w_loaded, 16)
            ov = out.rearrange("b (u p) c -> p (b u) c", p=P)
            for part in range(4):
                lo = part * TILES // 4
                sp.wait_ge(f_ready, part + 1)
                sp.dma_start(ov[:, lo:lo + TILES // 4, :], f_y[:, lo:lo + TILES // 4, :]).then_inc(out_stored, 16)
            sp.wait_ge(out_stored, 4 * 16)

        ZEROED = 7
        SET = UPS * GROUPS + 5

        @block.gpsimd
        def _(pool):
            G = nc.gpsimd
            for buf in (c_w1, c_w2, c_b1, a_kz, a_vz, hT, b_kz):
                G.memset(buf[:], 0.0).then_inc(zeroed, 1)
            pool.wait_ge(zeroed, ZEROED)
            for u in range(UPS):
                for g in range(GROUPS):
                    first = GH * A_DIM
                    G.memset(a_vz[:, u, g, first:first + (GH - 1) * (GROWS + 1) + 1:GROWS + 1],
                             1.0).then_inc(zeroed, 1)
            G.memset(b_v[:], 1.0).then_inc(zeroed, 1)
            G.memset(power[:, 0:1], -0.5).then_inc(zeroed, 1)
            G.memset(power[:, 1:2], 0.5).then_inc(zeroed, 1)
            G.memset(power[:, 2:3], EPS).then_inc(zeroed, 1)
            G.memset(power[:, 3:4], 0.0).then_inc(zeroed, 1)
            pool.wait_ge(zeroed, ZEROED + SET)

            def inverse_root(out, x):
                shape = list(out.shape)
                G.tensor_tensor(x, x, power[:, 2:3].broadcast_to(shape), ALU.add)
                pool.drain()
                return G.tensor_tensor(out, x, power[:, 0:1].broadcast_to(shape), ALU.pow)

            def copied(out, x, b):
                if isinstance(b, int):
                    return G.tensor_tensor(out, x, power[:, 3:4].unsqueeze(2).broadcast_to(list(out.shape)), ALU.add)
                return G.tensor_copy(out, x)

            def inverse_norm(out, x):
                G.tensor_tensor(out, x, power[:, 0:1].broadcast_to(list(out.shape)), ALU.pow)
                pool.drain()
                return G.tensor_scalar(out, out, 1e12, None, ALU.min)

            pool.wait_ge(root_in, 1)
            G.tensor_tensor(quad_t[:, 4], quad_t[:, 3], power[:, 1:2].broadcast_to([P, A_R]),
                            ALU.pow).then_inc(root_ready, 1)

            def a_rstds(i, g):
                pool.wait_ge(a_var[i], g + 1)
                inverse_root(rstd[:, i], st2[:, i, :, 1]).then_inc(a_rstd[i], 1)

            def a_head_norms(g):
                pool.wait_ge(a_ss_ready, g + 1)
                inverse_norm(a_rn[:], a_ss[:]).then_inc(a_rn_ready, 1)

            def a_step(g, more):
                if more:
                    a_rstds(0, g + 1)
                    a_head_norms(g + 1)
                a_rstds(1, g)
                a_rstds(2, g)

            a_rstds(0, 0)
            a_head_norms(0)
            with pool.Fori(0, BATCH - 1) as g:
                a_step(g, True)
            a_step(BATCH - 1, False)
            with pool.Fori(0, DEPTH) as l:
                pool.wait_ge(attn_w_loaded, (l + 1) * (ATTN_LOADS * 16))
                pool.wait_ge(const_loaded, CONST_LOADS * 16)
                pool.wait_ge(xc_ready, (l + 1) * STEPS_C)
                for u in range(UPS):
                    G.tensor_tensor(t_cos[:, u], rot_cos[:, u], qk_scale[:], ALU.mult).then_inc(tables_ready, 1)
                    for half in range(2):
                        here = slice(half * DIM // 2, (half + 1) * DIM // 2)
                        there = slice((1 - half) * DIM // 2, (2 - half) * DIM // 2)
                        G.tensor_tensor(t_sin[:, u, :, here], rot_sin[:, u, :, here],
                                        qk_scale[:, :, there], ALU.mult).then_inc(tables_ready, 1)

                def taken(m, b, u):
                    pool.wait_ge(hT_ps, m)
                    copied(b_x[:].unsqueeze(1), xt(xc, b, u), b).then_inc(bx_ready, 1)

                def head_norms(m):
                    pool.wait_ge(b_ss_ready, m + 1)
                    inverse_norm(b_rn[:], b_ss[:]).then_inc(b_rn_ready, 1)

                m0 = l * STEPS_B
                G.tensor_copy(b_x[:], one(xc, 0, 0)).then_inc(bx_ready, 1)
                taken(m0 + 1, 0, 1)
                head_norms(m0)
                head_norms(m0 + 1)
                with pool.Fori(0, BATCH - 1) as b:
                    for u in range(UPS):
                        m = m0 + b * UPS + u
                        taken(m + 2, b + 1, u)
                        head_norms(m + 2)

                def stream_out(b):
                    copied(c_x[:], xt(xc, b, 0, UPS), b).then_inc(cx_ready, 1)

                def stream_biased(m):
                    pool.wait_ge(cx_ready, m + 1)
                    G.tensor_tensor(c_xb[:], c_x[:], c_b2[:].unsqueeze(1).broadcast_to([P, UPS, CH]),
                                    ALU.add).then_inc(xb_ready, 1)

                def rstds(m):
                    pool.wait_ge(c_var, m + 1)
                    inverse_root(c_rstd[:], c_st2[:, :, 1]).then_inc(c_rstd_ready, 1)

                m1 = l * STEPS_C
                pool.wait_ge(attn_added, l * STEPS_B + UPS)
                stream_out(0)
                pool.wait_ge(ffn_w_loaded, (l + 1) * (FFN_LOADS * 16))
                stream_biased(m1)
                rstds(m1)
                with pool.Fori(0, BATCH - 1) as b:
                    pool.wait_ge(attn_added, l * STEPS_B + b * UPS + 2 * UPS)
                    pool.wait_ge(fT_ps, m1 + b + 1)
                    pool.wait_ge(xb_ready, m1 + b + 1)
                    stream_out(b + 1)
                    rstds(m1 + b + 1)
                    pool.wait_ge(xc_ready, m1 + STEPS_C + b + 1)
                    stream_biased(m1 + b + 1)

            with pool.Fori(0, 4) as f:
                pool.wait_ge(f_var, f + 1)
                inverse_root(f_rstd[:], f_st2[:, :, 1]).then_inc(f_rstd_ready, 1)

        @block.scalar
        def _(act):
            def copy(dst, src):
                return nc.scalar.activation(dst, src, ACT.Copy)

            act.wait_ge(quad_logs_in, 1)
            nc.scalar.activation(quad_t[:, 1], quad_t[:, 0], ACT.Ln).then_inc(quad_logs, 1)
            act.wait_ge(feat_bias_ready, 1)
            nc.scalar.activation(feat_ends[:], quad_t[:, 7], ACT.Exp).then_inc(feat_ends_exp, 1)

            def a_front1(g):
                act.wait_ge(xnT_ps, g + 1)
                copy(xnT[:], bank[0][:, 0:SEQ]).then_inc(xnT_sb, 1)

            def a_front2(g):
                act.wait_ge(aqkv_sb, (g + 1) * UPS)
                nc.scalar.activation(a_sq[:], a_qkv[:, :, 0:2 * CH], ACT.Square).then_inc(asq_sb, 1)

            def a_front3(g):
                act.wait_ge(aqkT_ps, g + 1)
                copy(a_qkT[:], bank[0][:].rearrange("p (a t) -> p a t", a=2)).then_inc(aqkT_sb, 1)

            def a_pair_exp(g, p):
                act.wait_ge(feat_ps, g * PAIRS + p + 1)
                at = p % 2 * 512
                nc.scalar.activation(a_exp[:, p % 2], wide[0][:, at:at + 512].rearrange("p (a t) -> p a t", a=2),
                                     ACT.Exp, bias=feat_bias[:, 0:1]).then_inc(feat_exp, 1)

            def a_pair_off(g, p):
                act.wait_ge(aS_ps, g * PAIRS + p + 1)
                copy(a_S[:, :, SEQ:SEQ + P],
                     wide[1][:, 512:512 + SEQ].rearrange("p (h t) -> p h t", t=P)).then_inc(aS_off, 1)

            def a_step(g, more):
                for k in range(PAIRS + 1):
                    if k < PAIRS:
                        a_pair_exp(g, k)
                    if k == 2 and more:
                        a_front1(g + 1)
                    if k >= 1:
                        a_pair_off(g, k - 1)
                    if k == 5 and more:
                        a_front2(g + 1)
                if more:
                    a_front3(g + 1)
                act.wait_ge(av_done, g + 1)
                copy(a_oT[:], wide[2][0:GROWS].rearrange("p (g c) -> p g c", c=512)[:, :, 0:SEQ]).then_inc(aoT_sb, 1)
                act.wait_ge(ao2_ps, g + 1)
                copy(a_oT2[:], bank[1][:, 0:SEQ]).then_inc(ao2_sb, 1)

            a_front1(0)
            a_front2(0)
            a_front3(0)
            act.wait_ge(prep_done, 1)
            with act.Fori(0, BATCH - 1) as g:
                a_step(g, True)
            a_step(BATCH - 1, False)

            with act.Fori(0, DEPTH) as l:
                def b_shifted(m, u):
                    act.wait_ge(hT_ps, m + 1)
                    at = WIN + u * P
                    copy(hT[0:64, at:at + P], bank[0][0:64, 0:P]).then_inc(hT_sb, 1)
                    copy(hT[64:P, at + 1:at + 1 + P], bank[0][64:P, 0:P]).then_inc(hT_sb, 1)

                def b_squares(m):
                    for a in range(2):
                        here = slice(a * INNER, (a + 1) * INNER)
                        act.wait_ge(qk_ps, m * 2 + 1 + a)
                        nc.scalar.activation(b_sq[:, here], wide[1][:, here], ACT.Square).then_inc(sq_sb, 1)

                def b_values(m, u):
                    act.wait_ge(v_ps, m + 1)
                    copy(b_v[:, u, :, :, 0:DIM],
                         wide[2][:].rearrange("p (w h d) -> p w h d", w=2, h=HEADS)).then_inc(v_sb, 1)

                def b_queries_keys(m, u):
                    act.wait_ge(qkT_ps, m + 1)
                    each = wide[2][:].rearrange("p (a k t) -> p a k t", a=2, t=P)
                    copy(b_qT[:], each[:, 0]).then_inc(qT_sb, 1)
                    at = WIN + u * P
                    for hh in range(2):
                        rows = slice(64 * hh, 64 * hh + 64)
                        copy(b_kz[rows, :, hh, at:at + P], each[rows, 1]).then_inc(kz_sb, 1)

                def b_exp(m, half):
                    if half == 0:
                        act.wait_ge(mx_ready, m + 1)
                    for h in range(half * HEADS // 2, (half + 1) * HEADS // 2):
                        last = nc.scalar.activation(b_p[:, h], wide[0][:, h * KEYS:(h + 1) * KEYS], ACT.Exp,
                                                    bias=b_mx[:, h:h + 1], scale=-1.0)
                    last.then_inc(p_exp, 1)

                def b_step(m, u, ahead1, ahead2):
                    b_exp(m, 0)
                    if ahead1:
                        b_values(m + 1, 1 - u)
                    b_exp(m, 1)
                    if ahead2:
                        b_shifted(m + 2, u)
                    act.wait_ge(pT_ps, m + 1)
                    copy(b_pT[:, 0:HEADS // 2],
                         wide[0][:, 0:512].rearrange("p (h t) -> p h t", t=P)).then_inc(pT_sb, 1)
                    if ahead1:
                        b_queries_keys(m + 1, 1 - u)
                    if ahead2:
                        b_squares(m + 2)
                    act.wait_ge(oT_ps, m + 1)
                    copy(b_oT[:], bank[0][:].rearrange("p (k t) -> p k t", t=P)).then_inc(oT_sb, 1)

                m0 = l * STEPS_B
                b_shifted(m0, 0)
                b_squares(m0)
                b_values(m0, 0)
                b_shifted(m0 + 1, 1)
                b_queries_keys(m0, 0)
                b_squares(m0 + 1)
                with act.Fori(0, BATCH - 1) as b:
                    for u in range(UPS):
                        b_step(m0 + b * UPS + u, u, True, True)
                b_step(m0 + TILES - 2, 0, True, False)
                b_step(m0 + TILES - 1, 1, False, False)

                def c_front1(m):
                    act.wait_ge(fT_ps, m + 1)
                    copy(hT[0:64, WIN:WIN + SEQ], bank[0][0:64, 0:SEQ]).then_inc(fT_sb, 1)
                    copy(hT[64:P, WIN + 1:WIN + 1 + SEQ], bank[0][64:P, 0:SEQ]).then_inc(fT_sb, 1)

                def c_front2(m):
                    act.wait_ge(fhnT_ps, m + 1)
                    nc.scalar.activation(c_hT[:], bank[0][:, 0:SEQ], ACT.Identity, bias=c_lb[:],
                                         scale=c_lg[:]).then_inc(fhnT_sb, 1)

                def c_step(m, more):
                    if more:
                        c_front1(m + 1)
                    act.wait_ge(w1_ps, m + 1)
                    for c in range(HCH):
                        last = nc.scalar.activation(c_gelu[:, c], wide[1][:, c * SEQ:(c + 1) * SEQ], ACT.Gelu,
                                                    bias=c_b1[:, 1, c:c + 1])
                    last.then_inc(gelu_sb, 1)
                    if more:
                        c_front2(m + 1)

                act.wait_ge(ffn_w_loaded, (l + 1) * (FFN_LOADS * 16))
                m1 = l * STEPS_C
                c_front1(m1)
                c_front2(m1)
                with act.Fori(0, BATCH - 1) as b:
                    c_step(m1 + b, True)
                c_step(m1 + BATCH - 1, False)

        @block.vector
        def _(dve):
            V = nc.vector

            def mult(out, a, b):
                return V.tensor_tensor(out, a, b, ALU.mult)

            def stats(tiles, st6, st2, own=True):
                if own:
                    dve.drain()
                for i, t in enumerate(tiles):
                    V.bn_stats(st6[:, i], t)
                dve.drain()
                for i in range(len(tiles)):
                    last = V.bn_aggr(st2[:, i], st6[:, i])
                return last

            def normalised(out, t, i, st2, rstd):
                return V.tensor_scalar(out, t, st2[:, i, 0:1], rstd[:, i:i + 1], ALU.subtract, ALU.mult)

            def then(ins):
                ins.then_inc(prep_dve, 1)
                prep_count[0] += 1
                dve.wait_ge(prep_dve, prep_count[0])

            prep_count = [0]

            dve.wait_ge(const_loaded, CONST_LOADS * 16)
            V.tensor_scalar(quad_t[:, 0], quad[:, 1], 1.0 / A_M, 2.0 ** -63, ALU.mult, ALU.max).then_inc(quad_logs_in, 1)
            V.tensor_copy(masks[:], masks_f[:].unsqueeze(2).broadcast_to([P, 2, 4, KEYS])).then_inc(masks_ready, 1)
            V.tensor_copy(ident_bf[:], ident[:]).then_inc(masks_ready, 1)
            then(V.tensor_scalar(quad_t[:, 2], quad[:, 1], 0.0, None, ALU.is_gt))
            V.tensor_scalar(quad_t[:, 3], quad[:, 0], 0.0, 2.0, ALU.max, ALU.mult).then_inc(root_in, 1)
            dve.wait_ge(root_ready, 1)
            then(mult(omega_rows[:], omega_rows[:], quad_t[:, 4].unsqueeze(2).broadcast_to([P, A_R, A_M])))
            then(mult(omega_pad[:],
                           omega_rows[:].rearrange("p r m -> p (r m)").unsqueeze(1).broadcast_to([P, A_HEADS, A_FEAT]),
                           owner[:].unsqueeze(2).broadcast_to([P, A_HEADS, A_FEAT])))
            dve.wait_ge(quad_logs, 1)
            then(V.tensor_scalar(quad_t[:, 1], quad_t[:, 1], 0.5, None, ALU.mult))
            then(V.tensor_tensor(quad_t[:, 5], quad_t[:, 1], quad[:, 0], ALU.subtract))
            then(mult(feat_sel[:, 0], quad_t[:, 5], node_sel[:]))
            then(mult(feat_sel[:, 1], quad_t[:, 1], node_sel[:]))
            then(V.tensor_reduce(out=feat_bias[:], in_=feat_sel[:], axis=AXX, op=ALU.add))
            then(V.tensor_scalar(quad_t[:, 7, 0:1], feat_bias[:, 1:2], -CLIP, None, ALU.add))
            V.tensor_scalar(quad_t[:, 7, 1:2], feat_bias[:, 1:2], CLIP, None, ALU.add).then_inc(feat_bias_ready, 1)
            then(mult(feat_sel[:, 0], quad_t[:, 2], node_sel[:]))
            then(V.tensor_reduce(out=feat_sel[:, 1, 0:1], in_=feat_sel[:, 0], axis=AXX, op=ALU.add))
            dve.wait_ge(feat_ends_exp, 1)
            then(mult(feat_ends[:], feat_ends[:], feat_sel[:, 1, 0:1].broadcast_to([P, 2])))
            V.tensor_copy(quad_t[:, 5], quad_t[:, 4]).then_inc(prep_done, 1)

            def a_front1(g):
                stats([one(x1, g, u) for u in range(UPS)], st6[:, 0], st2[:, 0]).then_inc(a_var[0], 1)

            def a_front1b(g):
                dve.wait_ge(a_rstd[0], g + 1)
                for u in range(UPS):
                    normalised(xn[:, u], one(x1, g, u), u, st2[:, 0], rstd[:, 0]).then_inc(xn_ready, 1)

            def a_front2(g):
                dve.wait_ge(aqkv_ps, g + 1)
                for u in range(UPS):
                    V.tensor_tensor(a_qkv[:, u], bank[u][:, 0:3 * CH], a_bqkv[:], ALU.add).then_inc(aqkv_sb, 1)

            def a_front3(g):
                dve.wait_ge(asq_sb, g + 1)
                V.tensor_reduce(out=a_ss[:], in_=a_sq[:].rearrange("p u (h d) -> p (u h) d", d=A_DIM),
                                axis=AXX, op=ALU.add).then_inc(a_ss_ready, 1)

            def a_front3b(g):
                dve.wait_ge(a_rn_ready, g + 1)
                dve.wait_ge(aqkv_sb, (g + 1) * UPS)
                for u in range(UPS):
                    r = a_rn[:, u * 2 * A_HEADS:(u + 1) * 2 * A_HEADS].unsqueeze(2)
                    mult(a_qkn[:, u].rearrange("p (h d) -> p h d", d=A_DIM),
                         a_qkv[:, u, 0:2 * CH].rearrange("p (h d) -> p h d", d=A_DIM),
                         r.broadcast_to([P, 2 * A_HEADS, A_DIM])).then_inc(aqkn_ready, 1)

            def a_front4(g):
                for u in range(UPS):
                    V.tensor_copy(
                        a_vz[:, u].rearrange("p g (h c) -> p g h c", c=GROWS + A_DIM)[:, :, :, 0:A_DIM],
                        a_qkv[:, u, 2 * CH:3 * CH].rearrange("p (g h d) -> p g h d", g=GROUPS, d=A_DIM)
                    ).then_inc(vz_ready, 1)

            def a_pair_clip(g, p):
                dve.wait_ge(feat_exp, g * PAIRS + p + 1)
                V.tensor_scalar(a_qf[:, p % 2], a_exp[:, p % 2, 0], feat_ends[:, 0:1], feat_ends[:, 1:2],
                                ALU.max, ALU.min).then_inc(feat_clip, 1)
                for hh in range(2):
                    rows = slice(64 * hh, 64 * hh + 64)
                    V.tensor_scalar(a_kz[rows, p % 2, hh], a_exp[rows, p % 2, 1], feat_ends[rows, 0:1],
                                    feat_ends[rows, 1:2], ALU.max, ALU.min).then_inc(feat_clip, 1)

            def a_pair_diag(g, p):
                dve.wait_ge(aS_ps, g * PAIRS + p + 1)
                mult(a_S[:, :, 0:SEQ].rearrange("p h (a t) -> p h a t", t=P),
                     wide[1][:, 0:512].rearrange("p (h a t) -> p h a t", h=2, t=P),
                     causal[:].unsqueeze(1).unsqueeze(1).broadcast_to([P, 2, 2, P])).then_inc(aS_diag, 1)

            def a_step(g, more):
                for k in range(PAIRS + 1):
                    if k < PAIRS:
                        a_pair_clip(g, k)
                    if k == 0 and more:
                        a_front1(g + 1)
                    if k == 1 and more:
                        a_front1b(g + 1)
                    if k >= 1:
                        a_pair_diag(g, k - 1)
                    if k == 3 and more:
                        a_front2(g + 1)
                    if k == 4 and more:
                        a_front3(g + 1)
                if more:
                    a_front3b(g + 1)
                dve.wait_ge(av_done, g + 1)
                if more:
                    a_front4(g + 1)
                dve.wait_ge(ao_ps, g + 1)
                o_v = bank[1][:, 0:UPS * GROUPS * GROWS].rearrange("p (a c) -> p a c", c=GROWS)
                V.tensor_scalar(a_den[:, 0].rearrange("p (a h) -> p a h", h=GH), o_v[:, :, GH * A_DIM:GROWS],
                                1e-6, None, ALU.max).then_inc(den_ready, 1)
                dve.wait_ge(den_ready, g * 2 + 1)
                V.reciprocal(a_den[:, 1], a_den[:, 0]).then_inc(den_ready, 1)
                dve.wait_ge(den_ready, g * 2 + 2)
                mult(a_o[:].rearrange("p u (g h d) -> p (u g) h d", g=GROUPS, d=A_DIM),
                     o_v[:, :, 0:GH * A_DIM].rearrange("p a (h d) -> p a h d", d=A_DIM),
                     a_den[:, 1].rearrange("p (a h) -> p a h", h=GH).unsqueeze(3)
                     .broadcast_to([P, UPS * GROUPS, GH, A_DIM])).then_inc(ao_ready, 1)
                dve.wait_ge(ay_ps, g + 1)
                V.tensor_tensor(a_y[:], bank[1][:, 0:SEQ].rearrange("p (u c) -> p u c", u=UPS),
                                a_bout[:].unsqueeze(1).broadcast_to([P, UPS, CH]), ALU.add)
                stats([a_y[:, u] for u in range(UPS)], st6[:, 1], st2[:, 1]).then_inc(a_var[1], 1)
                dve.wait_ge(a_rstd[1], g + 1)
                for u in range(UPS):
                    normalised(a_y[:, u], a_y[:, u], u, st2[:, 1], rstd[:, 1])
                dve.drain()
                V.tensor_tensor(xt(x1, g, 0, UPS), xt(x1, g, 0, UPS), a_y[:], ALU.add)
                stats([one(x1, g, u) for u in range(UPS)], st6[:, 2], st2[:, 2]).then_inc(a_var[2], 1)
                dve.wait_ge(a_rstd[2], g + 1)
                for u in range(UPS):
                    ins = normalised(one(xc, g, u), one(x1, g, u), u, st2[:, 2], rstd[:, 2])
                ins.then_inc(xc_ready, 1)

            dve.wait_ge(x_loaded, 4 * 16)
            for front in (a_front1, a_front1b, a_front2, a_front3, a_front3b):
                front(0)
            dve.wait_ge(zeroed, ZEROED + SET)
            a_front4(0)
            with dve.Fori(0, BATCH - 1) as g:
                a_step(g, True)
            a_step(BATCH - 1, False)

            with dve.Fori(0, DEPTH) as l:
                each = "p (a h d) -> p a h d"
                halves = "p (a h b d) -> p a h b d"

                def b_cosine(m, u):
                    for a in range(2):
                        dve.wait_ge(sq_sb, m * 2 + 1 + a)
                        here = slice(a * INNER, (a + 1) * INNER)
                        mult(b_ra[:, here].rearrange("p (h d) -> p h d", d=DIM),
                             wide[1][:, here].rearrange("p (h d) -> p h d", d=DIM),
                             t_cos[:, u, a].unsqueeze(1).broadcast_to([P, HEADS, DIM])).then_inc(rot_a, 1)

                def b_sine(m, u):
                    src = wide[1][:].rearrange(halves, a=2, h=HEADS, b=2)
                    dst = b_rb[:].rearrange(halves, a=2, h=HEADS, b=2)
                    for half in range(2):
                        sin = t_sin[:, u, :, half * DIM // 2:(half + 1) * DIM // 2]
                        mult(dst[:, :, :, half, :], src[:, :, :, 1 - half, :],
                             sin.unsqueeze(2).broadcast_to([P, 2, HEADS, DIM // 2])).then_inc(rot_a, 1)

                def b_squared_norms(m):
                    V.tensor_reduce(out=b_ss[:], in_=b_sq[:].rearrange("p (h d) -> p h d", d=DIM),
                                    axis=AXX, op=ALU.add).then_inc(b_ss_ready, 1)

                def b_rotated(m):
                    dve.wait_ge(rot_a, m * 4 + 4)
                    V.tensor_tensor(b_ra[:], b_ra[:], b_rb[:], ALU.add).then_inc(rot_sum, 1)

                def b_normalised(m):
                    dve.wait_ge(rot_sum, m + 1)
                    dve.wait_ge(b_rn_ready, m + 1)
                    mult(b_qk_rot[:].rearrange("p (h d) -> p h d", d=DIM), b_ra[:].rearrange("p (h d) -> p h d", d=DIM),
                         b_rn[:].unsqueeze(2).broadcast_to([P, 2 * HEADS, DIM])).then_inc(rot_ready, 1)

                def b_maximum(m):
                    dve.wait_ge(s_ps, m + 1)
                    V.tensor_reduce(out=b_mx[:], in_=wide[0][:].rearrange("p (h j) -> p h j", j=KEYS),
                                    axis=AXX, op=ALU.min).then_inc(mx_ready, 1)

                def b_weighted(m):
                    dve.wait_ge(o_ps, m + 1)
                    o_v = wide[2][:].rearrange("p (g c) -> p g c", c=512)[:, :, 0:4 * VCOL]
                    o_v = o_v.rearrange("p g (h d) -> p g h d", d=VCOL)
                    rs = b_rs[:].rearrange("p (g h) -> p g h", g=2).unsqueeze(3)
                    V.reciprocal(rs, o_v[:, :, :, DIM:VCOL]).then_inc(rs_ready, 1)
                    dve.wait_ge(rs_ready, m + 1)
                    mult(b_o[:].rearrange("p (g h) d -> p g h d", g=2), o_v[:, :, :, 0:DIM],
                         rs.broadcast_to([P, 2, HEADS // 2, DIM])).then_inc(o_ready, 1)

                def b_step(m, b, u, ahead1, ahead2):
                    dve.wait_ge(pT_ps, m + 1)
                    V.tensor_copy(b_pT[:, HEADS // 2:HEADS],
                                  wide[0][:, 512:1024].rearrange("p (h t) -> p h t", t=P)).then_inc(pT_sb, 1)
                    if ahead2:
                        b_cosine(m + 2, u)
                    b_weighted(m)
                    if ahead2:
                        b_squared_norms(m + 2)
                        b_sine(m + 2, u)
                    if ahead1:
                        b_maximum(m + 1)
                    if ahead2:
                        b_rotated(m + 2)
                    dve.wait_ge(wo_ps, m + 1)
                    V.tensor_tensor(one(xc, b, u), one(xc, b, u), bank[1][:, 0:CH],
                                    ALU.add).then_inc(attn_added, 1)
                    if ahead2:
                        dve.wait_ge(qkT_ps, m + 2)
                        b_normalised(m + 2)

                m0 = l * STEPS_B
                dve.wait_ge(tables_ready, (l + 1) * TABLE_OPS)
                for n in range(2):
                    b_cosine(m0 + n, n)
                    b_squared_norms(m0 + n)
                    b_sine(m0 + n, n)
                    b_rotated(m0 + n)
                    if n:
                        b_maximum(m0)
                        dve.wait_ge(qkT_ps, m0 + 1)
                    b_normalised(m0 + n)
                with dve.Fori(0, BATCH - 1) as b:
                    for u in range(UPS):
                        b_step(m0 + b * UPS + u, b, u, True, True)
                b_step(m0 + TILES - 2, BATCH - 1, 0, True, False)
                b_step(m0 + TILES - 1, BATCH - 1, 1, False, False)

                def c_front1(m):
                    dve.wait_ge(fh_ps, m + 1)
                    tiles = [bank[1][:, u * CH:(u + 1) * CH] for u in range(UPS)]
                    stats(tiles, c_st6, c_st2, own=False).then_inc(c_var, 1)
                    dve.wait_ge(c_rstd_ready, m + 1)
                    for u in range(UPS):
                        normalised(c_hn[:, u], tiles[u], u, c_st2, c_rstd).then_inc(fhn_ready, 1)

                def c_step(m, b, more):
                    dve.wait_ge(gelu_sb, m + 1)
                    for c in range(HCH):
                        V.scalar_tensor_tensor(out=c_act[:, c], in0=wide[0][:, c * SEQ:(c + 1) * SEQ],
                                               scalar=c_b1[:, 0, c:c + 1], in1=c_gelu[:, c],
                                               op0=ALU.add, op1=ALU.mult).then_inc(act_ready, 1)
                    if more:
                        c_front1(m + 1)
                    dve.wait_ge(w2_ps, m + 1)
                    dve.wait_ge(xb_ready, m + 1)
                    V.tensor_tensor(xt(xc, b, 0, UPS), c_xb[:],
                                    wide[2][:, 0:SEQ].rearrange("p (u c) -> p u c", u=UPS),
                                    ALU.add).then_inc(xc_ready, 1)

                m1 = l * STEPS_C
                dve.wait_ge(ffn_w_loaded, (l + 1) * (FFN_LOADS * 16))
                c_front1(m1)
                with dve.Fori(0, BATCH - 1) as b:
                    c_step(m1 + b, b, True)
                c_step(m1 + BATCH - 1, BATCH - 1, False)

            part = TILES // 4
            dve.wait_ge(xc_ready, (DEPTH + 1) * STEPS_C)
            with dve.Fori(0, 4) as f:
                def tile(buf, i):
                    return flat(buf[:, bass.ds(f * part + i, 1), :])

                stats([tile(xc, i) for i in range(part)], f_st6, f_st2).then_inc(f_var, 1)
                dve.wait_ge(f_rstd_ready, f + 1)
                for i in range(part):
                    normalised(tile(f_y, i), tile(xc, i), i, f_st2, f_rstd)
                dve.drain()
                here = bass.ds(f * part, part)
                V.tensor_tensor(f_y[:, here, :], f_y[:, here, :], x1[:, here, :], ALU.add).then_inc(f_ready, 1)

        @block.tensor
        def _(pe):
            T = nc.tensor

            def a_front1(g):
                pe.wait_ge(xn_ready, (g + 1) * UPS)
                for u in range(UPS):
                    last = T.transpose(bank[0][:, u * P:(u + 1) * P], xn[:, u], ident[:])
                last.then_inc(xnT_ps, 1)

            def a_front2(g):
                pe.wait_ge(xnT_sb, g + 1)
                for u in range(UPS):
                    last = T.matmul(bank[u][:, 0:3 * CH], xnT[:, u * P:(u + 1) * P], a_wqkv[:], start=True, stop=True)
                last.then_inc(aqkv_ps, 1)

            def a_front3(g):
                pe.wait_ge(aqkn_ready, (g + 1) * UPS)
                for a in range(2):
                    for u in range(UPS):
                        last = T.transpose(bank[0][:, a * SEQ + u * P:a * SEQ + (u + 1) * P],
                                           a_qkn[:, u, a * CH:(a + 1) * CH], ident[:])
                last.then_inc(aqkT_ps, 1)

            def a_pair_feat(g, p):
                half = p % 2 * 512
                T.matmul(wide[0][:, half:half + 512], omega_pad[:, 2 * p:2 * p + 2, :].rearrange("p a f -> p (a f)"),
                         a_qkT[:].rearrange("p a t -> p (a t)"), start=True, stop=True).then_inc(feat_ps, 1)

            def a_pair_scores(g, p):
                pe.wait_ge(feat_clip, g * (3 * PAIRS) + 3 * p + 3)
                for hh in range(2):
                    for keys, queries, at in ((1, 1, hh * SEQ), (0, 0, hh * SEQ + P), (0, 1, 512 + hh * P)):
                        last = T.matmul(wide[1][:, at:at + P], a_kz[:, p % 2, hh, keys * P:(keys + 1) * P],
                                        a_qf[:, p % 2, queries * P:(queries + 1) * P], start=True, stop=True)
                last.then_inc(aS_ps, 1)

            def a_pair_values(g, p):
                pe.wait_ge(aS_diag, g * PAIRS + p + 1)
                pe.wait_ge(aS_off, g * PAIRS + p + 1)
                for hh in range(2):
                    grp, h = divmod(2 * p + hh, GH)
                    cols = slice(h * GROWS, (h + 1) * GROWS)
                    at = grp * 512
                    T.matmul(wide[2][0:GROWS, at:at + SEQ], a_vz[:, 0, grp, cols], a_S[:, hh, P:P + SEQ],
                             start=h == 0, stop=False)
                    last = T.matmul(wide[2][0:GROWS, at + P:at + SEQ], a_vz[:, 1, grp, cols], a_S[:, hh, 0:P],
                                    start=False, stop=h == GH - 1)
                if p == PAIRS - 1:
                    last.then_inc(av_done, 1)

            def a_step(g, more):
                pe.wait_ge(aqkT_sb, g + 1)
                for k in range(PAIRS + 2):
                    if k < PAIRS:
                        a_pair_feat(g, k)
                    if k == 2 and more:
                        a_front1(g + 1)
                    if k == 4 and more:
                        a_front2(g + 1)
                    if k == 2:
                        pe.wait_ge(vz_ready, (g + 1) * UPS)
                    if k >= 2:
                        a_pair_values(g, k - 2)
                    if 1 <= k <= PAIRS:
                        a_pair_scores(g, k - 1)
                if more:
                    a_front3(g + 1)
                pe.wait_ge(aoT_sb, g + 1)
                for u in range(UPS):
                    for grp in range(GROUPS):
                        at = (u * GROUPS + grp) * GROWS
                        last = T.transpose(bank[1][:, at:at + GROWS], a_oT[:, grp, u * P:(u + 1) * P],
                                           ident[0:GROWS, 0:GROWS])
                last.then_inc(ao_ps, 1)
                pe.wait_ge(ao_ready, g + 1)
                for u in range(UPS):
                    last = T.transpose(bank[1][:, u * P:(u + 1) * P], a_o[:, u], ident[:])
                last.then_inc(ao2_ps, 1)
                pe.wait_ge(ao2_sb, g + 1)
                for u in range(UPS):
                    last = T.matmul(bank[1][:, u * CH:(u + 1) * CH], a_oT2[:, u * P:(u + 1) * P], a_wout[:],
                                    start=True, stop=True)
                last.then_inc(ay_ps, 1)

            pe.wait_ge(const_loaded, CONST_LOADS * 16)
            a_front1(0)
            a_front2(0)
            a_front3(0)
            pe.wait_ge(prep_done, 1)
            with pe.Fori(0, BATCH - 1) as g:
                a_step(g, True)
            a_step(BATCH - 1, False)

            pe.wait_ge(masks_ready, 2)
            with pe.Fori(0, DEPTH) as l:
                def b_stream(m):
                    pe.wait_ge(bx_ready, m + 1)
                    T.transpose(bank[0][:, 0:P], b_x[:], ident[:]).then_inc(hT_ps, 1)

                def b_qk(m, u):
                    pe.wait_ge(hT_sb, m * 2 + 2)
                    at = WIN + u * P
                    for a in range(2):
                        T.matmul(wide[1][:, a * INNER:(a + 1) * INNER], hT[:, at:at + P],
                                 b_wqkv[:, a * INNER:(a + 1) * INNER], start=True, stop=True).then_inc(qk_ps, 1)

                def b_values(u):
                    for w in range(2):
                        at = u * P + w * WIN
                        last = T.matmul(wide[2][:, w * INNER:(w + 1) * INNER], hT[:, at:at + KEYS],
                                        b_wqkv[:, 2 * INNER:3 * INNER], start=True, stop=True)
                    last.then_inc(v_ps, 1)

                def b_turn(m):
                    pe.wait_ge(v_sb, m + 1)
                    pe.wait_ge(rot_ready, m + 1)
                    for c in range(2 * HP):
                        last = T.transpose(wide[2][:, c * P:(c + 1) * P], b_qk_rot[:, c * P:(c + 1) * P], ident[:])
                    last.then_inc(qkT_ps, 1)

                def b_scores(u):
                    kind = 0 if u == 0 else 1
                    for half in range(2):
                        T.matmul(wide[0][:, half * 512:half * 512 + 512], ident_bf[:],
                                 masks[:, kind].rearrange("p h j -> p (h j)"), start=True, stop=False)
                        for k in range(half * HP // 2, (half + 1) * HP // 2):
                            for w in range(2):
                                at = u * P + w * WIN
                                last = T.matmul(wide[0][w * WIN:(w + 1) * WIN, k * 2 * KEYS:(k + 1) * 2 * KEYS],
                                                b_qT[:, k, w * WIN:(w + 1) * WIN], b_kz[:, k, :, at:at + KEYS],
                                                start=False, stop=k % 2 == 1)
                    last.then_inc(s_ps, 1)

                def b_queries_keys_out(m):
                    pe.wait_ge(qT_sb, m + 1)
                    pe.wait_ge(kz_sb, m * 2 + 2)

                def b_step(m, u, ahead1, ahead2):
                    if ahead2:
                        b_stream(m + 2)
                    for half in range(2):
                        pe.wait_ge(p_exp, m * 2 + 1 + half)
                        for h in range(half * HEADS // 2, (half + 1) * HEADS // 2):
                            last = T.transpose(wide[0][:, h * P:(h + 1) * P], b_p[:, h], ident[:])
                    last.then_inc(pT_ps, 1)
                    if ahead1:
                        b_turn(m + 1)
                    if ahead2:
                        b_qk(m + 2, u)
                    pe.wait_ge(pT_sb, m * 2 + 2)
                    if ahead1:
                        b_queries_keys_out(m + 1)
                    else:
                        pe.wait_ge(v_sb, m + 1)
                    for h in range(HEADS):
                        for w in range(2):
                            at = h // 4 * 512 + h % 4 * VCOL
                            last = T.matmul(wide[2][w * WIN:(w + 1) * WIN, at:at + VCOL],
                                            b_pT[:, h, w * WIN:(w + 1) * WIN], b_v[:, u, w, h, :],
                                            start=True, stop=True)
                    last.then_inc(o_ps, 1)
                    if ahead1:
                        b_scores(1 - u)
                    pe.wait_ge(o_ready, m + 1)
                    for k in range(HP):
                        last = T.transpose(bank[0][:, k * P:(k + 1) * P],
                                           b_o[:, 2 * k:2 * k + 2].rearrange("p h d -> p (h d)"), ident[:])
                    last.then_inc(oT_ps, 1)
                    if ahead2:
                        b_values(u)
                    pe.wait_ge(oT_sb, m + 1)
                    for k in range(HP):
                        last = T.matmul(bank[1][:, 0:CH], b_oT[:, k], b_wo[:, k], start=k == 0, stop=k == HP - 1)
                    last.then_inc(wo_ps, 1)

                m0 = l * STEPS_B
                pe.wait_ge(attn_w_loaded, (l + 1) * (ATTN_LOADS * 16))
                pe.wait_ge(xc_ready, (l + 1) * STEPS_C)
                b_stream(m0)
                b_qk(m0, 0)
                b_values(0)
                b_stream(m0 + 1)
                b_turn(m0)
                b_qk(m0 + 1, 1)
                b_queries_keys_out(m0)
                b_scores(0)
                b_values(1)
                with pe.Fori(0, BATCH - 1) as b:
                    for u in range(UPS):
                        b_step(m0 + b * UPS + u, u, True, True)
                b_step(m0 + TILES - 2, 0, True, False)
                b_step(m0 + TILES - 1, 1, False, False)

                def c_front1(m):
                    pe.wait_ge(cx_ready, m + 1)
                    for u in range(UPS):
                        last = T.transpose(bank[0][:, u * P:(u + 1) * P], c_x[:, u], ident[:])
                    last.then_inc(fT_ps, 1)

                def c_front2(m):
                    pe.wait_ge(fT_sb, m * 2 + 2)
                    for u in range(UPS):
                        at = WIN + u * P
                        last = T.transpose(bank[1][:, u * P:(u + 1) * P], hT[:, at:at + P], ident[:])
                    last.then_inc(fh_ps, 1)

                def c_front3(m):
                    pe.wait_ge(fhn_ready, (m + 1) * UPS)
                    for u in range(UPS):
                        last = T.transpose(bank[0][:, u * P:(u + 1) * P], c_hn[:, u], ident[:])
                    last.then_inc(fhnT_ps, 1)

                def c_step(m, more):
                    pe.wait_ge(fhnT_sb, m + 1)
                    if more:
                        c_front1(m + 1)
                    for g in (1, 0):
                        for c in range(HCH):
                            last = T.matmul(wide[g][:, c * SEQ:(c + 1) * SEQ], c_w1[:, g, c * P:(c + 1) * P],
                                            c_hT[:], start=True, stop=True)
                    last.then_inc(w1_ps, 1)
                    if more:
                        c_front2(m + 1)
                    pe.wait_ge(act_ready, (m + 1) * HCH)
                    for u in range(UPS):
                        for c in range(HCH):
                            last = T.matmul(wide[2][:, u * CH:(u + 1) * CH], c_act[:, c, u * P:(u + 1) * P],
                                            c_w2[:, c], start=c == 0, stop=c == HCH - 1)
                    last.then_inc(w2_ps, 1)
                    if more:
                        c_front3(m + 1)

                m1 = l * STEPS_C
                pe.wait_ge(ffn_w_loaded, (l + 1) * (FFN_LOADS * 16))
                c_front1(m1)
                pe.wait_ge(attn_added, (l + 1) * STEPS_B)
                c_front2(m1)
                c_front3(m1)
                with pe.Fori(0, BATCH - 1) as b:
                    c_step(m1 + b, True)
                c_step(m1 + BATCH - 1, False)


_INS = ['L0_attn_x', 'L0_attn_Wqkv', 'L0_attn_bqkv', 'L0_attn_Wout', 'L0_attn_bout', 'L0_attn_omega',
        'L0_attn_quad_nodes', 'L0_attn_quad_weights', 'L0_ffn_wqkv', 'L0_ffn_q_scale', 'L0_ffn_k_scale',
        'L0_ffn_wo', 'L0_ffn_ln_g', 'L0_ffn_ln_b', 'L0_ffn_w1', 'L0_ffn_b1', 'L0_ffn_w2', 'L0_ffn_b2']


def kernel(**inputs):
    import concourse.bacc as bacc
    from concourse.bass_utils import run_bass_kernel_spmd

    nc = bacc.Bacc("TRN2", target_bir_lowering=False, num_devices=1)
    arrays, args = {}, []
    constants = shape_constants()
    for name, a in [(n, inputs[n]) for n in _INS] + list(constants.items()):
        a = np.ascontiguousarray(a)
        arrays[name] = a
        args.append(nc.dram_tensor(name, a.shape, mybir.dt.from_np(a.dtype), kind="ExternalInput").ap())
    result = nc.dram_tensor("result", (BATCH, SEQ, CH), F32, kind="ExternalOutput").ap()
    build(nc, *args, result)
    r = run_bass_kernel_spmd(nc, [arrays], core_ids=[0])
    return r.results[0]["result"]
```

```python
from contextlib import ExitStack

import concourse.bass as bass
import numpy as np
from concourse import mybir

P = 128
F32 = mybir.dt.float32
BF16 = mybir.dt.bfloat16
ALU = mybir.AluOpType
ACT = mybir.ActivationFunctionType
AXX = mybir.AxisListType.X

BATCH, SEQ, CH = 8, 256, 128
TILES = BATCH * SEQ // P
UPS = SEQ // P
DEPTH = 2
A_HEADS, A_DIM, A_M, A_R = 16, 8, 32, 2
A_FEAT = A_R * A_M
PAIRS = A_HEADS // 2
QUAD = 32
GH = P // QUAD
GROUPS = A_HEADS // GH
CLIP = 20.0
HEADS, DIM, WIN = 8, 64, 64
INNER = HEADS * DIM
HP = HEADS // 2
QK_SCALE = -8.0
KEYS = 2 * WIN
VCOL = DIM + 1
MASKED = 1e30
HID = CH * 4 * 2 // 3
HCH = -(-HID // P)
HLAST = HID - (HCH - 1) * P
EPS = 1e-5


def shape_constants():
    half = np.arange(0, DIM, 2, dtype=np.float32)
    inv_freq = (np.float32(1.0) / np.float32(10000.0) ** (half / np.float32(DIM))).astype(np.float32)
    t = np.arange(SEQ, dtype=np.float32)
    freqs = t[:, None] * inv_freq[None, :]
    base = ((half + np.float32(0.4 * DIM)) / np.float32(1.4 * DIM)).astype(np.float32)
    power = (t - SEQ // 2) / np.float32(WIN // 2)
    scale = base[None, :] ** power[:, None]
    cos, sin = np.cos(freqs), np.sin(freqs)
    cos, sin = np.concatenate([cos, cos], 1), np.concatenate([-sin, sin], 1)
    scale = np.concatenate([scale, scale], 1)
    rot = np.stack([np.stack([cos * scale * QK_SCALE, cos / scale], 1),
                    np.stack([sin * scale * QK_SCALE, sin / scale], 1)], 0)
    rot = rot.reshape(2, UPS, P, 2, DIM).transpose(0, 2, 1, 3, 4).astype(np.float32)
    q = np.arange(WIN)[:, None] + WIN
    k = np.arange(KEYS)[None, :]
    seen = (k <= q) & (q <= k + WIN)
    mask = np.where(seen, 0.0, MASKED)
    first = np.where(seen & (k >= WIN), 0.0, MASKED)
    swap = np.roll(np.arange(KEYS), WIN)
    masks = np.stack([np.concatenate([first[:, swap], mask]), np.concatenate([mask[:, swap], mask])], 1)
    s = np.arange(P)
    causal = (s[:, None] <= s[None, :]).astype(np.float32)
    owner = (s[:, None] // A_DIM == np.arange(A_HEADS)[None, :]).astype(np.float32)
    node = ((s[:, None] // A_M) % A_R == np.arange(A_R)[None, :]).astype(np.float32)
    return {
        "c_rot_cos": np.ascontiguousarray(rot[0]), "c_rot_sin": np.ascontiguousarray(rot[1]),
        "c_masks": masks.astype(np.float32), "c_ident": np.eye(P, dtype=np.float32),
        "c_causal": causal, "c_owner": owner, "c_node": node,
    }


def build(nc, x, Wqkv, bqkv, Wout, bout, omega, nodes, weights, wqkv, q_scale, k_scale, wo, ln_g, ln_b,
          w1, b1, w2, b2, c_rot_cos, c_rot_sin, c_masks, c_ident, c_causal, c_owner, c_node, out):
    with ExitStack() as ctx:
        def sb(name, shape, dt=F32):
            return ctx.enter_context(nc.sbuf_tensor(name, shape, dt))

        def sem(name):
            return ctx.enter_context(nc.semaphore(name))

        x1 = sb("x1", [P, TILES, CH])
        xc = sb("xc", [P, TILES, CH])
        ident = sb("ident", [P, P])
        ident_bf = sb("ident_bf", [P, P], BF16)
        causal = sb("causal", [P, P])
        owner = sb("owner", [P, A_HEADS])
        node_sel = sb("node_sel", [P, A_R])
        rot_cos = sb("rot_cos", [P, UPS, 2, DIM])
        rot_sin = sb("rot_sin", [P, UPS, 2, DIM])
        masks_f = sb("masks_f", [P, 2, KEYS])
        masks = sb("masks", [P, 2, 4, KEYS], BF16)
        a_wqkv = sb("a_wqkv", [P, 3 * CH])
        a_bqkv = sb("a_bqkv", [P, 3 * CH])
        a_wout = sb("a_wout", [P, CH])
        a_bout = sb("a_bout", [P, CH])
        omega_rows = sb("omega_rows", [P, A_R, A_M])
        omega_pad = sb("omega_pad", [P, A_HEADS, A_FEAT])
        quad = sb("quad", [P, 2, A_R])
        quad_t = sb("quad_t", [P, 8, A_R])
        feat_sel = sb("feat_sel", [P, 2, A_R])
        feat_bias = sb("feat_bias", [P, 2])
        feat_ends = sb("feat_ends", [P, 2])
        power = sb("power", [P, 4])
        x_st6 = sb("x_st6", [P, TILES, 6])
        x_st2 = sb("x_st2", [P, TILES, 2])
        x_rstd = sb("x_rstd", [P, TILES])
        st6 = sb("st6", [P, 2, UPS, 6])
        st2 = sb("st2", [P, 2, UPS, 2])
        rstd = sb("rstd", [P, 2, UPS])
        a_ss = sb("a_ss", [P, UPS * 2 * A_HEADS])
        a_rn = sb("a_rn", [P, UPS * 2 * A_HEADS])
        xn = sb("xn", [P, TILES, CH])
        xnT_all = sb("xnT_all", [P, TILES, P])
        xnT = sb("xnT", [P, UPS, P])
        a_qk = sb("a_qk", [P, UPS, 2 * CH])
        a_v = sb("a_v", [P, UPS, CH])
        a_sq = sb("a_sq", [P, UPS, 2 * CH])
        a_qkn = sb("a_qkn", [P, UPS, 2 * CH])
        a_qkT = sb("a_qkT", [P, 2, SEQ])
        a_exp = sb("a_exp", [P, 2, 2, SEQ])
        a_qf = sb("a_qf", [P, 2, SEQ])
        a_kz = sb("a_kz", [P, 2, 2, SEQ])
        a_S = sb("a_S", [P, 4, 2, SEQ + P])
        a_vz = sb("a_vz", [P, UPS, A_HEADS, QUAD])
        a_oT = sb("a_oT", [P, GROUPS, SEQ])
        a_den = sb("a_den", [P, 2, UPS, A_HEADS])
        a_o = sb("a_o", [P, UPS, CH])
        a_oT2 = sb("a_oT2", [P, SEQ])
        a_y = sb("a_y", [P, UPS, CH])
        b_wqkv = sb("b_wqkv", [P, 3 * INNER])
        b_wo = sb("b_wo", [P, HP, CH])
        qk_scale = sb("qk_scale", [P, DEPTH, 2, DIM])
        t_cos = sb("t_cos", [P, DEPTH * UPS, 2, DIM])
        t_sin = sb("t_sin", [P, DEPTH * UPS, 2, DIM])
        hT = sb("hT", [P, WIN + SEQ + 1])
        b_x = sb("b_x", [P, CH])
        b_sq = sb("b_sq", [P, 2 * INNER])
        b_ss = sb("b_ss", [P, 2 * HEADS])
        b_rn = sb("b_rn", [P, 2 * HEADS])
        b_qk_rot = sb("b_qk_rot", [P, 2 * INNER])
        b_ra = sb("b_ra", [P, 2 * INNER])
        b_rb = sb("b_rb", [P, 2 * INNER])
        b_qT = sb("b_qT", [P, HP, P])
        b_kz = sb("b_kz", [P, HP, 2, 2, UPS, WIN])
        b_v = sb("b_v", [P, UPS, HEADS, VCOL])
        b_vb = sb("b_vb", [P, UPS, HEADS, VCOL])
        b_mx = sb("b_mx", [P, HEADS])
        b_p = sb("b_p", [P, HEADS, KEYS])
        b_pT = sb("b_pT", [P, HEADS, P])
        b_rs = sb("b_rs", [P, HEADS])
        b_o = sb("b_o", [P, HEADS, DIM])
        b_oT = sb("b_oT", [P, HP, P])
        c_w1 = sb("c_w1", [P, 2, HCH * P])
        c_w2 = sb("c_w2", [P, HCH, CH])
        c_b1 = sb("c_b1", [P, 2, HCH])
        c_b2 = sb("c_b2", [P, CH])
        c_lg = sb("c_lg", [P, 1])
        c_lb = sb("c_lb", [P, 1])
        c_x = sb("c_x", [P, UPS, CH])
        c_hn = sb("c_hn", [P, UPS, CH])
        c_hT = sb("c_hT", [P, SEQ])
        c_st6 = sb("c_st6", [P, UPS, 6])
        c_st2 = sb("c_st2", [P, UPS, 2])
        c_rstd = sb("c_rstd", [P, UPS])
        c_gelu = sb("c_gelu", [P, HCH, SEQ])
        c_act = sb("c_act", [P, HCH, SEQ])
        f_y = sb("f_y", [P, TILES, CH])
        f_st6 = sb("f_st6", [P, TILES, 6])
        f_st2 = sb("f_st2", [P, TILES, 2])
        f_rstd = sb("f_rstd", [P, TILES])

        wide = [ctx.enter_context(nc.psum_tensor(f"wide{i}", [P, 1024], F32)) for i in range(3)]
        bank = [ctx.enter_context(nc.psum_tensor(f"bank{i}", [P, 512], F32)) for i in range(2)]

        first_loaded = sem("first_loaded")
        x_loaded = sem("x_loaded")
        const_loaded = sem("const_loaded")
        attn_w_loaded = sem("attn_w_loaded")
        ffn_w_loaded = sem("ffn_w_loaded")
        out_stored = sem("out_stored")
        a_zeroed = sem("a_zeroed")
        zeroed = sem("zeroed")
        prep_dve = sem("prep_dve")
        root_in = sem("root_in")
        root_ready = sem("root_ready")
        quad_logs_in = sem("quad_logs_in")
        quad_logs = sem("quad_logs")
        feat_bias_ready = sem("feat_bias_ready")
        feat_ends_exp = sem("feat_ends_exp")
        prep_done = sem("prep_done")
        masks_ready = sem("masks_ready")
        x_var = sem("x_var")
        x_rstd_ready = sem("x_rstd_ready")
        a_var = [sem("a_var_out"), sem("a_var_in2")]
        a_rstd = [sem("a_rstd_out"), sem("a_rstd_in2")]
        a_ss_ready = sem("a_ss_ready")
        a_rn_ready = sem("a_rn_ready")
        den_ready = sem("den_ready")
        xn_ready = sem("xn_ready")
        xnT_ps = sem("xnT_ps")
        xnT_sb = sem("xnT_sb")
        aqkv_ps = sem("aqkv_ps")
        aqk_sb = sem("aqk_sb")
        av_sb = sem("av_sb")
        xnT_all_ps = sem("xnT_all_ps")
        xnT_all_sb = sem("xnT_all_sb")
        asq_sb = sem("asq_sb")
        vz_ready = sem("vz_ready")
        aqkn_ready = sem("aqkn_ready")
        aqkT_ps = sem("aqkT_ps")
        aqkT_sb = sem("aqkT_sb")
        feat_ps = sem("feat_ps")
        feat_exp = sem("feat_exp")
        feat_clip = sem("feat_clip")
        aS_ps = sem("aS_ps")
        aS_diag = sem("aS_diag")
        aS_off = sem("aS_off")
        av_done = sem("av_done")
        aoT_sb = sem("aoT_sb")
        ao_ps = sem("ao_ps")
        ao_ready = sem("ao_ready")
        ao2_ps = sem("ao2_ps")
        ao2_sb = sem("ao2_sb")
        ay_ps = sem("ay_ps")
        xc_ready = sem("xc_ready")
        tables_ready = sem("tables_ready")
        b_ss_ready = sem("b_ss_ready")
        b_rn_ready = sem("b_rn_ready")
        rot_a = sem("rot_a")
        rot_sum = sem("rot_sum")
        mx_ready = sem("mx_ready")
        rs_ready = sem("rs_ready")
        bx_ready = sem("bx_ready")
        hT_ps = sem("hT_ps")
        hT_sb = sem("hT_sb")
        qk_ps = sem("qk_ps")
        sq_sb = sem("sq_sb")
        v_ps = sem("v_ps")
        v_sb = sem("v_sb")
        vb_sb = sem("vb_sb")
        rot_ready = sem("rot_ready")
        qkT_ps = sem("qkT_ps")
        qT_sb = sem("qT_sb")
        kz_sb = sem("kz_sb")
        s_ps = sem("s_ps")
        p_exp = sem("p_exp")
        pT_ps = sem("pT_ps")
        pT_sb = sem("pT_sb")
        o_ps = sem("o_ps")
        o_ready = sem("o_ready")
        oT_ps = sem("oT_ps")
        oT_sb = sem("oT_sb")
        wo_ps = sem("wo_ps")
        attn_added = sem("attn_added")
        c_var = sem("c_var")
        c_rstd_ready = sem("c_rstd_ready")
        cx_ready = sem("cx_ready")
        fT_ps = sem("fT_ps")
        fT_sb = sem("fT_sb")
        fh_ps = sem("fh_ps")
        fhn_ready = sem("fhn_ready")
        fhnT_ps = sem("fhnT_ps")
        fhnT_sb = sem("fhnT_sb")
        w1_gate_ps = sem("w1_gate_ps")
        w1_ps = sem("w1_ps")
        gelu_sb = sem("gelu_sb")
        act_ready = sem("act_ready")
        xb_ready = sem("xb_ready")
        w2_ps = sem("w2_ps")
        f_var = sem("f_var")
        f_rstd_ready = sem("f_rstd_ready")
        f_normed = sem("f_normed")
        f_ready = sem("f_ready")

        FIRST_LOADS = 6
        X_LOADS = 2
        CONST_LOADS = 10 + 2 * DEPTH
        ATTN_LOADS = 2
        FFN_LOADS = 13
        TABLE_OPS = 3 * UPS * DEPTH
        ZEROED = 5
        B_SET = ZEROED + 2
        PARTS = 4
        STEPS_B = TILES
        STEPS_C = BATCH

        block = ctx.enter_context(nc.Block())

        def xt(buf, b, u=0, n=1):
            return buf[:, bass.ds(b * UPS + u, n), :]

        def flat(t):
            return t.rearrange("p a c -> p (a c)")

        def one(buf, b, u):
            return flat(xt(buf, b, u))

        @block.sync
        def _(sp):
            xv = x.rearrange("b (u p) c -> p (b u) c", p=P)
            for dst, src in ((x1[:, 0:UPS, :], xv[:, 0:UPS, :]), (quad[:, 0, :], nodes.partition_broadcast(P)),
                             (quad[:, 1, :], weights.partition_broadcast(P)), (ident[:], c_ident),
                             (a_wqkv[:], Wqkv), (a_bqkv[:], bqkv.partition_broadcast(P))):
                sp.dma_start(dst, src).then_inc(first_loaded, 16)
            for r in range(A_R):
                sp.dma_start(omega_rows[:, r, :], omega[r].rearrange("h d m -> (h d) m")).then_inc(const_loaded, 16)
            for dst, src in ((owner, c_owner), (node_sel, c_node), (causal, c_causal), (masks_f, c_masks)):
                sp.dma_start(dst[:], src).then_inc(const_loaded, 16)
            for lo, hi in ((UPS, TILES // 2), (TILES // 2, TILES)):
                sp.dma_start(x1[:, lo:hi, :], xv[:, lo:hi, :]).then_inc(x_loaded, 16)
            for dst, src in ((rot_cos, c_rot_cos), (rot_sin, c_rot_sin), (a_wout, Wout)):
                sp.dma_start(dst[:], src).then_inc(const_loaded, 16)
            sp.dma_start(a_bout[:], bout.partition_broadcast(P)).then_inc(const_loaded, 16)
            for l in range(DEPTH):
                sp.dma_start(qk_scale[:, l, 0, :], q_scale[l].partition_broadcast(P)).then_inc(const_loaded, 16)
                sp.dma_start(qk_scale[:, l, 1, :], k_scale[l].partition_broadcast(P)).then_inc(const_loaded, 16)
            for l in range(DEPTH):
                if l:
                    sp.wait_ge(wo_ps, l * STEPS_B)
                sp.dma_start(b_wqkv[:], wqkv[l]).then_inc(attn_w_loaded, 16)
                sp.dma_start(b_wo[:], wo[l].rearrange("(k p) n -> p k n", p=P)).then_inc(attn_w_loaded, 16)
                if l:
                    sp.wait_ge(xc_ready, (l + 1) * STEPS_C)
                    sp.wait_ge(fhnT_sb, l * STEPS_C)
                    sp.wait_ge(gelu_sb, l * STEPS_C)
                    sp.wait_ge(xb_ready, l * STEPS_C)
                else:
                    sp.wait_ge(zeroed, ZEROED)
                for g in range(2):
                    sp.dma_start(c_w1[:, g, 0:HID], w1[l][:, g * HID:(g + 1) * HID]).then_inc(ffn_w_loaded, 16)
                    for c in range(HCH):
                        n = P if c < HCH - 1 else HLAST
                        at = g * HID + c * P
                        sp.dma_start(c_b1[0:n, g, c:c + 1], b1[l][at:at + n].unsqueeze(1)).then_inc(ffn_w_loaded, 16)
                sp.dma_start(c_w2[:, 0:HCH - 1, :],
                             w2[l][0:(HCH - 1) * P].rearrange("(k p) n -> p k n", p=P)).then_inc(ffn_w_loaded, 16)
                sp.dma_start(c_w2[0:HLAST, HCH - 1, :], w2[l][(HCH - 1) * P:HID]).then_inc(ffn_w_loaded, 16)
                sp.dma_start(c_b2[:], b2[l].partition_broadcast(P)).then_inc(ffn_w_loaded, 16)
                sp.dma_start(c_lg[:], ln_g[l].unsqueeze(1)).then_inc(ffn_w_loaded, 16)
                sp.dma_start(c_lb[:], ln_b[l].unsqueeze(1)).then_inc(ffn_w_loaded, 16)
            ov = out.rearrange("b (u p) c -> p (b u) c", p=P)
            for f in range(PARTS):
                here = slice(f * TILES // PARTS, (f + 1) * TILES // PARTS)
                sp.wait_ge(f_ready, f + 1)
                sp.dma_start(ov[:, here, :], f_y[:, here, :]).then_inc(out_stored, 16)
            sp.wait_ge(out_stored, PARTS * 16)

        @block.gpsimd
        def _(pool):
            G = nc.gpsimd
            for i, value in enumerate((-0.5, 0.5, EPS, 0.0)):
                G.memset(power[:, i:i + 1], value)
            pool.drain()

            def inverse_root(out, x):
                shape = list(out.shape)
                G.tensor_tensor(x, x, power[:, 2:3].broadcast_to(shape), ALU.add)
                pool.drain()
                return G.tensor_tensor(out, x, power[:, 0:1].broadcast_to(shape), ALU.pow)

            def copied(out, x, b):
                if isinstance(b, int):
                    return G.tensor_tensor(out, x, power[:, 3:4].unsqueeze(2).broadcast_to(list(out.shape)), ALU.add)
                return G.tensor_copy(out, x)

            def inverse_norm(out, x):
                G.tensor_tensor(out, x, power[:, 0:1].broadcast_to(list(out.shape)), ALU.pow)
                pool.drain()
                return G.tensor_scalar(out, out, 1e12, None, ALU.min)

            def a_rstds(i, g):
                pool.wait_ge(a_var[i], g + 1)
                inverse_root(rstd[:, i], st2[:, i, :, 1]).then_inc(a_rstd[i], 1)

            def a_head_norms(g):
                pool.wait_ge(a_ss_ready, g + 1)
                inverse_norm(a_rn[:], a_ss[:]).then_inc(a_rn_ready, 1)

            def a_step(g, front, back, back2):
                if back2:
                    a_rstds(1, g - 2)
                if front:
                    a_head_norms(g + 1)
                if back:
                    a_rstds(0, g - 1)

            def x_rstds(i, tiles):
                pool.wait_ge(x_var, i + 1)
                inverse_root(x_rstd[:, tiles], x_st2[:, tiles, 1]).then_inc(x_rstd_ready, 1)

            pool.wait_ge(root_in, 1)
            G.tensor_tensor(quad_t[:, 4], quad_t[:, 3], power[:, 1:2].broadcast_to([P, A_R]),
                            ALU.pow).then_inc(root_ready, 1)
            x_rstds(0, slice(0, UPS))
            for buf in (a_kz, a_vz):
                G.memset(buf[:], 0.0).then_inc(a_zeroed, 1)
            pool.wait_ge(a_zeroed, 2)
            G.memset(a_vz[:, :, :, A_DIM:A_DIM + 1], 1.0).then_inc(a_zeroed, 1)
            x_rstds(1, slice(UPS, TILES))
            a_head_norms(0)
            for buf in (c_w1, c_w2, c_b1, hT, b_kz):
                G.memset(buf[:], 0.0).then_inc(zeroed, 1)
            for buf in (b_v, b_vb):
                G.memset(buf[:], 1.0).then_inc(zeroed, 1)
            pool.wait_ge(const_loaded, CONST_LOADS * 16)
            for l in range(DEPTH):
                for u in range(UPS):
                    at = l * UPS + u
                    G.tensor_tensor(t_cos[:, at], rot_cos[:, u], qk_scale[:, l], ALU.mult).then_inc(tables_ready, 1)
                    for half in range(2):
                        here = slice(half * DIM // 2, (half + 1) * DIM // 2)
                        there = slice((1 - half) * DIM // 2, (2 - half) * DIM // 2)
                        G.tensor_tensor(t_sin[:, at, :, here], rot_sin[:, u, :, here],
                                        qk_scale[:, l, :, there], ALU.mult).then_inc(tables_ready, 1)
            a_step(0, True, False, False)
            a_step(1, True, True, False)
            with pool.Fori(2, BATCH - 1) as g:
                a_step(g, True, True, True)
            a_step(BATCH - 1, False, True, True)
            a_step(BATCH, False, True, True)
            a_step(BATCH + 1, False, False, True)
            with pool.Fori(0, DEPTH) as l:
                pool.wait_ge(xc_ready, l * STEPS_C + 1)

                def taken(m, b, u):
                    pool.wait_ge(hT_ps, m)
                    copied(b_x[:].unsqueeze(1), xt(xc, b, u), b).then_inc(bx_ready, 1)

                def head_norms(m):
                    pool.wait_ge(b_ss_ready, m + 1)
                    inverse_norm(b_rn[:], b_ss[:]).then_inc(b_rn_ready, 1)

                def values_beside(m, u):
                    pool.drain()
                    pool.wait_ge(v_sb, m + 1)
                    for n, (here, at) in enumerate(((slice(0, WIN), u), (slice(WIN, P), 1 - u))):
                        if n:
                            pool.drain()
                        zero = power[here, 3:4].unsqueeze(2).broadcast_to([WIN, HEADS, DIM])
                        last = G.tensor_tensor(b_vb[here, u, :, 0:DIM], b_v[here, at, :, 0:DIM], zero, ALU.add)
                    last.then_inc(vb_sb, 1)
                    pool.drain()

                m0 = l * STEPS_B
                copied(b_x[:].unsqueeze(1), xt(xc, 0, 0), 0).then_inc(bx_ready, 1)
                taken(m0 + 1, 0, 1)
                head_norms(m0)
                values_beside(m0, 0)
                pool.wait_ge(xc_ready, l * STEPS_C + 2)
                taken(m0 + 2, 1, 0)
                head_norms(m0 + 1)
                with pool.Fori(0, BATCH - 2) as b:
                    for u in range(UPS):
                        m = m0 + b * UPS + u
                        values_beside(m + 1, 1 - u)
                        if u == 1:
                            pool.wait_ge(xc_ready, l * STEPS_C + b + 3)
                        taken(m + 3, b + 1 + u, 1 - u)
                        head_norms(m + 2)
                m2 = m0 + TILES - 4
                values_beside(m2 + 1, 1)
                taken(m2 + 3, BATCH - 1, 1)
                head_norms(m2 + 2)
                values_beside(m2 + 2, 0)
                head_norms(m2 + 3)
                values_beside(m2 + 3, 1)

                def stream_out(b):
                    copied(c_x[:], xt(xc, b, 0, UPS), b).then_inc(cx_ready, 1)
                    pool.drain()
                    G.tensor_tensor(xt(xc, b, 0, UPS), c_x[:], c_b2[:].unsqueeze(1).broadcast_to([P, UPS, CH]),
                                    ALU.add).then_inc(xb_ready, 1)

                def rstds(m):
                    pool.wait_ge(c_var, m + 1)
                    inverse_root(c_rstd[:], c_st2[:, :, 1]).then_inc(c_rstd_ready, 1)

                def c_read(m):
                    pool.wait_ge(fT_ps, m)
                    pool.wait_ge(xb_ready, m)

                m1 = l * STEPS_C
                pool.wait_ge(ffn_w_loaded, (l + 1) * (FFN_LOADS * 16))
                pool.wait_ge(attn_added, l * STEPS_B + 3 * UPS)
                stream_out(0)
                c_read(m1 + 1)
                stream_out(1)
                rstds(m1)
                c_read(m1 + 2)
                stream_out(2)
                rstds(m1 + 1)
                rstds(m1 + 2)
                with pool.Fori(0, BATCH - 3) as b:
                    pool.wait_ge(attn_added, l * STEPS_B + b * UPS + 4 * UPS)
                    c_read(m1 + b + 3)
                    stream_out(b + 3)
                    rstds(m1 + b + 3)

            for f in range(PARTS + 1):
                if f < PARTS:
                    here = slice(f * TILES // PARTS, (f + 1) * TILES // PARTS)
                    pool.wait_ge(f_var, f + 1)
                    inverse_root(f_rstd[:, here], f_st2[:, here, 1]).then_inc(f_rstd_ready, 1)
                if f >= 1:
                    here = slice((f - 1) * TILES // PARTS, f * TILES // PARTS)
                    pool.wait_ge(f_normed, f)
                    G.tensor_tensor(f_y[:, here, :], f_y[:, here, :], x1[:, here, :], ALU.add).then_inc(f_ready, 1)

        @block.scalar
        def _(act):
            def copy(dst, src):
                return nc.scalar.activation(dst, src, ACT.Copy)

            def same(dst, src):
                return nc.scalar.activation(dst, src, ACT.Identity)

            act.wait_ge(quad_logs_in, 1)
            nc.scalar.activation(quad_t[:, 1], quad_t[:, 0], ACT.Ln).then_inc(quad_logs, 1)

            def a_squares(g):
                act.wait_ge(aqk_sb, (g + 1) * UPS)
                nc.scalar.activation(a_sq[:], a_qk[:], ACT.Square).then_inc(asq_sb, 1)

            def a_qkT_out(g):
                act.wait_ge(aqkT_ps, g + 1)
                copy(a_qkT[:], bank[0][:].rearrange("p (a t) -> p a t", a=2)).then_inc(aqkT_sb, 1)

            def a_pair_exp(g, p):
                act.wait_ge(feat_ps, g * PAIRS + p + 1)
                at = p % 2 * 512
                nc.scalar.activation(a_exp[:, p % 2], wide[0][:, at:at + 512].rearrange("p (a t) -> p a t", a=2),
                                     ACT.Exp, bias=feat_bias[:, 0:1]).then_inc(feat_exp, 1)

            def a_pair_off(g, p):
                act.wait_ge(aS_ps, g * PAIRS + p + 1)
                copy(a_S[:, p % 4, :, SEQ:SEQ + P],
                     wide[1][:, 512:512 + SEQ].rearrange("p (h t) -> p h t", t=P)).then_inc(aS_off, 1)

            def a_values(g):
                for u in range(UPS):
                    copy(a_vz[:, u, :, 0:A_DIM],
                         a_v[:, u].rearrange("p (h d) -> p h d", d=A_DIM)).then_inc(vz_ready, 1)

            def a_step(g, front, pairs, back):
                for k in range(PAIRS):
                    if k == 0 and front:
                        copy(xnT[:], xt(xnT_all, g + 1, 0, UPS)).then_inc(xnT_sb, 1)
                    if k == 0 and back or k > 0 and pairs:
                        a_pair_off(g, k - 1)
                    if k == 6 and back:
                        act.wait_ge(ao2_ps, g)
                        copy(a_oT2[:], bank[1][:, 0:SEQ]).then_inc(ao2_sb, 1)
                    if k < PAIRS - 1 and pairs:
                        a_pair_exp(g, k + 1)
                    if k == PAIRS - 1 and front:
                        a_pair_exp(g + 1, 0)
                    if k == 1 and front:
                        a_squares(g + 1)
                    if k == 2 and back:
                        act.wait_ge(av_done, g)
                        if pairs:
                            act.wait_ge(av_sb, (g + 1) * UPS)
                            a_values(g)
                        copy(a_oT[:], wide[2][:].rearrange("p (g t) -> p g t", t=SEQ)).then_inc(aoT_sb, 1)
                    if k == 6 and front:
                        a_qkT_out(g + 1)

            act.wait_ge(xnT_ps, 1)
            copy(xnT[:], bank[0][:, 0:SEQ].rearrange("p (u t) -> p u t", u=UPS)).then_inc(xnT_sb, 1)
            a_squares(0)
            for i, (lo, hi) in enumerate(((UPS, UPS + 8), (UPS + 8, TILES))):
                act.wait_ge(xnT_all_ps, i + 1)
                copy(xnT_all[:, lo:hi], wide[i][:, 0:(hi - lo) * P].rearrange("p (i t) -> p i t", t=P)
                     ).then_inc(xnT_all_sb, 1)
            act.wait_ge(feat_bias_ready, 1)
            nc.scalar.activation(feat_ends[:], quad_t[:, 7], ACT.Exp).then_inc(feat_ends_exp, 1)
            act.wait_ge(a_zeroed, 3)
            act.wait_ge(av_sb, UPS)
            a_values(0)
            a_qkT_out(0)
            act.wait_ge(prep_done, 1)
            a_pair_exp(0, 0)
            act.wait_ge(xnT_all_sb, 2)
            a_step(0, True, True, False)
            act.wait_ge(zeroed, B_SET)
            with act.Fori(1, BATCH - 1) as g:
                a_step(g, True, True, True)
            a_step(BATCH - 1, False, True, True)
            a_step(BATCH, False, False, True)

            with act.Fori(0, DEPTH) as l:
                def b_shifted(m, u):
                    act.wait_ge(hT_ps, m + 1)
                    at = WIN + u * P
                    copy(hT[0:64, at:at + P], bank[0][0:64, 0:P]).then_inc(hT_sb, 1)
                    copy(hT[64:P, at + 1:at + 1 + P], bank[0][64:P, 0:P]).then_inc(hT_sb, 1)

                def b_squares(m, parts=(0, 1)):
                    for a in parts:
                        here = slice(a * INNER, (a + 1) * INNER)
                        act.wait_ge(qk_ps, m * 2 + 1 + a)
                        nc.scalar.activation(b_sq[:, here], wide[1][:, here], ACT.Square).then_inc(sq_sb, 1)

                def b_values(m, u):
                    act.wait_ge(v_ps, m + 1)
                    each = wide[2][:, 0:INNER].rearrange("p (h d) -> p h d", h=HEADS)
                    copy(b_v[:, u, :, 0:DIM], each).then_inc(v_sb, 1)

                def b_queries_keys(m, u):
                    act.wait_ge(qkT_ps, m + 1)
                    copy(b_qT[:], bank[0][:].rearrange("p (k t) -> p k t", t=P)).then_inc(qT_sb, 1)
                    copy(b_kz[0:DIM, :, 0, :, u, :],
                         bank[1][0:DIM].rearrange("p (k w t) -> p k w t", w=2, t=WIN)).then_inc(kz_sb, 1)

                def b_exp(m, half):
                    if half == 0:
                        act.wait_ge(mx_ready, m + 1)
                    for h in range(half * HEADS // 2, (half + 1) * HEADS // 2):
                        last = nc.scalar.activation(b_p[:, h], wide[0][:, h * KEYS:(h + 1) * KEYS], ACT.Exp,
                                                    bias=b_mx[:, h:h + 1], scale=-1.0)
                    last.then_inc(p_exp, 1)

                def b_out_turned(m):
                    act.wait_ge(oT_ps, m + 1)
                    copy(b_oT[:], bank[0][:].rearrange("p (k t) -> p k t", t=P)).then_inc(oT_sb, 1)

                def b_step(m, u, back, ahead1, ahead2):
                    if back:
                        b_out_turned(m - 1)
                    if ahead2:
                        act.wait_ge(v_ps, m + 2)
                        b_shifted(m + 2, u)
                    b_exp(m, 0)
                    b_exp(m, 1)
                    if ahead1:
                        act.wait_ge(vb_sb, m + 1)
                        b_values(m + 1, 1 - u)
                    if ahead2:
                        b_squares(m + 2, (0,))
                    for half in range(2):
                        act.wait_ge(pT_ps, m * 2 + half + 1)
                        heads = slice(half * HEADS // 2, (half + 1) * HEADS // 2)
                        copy(b_pT[:, heads], wide[0][:, half * 512:half * 512 + 512].rearrange(
                            "p (h t) -> p h t", t=P)).then_inc(pT_sb, 1)
                    if ahead2:
                        b_squares(m + 2, (1,))
                    if ahead1:
                        b_queries_keys(m + 1, 1 - u)

                m0 = l * STEPS_B
                b_shifted(m0, 0)
                b_squares(m0)
                b_values(m0, 0)
                b_shifted(m0 + 1, 1)
                b_squares(m0 + 1)
                b_queries_keys(m0, 0)
                b_step(m0, 0, False, True, True)
                b_step(m0 + 1, 1, True, True, True)
                with act.Fori(1, BATCH - 1) as b:
                    for u in range(UPS):
                        b_step(m0 + b * UPS + u, u, True, True, True)
                b_step(m0 + TILES - 2, 0, True, True, False)
                b_step(m0 + TILES - 1, 1, True, False, False)
                b_out_turned(m0 + TILES - 1)

                def c_shifted(m):
                    act.wait_ge(fT_ps, m + 1)
                    same(hT[0:64, WIN:WIN + SEQ], wide[2][0:64, 512:512 + SEQ]).then_inc(fT_sb, 1)
                    same(hT[64:P, WIN + 1:WIN + 1 + SEQ], wide[2][64:P, 512:512 + SEQ]).then_inc(fT_sb, 1)

                def c_gelus(m, first):
                    act.wait_ge(w1_gate_ps, m + 1)
                    if not first:
                        act.wait_ge(act_ready, m * HCH)
                    for c in range(HCH):
                        last = nc.scalar.activation(c_gelu[:, c], wide[1][:, c * SEQ:(c + 1) * SEQ], ACT.Gelu,
                                                    bias=c_b1[:, 1, c:c + 1])
                    last.then_inc(gelu_sb, 1)

                def c_affine(m):
                    act.wait_ge(fhnT_ps, m + 1)
                    nc.scalar.activation(c_hT[:], bank[0][:, 0:SEQ], ACT.Identity, bias=c_lb[:],
                                         scale=c_lg[:]).then_inc(fhnT_sb, 1)

                def c_step(m, ahead, first=False):
                    if ahead >= 3:
                        c_shifted(m + 3)
                    if ahead >= 1:
                        c_gelus(m + 1, first)
                    if ahead >= 2:
                        c_affine(m + 2)

                act.wait_ge(ffn_w_loaded, (l + 1) * (FFN_LOADS * 16))
                m1 = l * STEPS_C
                c_shifted(m1)
                c_shifted(m1 + 1)
                c_affine(m1)
                c_step(m1 - 1, 3, first=True)
                with act.Fori(0, BATCH - 3) as b:
                    c_step(m1 + b, 3)
                for b in range(BATCH - 3, BATCH):
                    c_step(m1 + b, BATCH - 1 - b)

        @block.vector
        def _(dve):
            V = nc.vector

            def mult(out, a, b):
                return V.tensor_tensor(out, a, b, ALU.mult)

            def stats(tiles, st6, st2, own=True):
                if own:
                    dve.drain()
                for i, t in enumerate(tiles):
                    V.bn_stats(st6[:, i], t)
                dve.drain()
                for i in range(len(tiles)):
                    last = V.bn_aggr(st2[:, i], st6[:, i])
                return last

            def normalised(out, t, i, st2, rstd):
                return V.tensor_scalar(out, t, st2[:, i, 0:1], rstd[:, i:i + 1], ALU.subtract, ALU.mult)

            def then(ins):
                ins.then_inc(prep_dve, 1)
                prep_count[0] += 1
                dve.wait_ge(prep_dve, prep_count[0])

            prep_count = [0]

            dve.wait_ge(first_loaded, FIRST_LOADS * 16)
            x_tiles = [x1[:, i] for i in range(TILES)]
            stats(x_tiles[0:UPS], x_st6, x_st2, own=False).then_inc(x_var, 1)
            V.tensor_scalar(quad_t[:, 0], quad[:, 1], 1.0 / A_M, 2.0 ** -63, ALU.mult, ALU.max).then_inc(quad_logs_in, 1)
            then(V.tensor_scalar(quad_t[:, 2], quad[:, 1], 0.0, None, ALU.is_gt))
            V.tensor_scalar(quad_t[:, 3], quad[:, 0], 0.0, 2.0, ALU.max, ALU.mult).then_inc(root_in, 1)
            def x_normalised(i):
                return normalised(xn[:, i], x1[:, i], i, x_st2, x_rstd)

            def a_biased_qk(g):
                dve.wait_ge(aqkv_ps, g + 1)
                for u in range(UPS):
                    V.tensor_tensor(a_qk[:, u], bank[u][:, 0:2 * CH], a_bqkv[:, 0:2 * CH], ALU.add).then_inc(aqk_sb, 1)

            def a_biased_v(g, first=False):
                if not first:
                    dve.wait_ge(vz_ready, g * UPS)
                for u in range(UPS):
                    V.tensor_tensor(a_v[:, u], bank[u][:, 2 * CH:3 * CH], a_bqkv[:, 2 * CH:3 * CH],
                                    ALU.add).then_inc(av_sb, 1)

            def a_squared_norms(g):
                dve.wait_ge(asq_sb, g + 1)
                V.tensor_reduce(out=a_ss[:], in_=a_sq[:].rearrange("p u (h d) -> p (u h) d", d=A_DIM),
                                axis=AXX, op=ALU.add).then_inc(a_ss_ready, 1)

            def a_normalised(g):
                dve.wait_ge(a_rn_ready, g + 1)
                dve.wait_ge(aqk_sb, (g + 1) * UPS)
                for u in range(UPS):
                    r = a_rn[:, u * 2 * A_HEADS:(u + 1) * 2 * A_HEADS].unsqueeze(2)
                    mult(a_qkn[:, u].rearrange("p (h d) -> p h d", d=A_DIM),
                         a_qk[:, u].rearrange("p (h d) -> p h d", d=A_DIM),
                         r.broadcast_to([P, 2 * A_HEADS, A_DIM])).then_inc(aqkn_ready, 1)

            def a_pair_clip(g, p):
                dve.wait_ge(feat_exp, g * PAIRS + p + 1)
                V.tensor_scalar(a_qf[:, p % 2], a_exp[:, p % 2, 0], feat_ends[:, 0:1], feat_ends[:, 1:2],
                                ALU.max, ALU.min).then_inc(feat_clip, 1)
                for hh in range(2):
                    rows = slice(64 * hh, 64 * hh + 64)
                    V.tensor_scalar(a_kz[rows, p % 2, hh], a_exp[rows, p % 2, 1], feat_ends[rows, 0:1],
                                    feat_ends[rows, 1:2], ALU.max, ALU.min).then_inc(feat_clip, 1)

            def a_pair_diag(g, p):
                dve.wait_ge(aS_ps, g * PAIRS + p + 1)
                mult(a_S[:, p % 4, :, 0:SEQ].rearrange("p h (a t) -> p h a t", t=P),
                     wide[1][:, 0:512].rearrange("p (h a t) -> p h a t", h=2, t=P),
                     causal[:].unsqueeze(1).unsqueeze(1).broadcast_to([P, 2, 2, P])).then_inc(aS_diag, 1)

            def a_outputs(g):
                dve.wait_ge(ao_ps, g + 1)
                o_v = [bank[u][:].rearrange("p (h c) -> p h c", c=QUAD) for u in range(UPS)]
                for u in range(UPS):
                    V.tensor_scalar(a_den[:, 0, u].unsqueeze(2), o_v[u][:, :, A_DIM:A_DIM + 1],
                                    1e-6, None, ALU.max).then_inc(den_ready, 1)
                dve.wait_ge(den_ready, g * 3 + 2)
                V.reciprocal(a_den[:, 1], a_den[:, 0]).then_inc(den_ready, 1)
                dve.wait_ge(den_ready, g * 3 + 3)
                for u in range(UPS):
                    ins = mult(a_o[:, u].rearrange("p (h d) -> p h d", d=A_DIM), o_v[u][:, :, 0:A_DIM],
                               a_den[:, 1, u].unsqueeze(2).broadcast_to([P, A_HEADS, A_DIM]))
                ins.then_inc(ao_ready, 1)

            def a_projected(g):
                dve.wait_ge(ay_ps, g + 1)
                V.tensor_tensor(a_y[:], bank[1][:, 0:SEQ].rearrange("p (u c) -> p u c", u=UPS),
                                a_bout[:].unsqueeze(1).broadcast_to([P, UPS, CH]), ALU.add)
                stats([a_y[:, u] for u in range(UPS)], st6[:, 0], st2[:, 0]).then_inc(a_var[0], 1)

            def a_residual(g):
                dve.wait_ge(a_rstd[0], g + 1)
                for u in range(UPS):
                    normalised(a_y[:, u], a_y[:, u], u, st2[:, 0], rstd[:, 0])
                dve.drain()
                V.tensor_tensor(xt(x1, g, 0, UPS), xt(x1, g, 0, UPS), a_y[:], ALU.add)
                stats([one(x1, g, u) for u in range(UPS)], st6[:, 1], st2[:, 1]).then_inc(a_var[1], 1)

            def a_input2(g):
                dve.wait_ge(a_rstd[1], g + 1)
                for u in range(UPS):
                    ins = normalised(one(xc, g, u), one(x1, g, u), u, st2[:, 1], rstd[:, 1])
                ins.then_inc(xc_ready, 1)

            def a_step(g, front, pairs, back, back2):
                for k in range(PAIRS):
                    if k == 0 and back or k > 0 and pairs:
                        a_pair_diag(g, k - 1)
                    if k == 0 and back2:
                        a_residual(g - 2)
                    if k == 1 and front:
                        a_biased_qk(g + 1)
                    if k == 2 and front:
                        a_squared_norms(g + 1)
                    if k == 2 and back2:
                        a_input2(g - 2)
                    if k == 3 and front:
                        a_biased_v(g + 1)
                    if k == 5 and back:
                        a_outputs(g - 1)
                    if k == 6 and front:
                        a_normalised(g + 1)
                    if k == 7 and back:
                        a_projected(g - 1)
                    if k < PAIRS - 1 and pairs:
                        a_pair_clip(g, k + 1)
                    if k == PAIRS - 1 and front:
                        a_pair_clip(g + 1, 0)

            dve.wait_ge(x_rstd_ready, 1)
            for i in range(UPS):
                x_normalised(i).then_inc(xn_ready, 1)
            dve.wait_ge(x_loaded, X_LOADS * 16)
            stats(x_tiles[UPS:], x_st6[:, UPS:], x_st2[:, UPS:], own=False).then_inc(x_var, 1)
            a_biased_qk(0)
            a_biased_v(0, first=True)
            a_squared_norms(0)
            dve.wait_ge(x_rstd_ready, 2)
            for i in range(UPS, TILES):
                x_normalised(i).then_inc(xn_ready, 1)
            dve.wait_ge(const_loaded, CONST_LOADS * 16)
            V.tensor_copy(masks[:], masks_f[:].unsqueeze(2).broadcast_to([P, 2, 4, KEYS])).then_inc(masks_ready, 1)
            V.tensor_copy(ident_bf[:], ident[:]).then_inc(masks_ready, 1)
            dve.wait_ge(root_ready, 1)
            then(mult(omega_rows[:], omega_rows[:], quad_t[:, 4].unsqueeze(2).broadcast_to([P, A_R, A_M])))
            then(mult(omega_pad[:],
                           omega_rows[:].rearrange("p r m -> p (r m)").unsqueeze(1).broadcast_to([P, A_HEADS, A_FEAT]),
                           owner[:].unsqueeze(2).broadcast_to([P, A_HEADS, A_FEAT])))
            dve.wait_ge(quad_logs, 1)
            then(V.tensor_scalar(quad_t[:, 1], quad_t[:, 1], 0.5, None, ALU.mult))
            then(V.tensor_tensor(quad_t[:, 5], quad_t[:, 1], quad[:, 0], ALU.subtract))
            then(mult(feat_sel[:, 0], quad_t[:, 5], node_sel[:]))
            then(mult(feat_sel[:, 1], quad_t[:, 1], node_sel[:]))
            then(V.tensor_reduce(out=feat_bias[:], in_=feat_sel[:], axis=AXX, op=ALU.add))
            then(V.tensor_scalar(quad_t[:, 7, 0:1], feat_bias[:, 1:2], -CLIP, None, ALU.add))
            V.tensor_scalar(quad_t[:, 7, 1:2], feat_bias[:, 1:2], CLIP, None, ALU.add).then_inc(feat_bias_ready, 1)
            then(mult(feat_sel[:, 0], quad_t[:, 2], node_sel[:]))
            then(V.tensor_reduce(out=feat_sel[:, 1, 0:1], in_=feat_sel[:, 0], axis=AXX, op=ALU.add))
            dve.wait_ge(feat_ends_exp, 1)
            then(mult(feat_ends[:], feat_ends[:], feat_sel[:, 1, 0:1].broadcast_to([P, 2])))
            V.tensor_copy(quad_t[:, 5], quad_t[:, 4]).then_inc(prep_done, 1)

            a_normalised(0)
            dve.wait_ge(a_zeroed, 1)
            a_pair_clip(0, 0)
            a_step(0, True, True, False, False)
            a_step(1, True, True, True, False)
            with dve.Fori(2, BATCH - 1) as g:
                a_step(g, True, True, True, True)
            a_step(BATCH - 1, False, True, True, True)
            a_step(BATCH, False, False, True, True)
            a_step(BATCH + 1, False, False, False, True)

            dve.wait_ge(tables_ready, TABLE_OPS)
            with dve.Fori(0, DEPTH) as l:
                each = "p (a h d) -> p a h d"
                halves = "p (a h b d) -> p a h b d"

                def table(t, u):
                    return t[:, bass.ds(l * UPS + u, 1)].rearrange("p o a d -> p (o a) d")

                def b_cosine(m, u, first=False, parts=(0, 1)):
                    if not first and parts[0] == 0:
                        dve.wait_ge(rot_ready, m)
                    for a in parts:
                        dve.wait_ge(sq_sb, m * 2 + 1 + a)
                        here = slice(a * INNER, (a + 1) * INNER)
                        mult(b_ra[:, here].rearrange("p (h d) -> p h d", d=DIM),
                             wide[1][:, here].rearrange("p (h d) -> p h d", d=DIM),
                             table(t_cos, u)[:, a].unsqueeze(1).broadcast_to([P, HEADS, DIM])).then_inc(rot_a, 1)

                def b_sine(m, u):
                    src = wide[1][:].rearrange(halves, a=2, h=HEADS, b=2)
                    dst = b_rb[:].rearrange(halves, a=2, h=HEADS, b=2)
                    for half in range(2):
                        sin = table(t_sin, u)[:, :, half * DIM // 2:(half + 1) * DIM // 2]
                        mult(dst[:, :, :, half, :], src[:, :, :, 1 - half, :],
                             sin.unsqueeze(2).broadcast_to([P, 2, HEADS, DIM // 2])).then_inc(rot_a, 1)

                def b_squared_norms(m):
                    V.tensor_reduce(out=b_ss[:], in_=b_sq[:].rearrange("p (h d) -> p h d", d=DIM),
                                    axis=AXX, op=ALU.add).then_inc(b_ss_ready, 1)

                def b_rotated(m):
                    dve.wait_ge(rot_a, m * 4 + 4)
                    V.tensor_tensor(b_ra[:], b_ra[:], b_rb[:], ALU.add).then_inc(rot_sum, 1)

                def b_normalised(m):
                    dve.wait_ge(rot_sum, m + 1)
                    dve.wait_ge(b_rn_ready, m + 1)
                    mult(b_qk_rot[:].rearrange("p (h d) -> p h d", d=DIM), b_ra[:].rearrange("p (h d) -> p h d", d=DIM),
                         b_rn[:].unsqueeze(2).broadcast_to([P, 2 * HEADS, DIM])).then_inc(rot_ready, 1)

                def b_odd_keys(m, u):
                    dve.wait_ge(qkT_ps, m + 1)
                    V.tensor_copy(b_kz[DIM:P, :, 1, :, u, :], bank[1][DIM:P].rearrange(
                        "p (k w t) -> p k w t", w=2, t=WIN)).then_inc(kz_sb, 1)

                def b_maximum(m):
                    dve.wait_ge(s_ps, m + 1)
                    V.tensor_reduce(out=b_mx[:], in_=wide[0][:].rearrange("p (h j) -> p h j", j=KEYS),
                                    axis=AXX, op=ALU.min).then_inc(mx_ready, 1)

                def b_weighted(m):
                    dve.wait_ge(o_ps, m + 1)
                    o_v = wide[2][:].rearrange("p (g c) -> p g c", c=512)[:, :, 0:4 * VCOL]
                    o_v = o_v.rearrange("p g (h d) -> p g h d", d=VCOL)
                    rs = b_rs[:].rearrange("p (g h) -> p g h", g=2).unsqueeze(3)
                    V.reciprocal(rs, o_v[:, :, :, DIM:VCOL]).then_inc(rs_ready, 1)
                    dve.wait_ge(rs_ready, m + 1)
                    mult(b_o[:].rearrange("p (g h) d -> p g h d", g=2), o_v[:, :, :, 0:DIM],
                         rs.broadcast_to([P, 2, HEADS // 2, DIM])).then_inc(o_ready, 1)

                def b_added(m, b, u):
                    dve.wait_ge(wo_ps, m + 1)
                    V.tensor_tensor(one(xc, b, u), one(xc, b, u), bank[1][:, 0:CH],
                                    ALU.add).then_inc(attn_added, 1)

                def b_step(m, b, u, back, ahead1, ahead2):
                    b_maximum(m)
                    if ahead1:
                        b_rotated(m + 1)
                    if back:
                        b_added(m - 1, b, u - 1)
                    if ahead1:
                        b_normalised(m + 1)
                    if ahead2:
                        b_cosine(m + 2, u, parts=(0,))
                    if ahead1:
                        b_odd_keys(m + 1, 1 - u)
                    if ahead2:
                        b_cosine(m + 2, u, parts=(1,))
                        b_squared_norms(m + 2)
                    b_weighted(m)
                    if ahead2:
                        b_sine(m + 2, u)

                m0 = l * STEPS_B
                b_cosine(m0, 0, first=True)
                b_squared_norms(m0)
                b_sine(m0, 0)
                b_rotated(m0)
                b_normalised(m0)
                b_odd_keys(m0, 0)
                b_cosine(m0 + 1, 1)
                b_squared_norms(m0 + 1)
                b_sine(m0 + 1, 1)
                b_step(m0, 0, 0, False, True, True)
                b_step(m0 + 1, 0, 1, True, True, True)
                with dve.Fori(1, BATCH - 1) as b:
                    for u in range(UPS):
                        b_step(m0 + b * UPS + u, b, u, True, True, True)
                b_step(m0 + TILES - 2, BATCH - 1, 0, True, True, False)
                b_step(m0 + TILES - 1, BATCH - 1, 1, True, False, False)
                b_added(m0 + TILES - 1, BATCH - 1, 1)

                tiles = [bank[1][:, u * CH:(u + 1) * CH] for u in range(UPS)]

                def c_stats(m):
                    dve.wait_ge(fh_ps, m + 1)
                    stats(tiles, c_st6, c_st2, own=False).then_inc(c_var, 1)

                def c_normalised(m):
                    dve.wait_ge(c_rstd_ready, m + 1)
                    for u in range(UPS):
                        normalised(c_hn[:, u], tiles[u], u, c_st2, c_rstd).then_inc(fhn_ready, 1)

                def c_gated(m):
                    dve.wait_ge(w1_ps, m + 1)
                    dve.wait_ge(gelu_sb, m + 1)
                    for c in range(HCH):
                        V.scalar_tensor_tensor(out=c_act[:, c], in0=wide[0][:, c * SEQ:(c + 1) * SEQ],
                                               scalar=c_b1[:, 0, c:c + 1], in1=c_gelu[:, c],
                                               op0=ALU.add, op1=ALU.mult).then_inc(act_ready, 1)

                def c_added(m, b):
                    dve.wait_ge(xb_ready, m + 1)
                    V.tensor_tensor(xt(xc, b, 0, UPS), xt(xc, b, 0, UPS),
                                    wide[2][:, 0:SEQ].rearrange("p (u c) -> p u c", u=UPS),
                                    ALU.add).then_inc(xc_ready, 1)

                def c_step(m, b, ahead, first=False):
                    if ahead >= 2:
                        c_normalised(m + 2)
                    if ahead >= 3:
                        c_stats(m + 3)
                    if not first:
                        dve.wait_ge(w2_ps, m + 1)
                    if ahead >= 1:
                        c_gated(m + 1)
                    if not first:
                        c_added(m, b)

                m1 = l * STEPS_C
                dve.wait_ge(ffn_w_loaded, (l + 1) * (FFN_LOADS * 16))
                c_stats(m1)
                c_normalised(m1)
                c_stats(m1 + 1)
                c_step(m1 - 1, 0, 3, first=True)
                with dve.Fori(0, BATCH - 3) as b:
                    c_step(m1 + b, b, 3)
                for b in range(BATCH - 3, BATCH):
                    c_step(m1 + b, b, BATCH - 1 - b)

            dve.wait_ge(xc_ready, (DEPTH + 1) * STEPS_C)
            for f in range(PARTS + 1):
                if f < PARTS:
                    here = slice(f * TILES // PARTS, (f + 1) * TILES // PARTS)
                    stats([xc[:, i] for i in range(here.start, here.stop)], f_st6[:, here], f_st2[:, here],
                          own=False).then_inc(f_var, 1)
                if f >= 1:
                    dve.wait_ge(f_rstd_ready, f)
                    for i in range((f - 1) * TILES // PARTS, f * TILES // PARTS):
                        ins = normalised(f_y[:, i], xc[:, i], i, f_st2, f_rstd)
                    ins.then_inc(f_normed, 1)

        @block.tensor
        def _(pe):
            T = nc.tensor

            def x_turned(tiles, where, at):
                for i in tiles:
                    pe.wait_ge(xn_ready, i + 1)
                    last = T.transpose(where[:, (i - at) * P:(i - at + 1) * P], xn[:, i], ident[:])
                return last

            def a_qkv(g):
                pe.wait_ge(xnT_sb, g + 1)
                for u in range(UPS):
                    last = T.matmul(bank[u][:, 0:3 * CH], xnT[:, u], a_wqkv[:], start=True, stop=True)
                last.then_inc(aqkv_ps, 1)

            def a_qk_turned(g):
                pe.wait_ge(aqkn_ready, (g + 1) * UPS)
                for a in range(2):
                    for u in range(UPS):
                        last = T.transpose(bank[0][:, a * SEQ + u * P:a * SEQ + (u + 1) * P],
                                           a_qkn[:, u, a * CH:(a + 1) * CH], ident[:])
                last.then_inc(aqkT_ps, 1)

            def a_pair_feat(g, p):
                half = p % 2 * 512
                T.matmul(wide[0][:, half:half + 512], omega_pad[:, 2 * p:2 * p + 2, :].rearrange("p a f -> p (a f)"),
                         a_qkT[:].rearrange("p a t -> p (a t)"), start=True, stop=True).then_inc(feat_ps, 1)

            def a_pair_scores(g, p):
                pe.wait_ge(feat_clip, g * (3 * PAIRS) + 3 * p + 3)
                if not (p == 0 and isinstance(g, int) and g == 0):
                    pe.wait_ge(aS_diag, g * PAIRS + p)
                    pe.wait_ge(aS_off, g * PAIRS + p)
                for hh in range(2):
                    for keys, queries, at in ((1, 1, hh * SEQ), (0, 0, hh * SEQ + P), (0, 1, 512 + hh * P)):
                        last = T.matmul(wide[1][:, at:at + P], a_kz[:, p % 2, hh, keys * P:(keys + 1) * P],
                                        a_qf[:, p % 2, queries * P:(queries + 1) * P], start=True, stop=True)
                last.then_inc(aS_ps, 1)

            def a_values(g, grp):
                pe.wait_ge(aS_diag, g * PAIRS + 2 * grp + 2)
                pe.wait_ge(aS_off, g * PAIRS + 2 * grp + 2)
                for keys in range(UPS):
                    for j in range(GH):
                        p, hh = 2 * grp + j // 2, j % 2
                        weights = a_S[:, p % 4, hh, P:P + SEQ] if keys == 0 else a_S[:, p % 4, hh, 0:P]
                        last = T.matmul(wide[2][j * QUAD:(j + 1) * QUAD, grp * SEQ + keys * P:(grp + 1) * SEQ],
                                        a_vz[:, keys, grp * GH + j], weights,
                                        start=keys == 0, stop=keys == UPS - 1)
                if grp == GROUPS - 1:
                    last.then_inc(av_done, 1)

            def a_turned_back(g):
                pe.wait_ge(aoT_sb, g + 1)
                for u in range(UPS):
                    for grp in range(GROUPS):
                        last = T.transpose(bank[u][:, grp * P:(grp + 1) * P], a_oT[:, grp, u * P:(u + 1) * P],
                                           ident[:])
                last.then_inc(ao_ps, 1)

            def a_step(g, front, pairs, back):
                for k in range(PAIRS):
                    if k < PAIRS - 1 and pairs:
                        a_pair_feat(g, k + 1)
                    if k == PAIRS - 1 and front:
                        pe.wait_ge(aqkT_sb, g + 2)
                        a_pair_feat(g + 1, 0)
                    if k in (0, 2) and back:
                        a_values(g - 1, 2 + k // 2)
                    if k in (4, 6) and pairs:
                        if k == 4:
                            pe.wait_ge(vz_ready, (g + 1) * UPS)
                            if back:
                                pe.wait_ge(aoT_sb, g)
                        a_values(g, k // 2 - 2)
                    if pairs:
                        a_pair_scores(g, k)
                    if k == 0 and front:
                        a_qkv(g + 1)
                    if k == 4 and back:
                        if front:
                            pe.wait_ge(av_sb, (g + 2) * UPS)
                        a_turned_back(g - 1)
                    if k == 5 and back:
                        pe.wait_ge(ao_ready, g)
                        for u in range(UPS):
                            last = T.transpose(bank[1][:, u * P:(u + 1) * P], a_o[:, u], ident[:])
                        last.then_inc(ao2_ps, 1)
                    if k == 6 and back:
                        pe.wait_ge(ao2_sb, g)
                        for u in range(UPS):
                            last = T.matmul(bank[1][:, u * CH:(u + 1) * CH], a_oT2[:, u * P:(u + 1) * P], a_wout[:],
                                            start=True, stop=True)
                        last.then_inc(ay_ps, 1)
                    if k == 6 and front:
                        a_qk_turned(g + 1)

            pe.wait_ge(first_loaded, FIRST_LOADS * 16)
            x_turned(range(UPS), bank[0], 0).then_inc(xnT_ps, 1)
            a_qkv(0)
            x_turned(range(UPS, UPS + 8), wide[0], UPS).then_inc(xnT_all_ps, 1)
            x_turned(range(UPS + 8, TILES), wide[1], UPS + 8).then_inc(xnT_all_ps, 1)
            pe.wait_ge(av_sb, UPS)
            a_qk_turned(0)
            pe.wait_ge(prep_done, 1)
            pe.wait_ge(xnT_all_sb, 2)
            pe.wait_ge(aqkT_sb, 1)
            a_pair_feat(0, 0)
            a_step(0, True, True, False)
            with pe.Fori(1, BATCH - 1) as g:
                a_step(g, True, True, True)
            a_step(BATCH - 1, False, True, True)
            a_step(BATCH, False, False, True)

            pe.wait_ge(masks_ready, 2)
            with pe.Fori(0, DEPTH) as l:
                def b_stream(m):
                    pe.wait_ge(bx_ready, m + 1)
                    T.transpose(bank[0][:, 0:P], b_x[:], ident[:]).then_inc(hT_ps, 1)

                def b_qk(m, u, first=False):
                    pe.wait_ge(hT_sb, m * 2 + 2)
                    if not first:
                        pe.wait_ge(rot_a, m * 4)
                    at = WIN + u * P
                    for a in range(2):
                        T.matmul(wide[1][:, a * INNER:(a + 1) * INNER], hT[:, at:at + P],
                                 b_wqkv[:, a * INNER:(a + 1) * INNER], start=True, stop=True).then_inc(qk_ps, 1)

                def b_values(u):
                    at = WIN + u * P
                    T.matmul(wide[2][:, 0:INNER], hT[:, at:at + P], b_wqkv[:, 2 * INNER:3 * INNER],
                             start=True, stop=True).then_inc(v_ps, 1)

                def b_turn(m):
                    pe.wait_ge(rot_ready, m + 1)
                    for c in range(2 * HP):
                        last = T.transpose(bank[c // HP][:, c % HP * P:(c % HP + 1) * P],
                                           b_qk_rot[:, c * P:(c + 1) * P], ident[:])
                    last.then_inc(qkT_ps, 1)

                def b_masks(u, half):
                    kind = 0 if u == 0 else 1
                    T.matmul(wide[0][:, half * 512:half * 512 + 512], ident_bf[:],
                             masks[:, kind].rearrange("p h j -> p (h j)"), start=True, stop=False)

                def b_scores(u):
                    for k in range(HP):
                        out_k = wide[0][:, k * 2 * KEYS:(k + 1) * 2 * KEYS]
                        out_k = out_k.rearrange("p (h c t) -> p h c t", h=2, t=WIN)
                        for c in range(2):
                            for w in range(2):
                                keys = b_kz[:, k, :, c, 1 - u if c > w else u, :]
                                last = T.matmul(out_k[w * WIN:(w + 1) * WIN, :, c, :],
                                                b_qT[:, k, w * WIN:(w + 1) * WIN], keys,
                                                start=False, stop=k % 2 == 1 and c == 1)
                    last.then_inc(s_ps, 1)

                def b_queries_keys_out(m):
                    pe.wait_ge(qT_sb, m + 1)
                    pe.wait_ge(kz_sb, m * 2 + 2)

                def b_out_turn(m):
                    pe.wait_ge(o_ready, m + 1)
                    for k in range(HP):
                        last = T.transpose(bank[0][:, k * P:(k + 1) * P],
                                           b_o[:, 2 * k:2 * k + 2].rearrange("p h d -> p (h d)"), ident[:])
                    last.then_inc(oT_ps, 1)

                def b_out(m):
                    for k in range(HP):
                        last = T.matmul(bank[1][:, 0:CH], b_oT[:, k], b_wo[:, k], start=k == 0, stop=k == HP - 1)
                    last.then_inc(wo_ps, 1)

                def b_step(m, u, back, ahead1, ahead2):
                    if back:
                        b_out_turn(m - 1)
                    if ahead1:
                        b_values(1 - u)
                    if back:
                        pe.wait_ge(oT_sb, m)
                    if ahead2:
                        b_stream(m + 2)
                    if back:
                        b_out(m - 1)
                    if ahead2:
                        b_qk(m + 2, u)
                    for half in range(2):
                        pe.wait_ge(p_exp, m * 2 + 1 + half)
                        for h in range(half * HEADS // 2, (half + 1) * HEADS // 2):
                            last = T.transpose(wide[0][:, h * P:(h + 1) * P], b_p[:, h], ident[:])
                        last.then_inc(pT_ps, 1)
                    if ahead1:
                        if back:
                            pe.wait_ge(attn_added, m)
                        b_turn(m + 1)
                        pe.wait_ge(pT_sb, m * 2 + 1)
                        b_masks(1 - u, 0)
                    pe.wait_ge(pT_sb, m * 2 + 2)
                    if ahead1:
                        pe.wait_ge(v_sb, m + 2)
                    pe.wait_ge(vb_sb, m + 1)
                    for h in range(HEADS):
                        for w in range(2):
                            at = h // 4 * 512 + h % 4 * VCOL
                            last = T.matmul(wide[2][w * WIN:(w + 1) * WIN, at:at + VCOL],
                                            b_pT[:, h, w * WIN:(w + 1) * WIN], (b_vb, b_v)[w][:, u, h, :],
                                            start=True, stop=True)
                    last.then_inc(o_ps, 1)
                    if ahead1:
                        b_masks(1 - u, 1)
                        b_queries_keys_out(m + 1)
                        b_scores(1 - u)

                m0 = l * STEPS_B
                pe.wait_ge(attn_w_loaded, (l + 1) * (ATTN_LOADS * 16))
                b_stream(m0)
                b_qk(m0, 0, first=True)
                pe.wait_ge(xc_ready, (l + 1) * STEPS_C)
                b_values(0)
                b_stream(m0 + 1)
                b_qk(m0 + 1, 1)
                pe.wait_ge(hT_sb, m0 * 2 + 4)
                b_turn(m0)
                for half in range(2):
                    b_masks(0, half)
                b_queries_keys_out(m0)
                b_scores(0)
                pe.wait_ge(v_sb, m0 + 1)
                b_step(m0, 0, False, True, True)
                b_step(m0 + 1, 1, True, True, True)
                with pe.Fori(1, BATCH - 1) as b:
                    for u in range(UPS):
                        b_step(m0 + b * UPS + u, u, True, True, True)
                b_step(m0 + TILES - 2, 0, True, True, False)
                b_step(m0 + TILES - 1, 1, True, False, False)
                b_out_turn(m0 + TILES - 1)
                pe.wait_ge(oT_sb, m0 + TILES)
                b_out(m0 + TILES - 1)

                def c_stream(m):
                    pe.wait_ge(cx_ready, m + 1)
                    for u in range(UPS):
                        last = T.transpose(wide[2][:, 512 + u * P:512 + (u + 1) * P], c_x[:, u], ident[:])
                    last.then_inc(fT_ps, 1)

                def c_back(m):
                    pe.wait_ge(fT_sb, m * 2 + 2)
                    for u in range(UPS):
                        at = WIN + u * P
                        last = T.transpose(bank[1][:, u * P:(u + 1) * P], hT[:, at:at + P], ident[:])
                    last.then_inc(fh_ps, 1)

                def c_normed(m):
                    pe.wait_ge(fhn_ready, (m + 1) * UPS)
                    for u in range(UPS):
                        last = T.transpose(bank[0][:, u * P:(u + 1) * P], c_hn[:, u], ident[:])
                    last.then_inc(fhnT_ps, 1)

                def c_hidden(m, g):
                    for c in range(HCH):
                        last = T.matmul(wide[g][:, c * SEQ:(c + 1) * SEQ], c_w1[:, g, c * P:(c + 1) * P],
                                        c_hT[:], start=True, stop=True)
                    last.then_inc(w1_gate_ps if g else w1_ps, 1)

                def c_step(m, ahead, first=False):
                    if ahead >= 1:
                        pe.wait_ge(fhnT_sb, m + 2)
                        if not first:
                            pe.wait_ge(gelu_sb, m + 1)
                        c_hidden(m + 1, 1)
                    if ahead >= 3:
                        c_stream(m + 3)
                    if ahead >= 1:
                        if not first:
                            pe.wait_ge(act_ready, (m + 1) * HCH)
                        c_hidden(m + 1, 0)
                    if ahead >= 2:
                        c_normed(m + 2)
                    if ahead >= 3:
                        c_back(m + 3)
                    if not first:
                        if ahead < 1:
                            pe.wait_ge(act_ready, (m + 1) * HCH)
                        if ahead < 2:
                            pe.wait_ge(xc_ready, STEPS_C + m)
                        for u in range(UPS):
                            for c in range(HCH):
                                last = T.matmul(wide[2][:, u * CH:(u + 1) * CH], c_act[:, c, u * P:(u + 1) * P],
                                                c_w2[:, c], start=c == 0, stop=c == HCH - 1)
                        last.then_inc(w2_ps, 1)

                m1 = l * STEPS_C
                pe.wait_ge(ffn_w_loaded, (l + 1) * (FFN_LOADS * 16))
                c_stream(m1)
                pe.wait_ge(attn_added, (l + 1) * STEPS_B)
                c_back(m1)
                c_stream(m1 + 1)
                c_normed(m1)
                c_back(m1 + 1)
                c_step(m1 - 1, 3, first=True)
                with pe.Fori(0, BATCH - 3) as b:
                    c_step(m1 + b, 3)
                for b in range(BATCH - 3, BATCH):
                    c_step(m1 + b, BATCH - 1 - b)


_INS = ['L0_attn_x', 'L0_attn_Wqkv', 'L0_attn_bqkv', 'L0_attn_Wout', 'L0_attn_bout', 'L0_attn_omega',
        'L0_attn_quad_nodes', 'L0_attn_quad_weights', 'L0_ffn_wqkv', 'L0_ffn_q_scale', 'L0_ffn_k_scale',
        'L0_ffn_wo', 'L0_ffn_ln_g', 'L0_ffn_ln_b', 'L0_ffn_w1', 'L0_ffn_b1', 'L0_ffn_w2', 'L0_ffn_b2']


def kernel(**inputs):
    import concourse.bacc as bacc
    from concourse.bass_utils import run_bass_kernel_spmd

    nc = bacc.Bacc("TRN2", target_bir_lowering=False, num_devices=1)
    arrays, args = {}, []
    constants = shape_constants()
    for name, a in [(n, inputs[n]) for n in _INS] + list(constants.items()):
        a = np.ascontiguousarray(a)
        arrays[name] = a
        args.append(nc.dram_tensor(name, a.shape, mybir.dt.from_np(a.dtype), kind="ExternalInput").ap())
    result = nc.dram_tensor("result", (BATCH, SEQ, CH), F32, kind="ExternalOutput").ap()
    build(nc, *args, result)
    r = run_bass_kernel_spmd(nc, [arrays], core_ids=[0])
    return r.results[0]["result"]
```
